# Optimizing a Trainium2 kernel written in Bass

```python
import numpy as np
import jax
import jax.numpy as jnp

def _softmax(x, axis=-1):
    return jax.nn.softmax(x, axis=axis)

def _gelu(x):
    return jax.nn.gelu(x, approximate=True)

def _silu(x):
    return jax.nn.silu(x)

def _sigmoid(x):
    return jax.nn.sigmoid(x)

def _layernorm(x, axis=-1, eps=1e-05):
    m = jnp.mean(x, axis=axis, keepdims=True)
    v = jnp.var(x, axis=axis, keepdims=True)
    return (x - m) / jnp.sqrt(v + eps)

def _scatter_add(tgt, idx, src, axis=0):
    return tgt.at[idx].add(src)

def _segment_sum(src, seg, n):
    return jax.ops.segment_sum(src, seg, n)
kernel_name = 'mk_prb_d1_jaxref_r8_8b0793'

def setup_inputs(seed: int=0):
    np.random.seed(seed)
    _w = jnp.asarray

    def _L0_attn_setup():
        import jax, jax.numpy as jnp
        import numpy as np
        import math
        B, T, C = (2, 256, 128)
        H, L = (16, 64)
        DH = C // H
        DHE = DH // 2
        THETA = 10000.0

        def _rope_cache(t, dim):
            inv_freq = 1.0 / THETA ** (jnp.arange(0, dim, 2, dtype=jnp.float32) / dim)
            freqs = jnp.arange(t, dtype=jnp.float32)[:, None] * inv_freq[None, :]
            emb = jnp.concatenate((freqs, freqs), axis=-1)
            return (jnp.cos(emb), jnp.sin(emb))

        def _apply_rope(x, cos, sin):
            x1 = x[..., 0::2]
            x2 = x[..., 1::2]
            rot = jnp.stack((-x2, x1), axis=-1).reshape(x.shape)
            return x * cos[None, None] + rot * sin[None, None]
        key = jax.random.key(seed)
        ks = jax.random.split(key, 10)
        s = 0.02
        return {'x': jax.random.normal(ks[0], (B, T, C), jnp.float32), 'Wq_down': jax.random.normal(ks[1], (C, H * L), jnp.float32) * s, 'Wk_down': jax.random.normal(ks[2], (C, H * L), jnp.float32) * s, 'Wv_down': jax.random.normal(ks[3], (C, H * L), jnp.float32) * s, 'Wq_up_c': jax.random.normal(ks[4], (L, DHE), jnp.float32) * s, 'Wq_up_e': jax.random.normal(ks[5], (L, DHE), jnp.float32) * s, 'Wk_up_c': jax.random.normal(ks[6], (L, DHE), jnp.float32) * s, 'Wk_up_e': jax.random.normal(ks[7], (L, DHE), jnp.float32) * s, 'Wv_up': jax.random.normal(ks[8], (L, DH), jnp.float32) * s, 'Wc': jax.random.normal(ks[9], (C, C), jnp.float32) * s}
    _L0_attn_in = _L0_attn_setup()

    def _L0_ffn_setup():
        import jax, jax.numpy as jnp
        import numpy as np
        DIM = 128
        DEPTH = 6
        HEADS = 16
        DIM_HEAD = 64
        WINDOW = 32
        INNER = HEADS * DIM_HEAD
        DIM_INNER = int(DIM * 4 * 2 / 3)
        QK_SCALE = 8.0

        def shift_tokens(t):
            a, s = jnp.split(t, 2, -1)
            s = jnp.pad(s, ((0, 0), (1, 0), (0, 0)))[:, :-1]
            return jnp.concatenate([a, s], -1)

        def l2norm(t):
            return t / jnp.maximum(jnp.linalg.norm(t, axis=-1, keepdims=True), 1e-12)

        def rotate_half(x):
            x1, x2 = jnp.split(x, 2, -1)
            return jnp.concatenate([-x2, x1], -1)

        def rotary_tables(n):
            half = jnp.arange(0, DIM_HEAD, 2, dtype=jnp.float32)
            inv_freq = 1.0 / 10000.0 ** (half / DIM_HEAD)
            t = jnp.arange(n, dtype=jnp.float32)
            freqs = t[:, None] * inv_freq[None, :]
            freqs = jnp.concatenate([freqs, freqs], -1)
            base_scale = (half + 0.4 * DIM_HEAD) / (1.4 * DIM_HEAD)
            power = (t - n // 2) / (WINDOW // 2)
            scale = base_scale[None, :] ** power[:, None]
            scale = jnp.concatenate([scale, scale], -1)
            return (freqs, scale)

        def local_attention(q, k, v):
            b, h, n, d = q.shape
            w = WINDOW
            nw = n // w
            bq = q.reshape(b, h, nw, w, d)
            bk = k.reshape(b, h, nw, w, d)
            bv = v.reshape(b, h, nw, w, d)

            def look(t):
                p = jnp.pad(t, ((0, 0), (0, 0), (1, 0), (0, 0), (0, 0)))
                return jnp.concatenate([p[:, :, :nw], p[:, :, 1:]], axis=3)
            bk2, bv2 = (look(bk), look(bv))
            seq = jnp.arange(n).reshape(nw, w)
            seq_p = jnp.pad(seq, ((1, 0), (0, 0)), constant_values=-1)
            jt = jnp.concatenate([seq_p[:nw], seq_p[1:]], axis=1)
            it = seq[:, :, None]
            jb = jt[:, None, :]
            mask = (it < jb) | (it > jb + w) | (jb == -1)
            sim = jnp.einsum('bhwie,bhwje->bhwij', bq, bk2) * QK_SCALE
            sim = jnp.where(mask, -jnp.finfo(sim.dtype).max, sim)
            attn = jax.nn.softmax(sim, -1)
            out = jnp.einsum('bhwij,bhwje->bhwie', attn, bv2)
            return out.reshape(b, h, n, d)

        def attn_layer(x, Wqkv, qs, ksc, Wo):
            b, n, _ = x.shape
            qkv = x @ Wqkv
            q, k, v = jnp.split(qkv, 3, -1)
            sh = lambda t: t.reshape(b, n, HEADS, DIM_HEAD).transpose(0, 2, 1, 3)
            q, k, v = (sh(q), sh(k), sh(v))
            q = l2norm(q) * qs
            k = l2norm(k) * ksc
            freqs, scale = rotary_tables(n)
            cos, sin = (jnp.cos(freqs), jnp.sin(freqs))
            q = q * cos * scale + rotate_half(q) * sin * scale
            inv = 1.0 / scale
            k = k * cos * inv + rotate_half(k) * sin * inv
            out = local_attention(q, k, v)
            out = out.transpose(0, 2, 1, 3).reshape(b, n, INNER)
            return out @ Wo

        def ffn_layer(x, g, bln, W1, b1, W2, b2):
            mu = x.mean(-1, keepdims=True)
            var = ((x - mu) ** 2).mean(-1, keepdims=True)
            xn = (x - mu) / jnp.sqrt(var + 1e-05) * g + bln
            hg = xn @ W1 + b1
            a, gate = jnp.split(hg, 2, -1)
            return a * jax.nn.gelu(gate, approximate=False) @ W2 + b2
        key = jax.random.key(seed)
        ks = jax.random.split(key, 8)
        B, N = (2, 256)
        init = lambda k, shape: jax.random.normal(k, shape, jnp.float32) * 0.02
        return {'x': jax.random.normal(ks[0], (B, N, DIM), jnp.float32), 'Wqkv': init(ks[1], (DEPTH, DIM, 3 * INNER)), 'q_scale': jnp.ones((DEPTH, DIM_HEAD), jnp.float32), 'k_scale': jnp.ones((DEPTH, DIM_HEAD), jnp.float32), 'Wo': init(ks[2], (DEPTH, INNER, DIM)), 'ln_g': jnp.ones((DEPTH, DIM), jnp.float32), 'ln_b': jnp.zeros((DEPTH, DIM), jnp.float32), 'W1': init(ks[3], (DEPTH, DIM, 2 * DIM_INNER)), 'b1': jnp.zeros((DEPTH, 2 * DIM_INNER), jnp.float32), 'W2': init(ks[4], (DEPTH, DIM_INNER, DIM)), 'b2': jnp.zeros((DEPTH, DIM), jnp.float32)}
    _L0_ffn_in = _L0_ffn_setup()
    _d = {'L0_attn_x': _L0_attn_in['x'], 'L0_attn_Wq_down': _L0_attn_in['Wq_down'], 'L0_attn_Wk_down': _L0_attn_in['Wk_down'], 'L0_attn_Wv_down': _L0_attn_in['Wv_down'], 'L0_attn_Wq_up_c': _L0_attn_in['Wq_up_c'], 'L0_attn_Wq_up_e': _L0_attn_in['Wq_up_e'], 'L0_attn_Wk_up_c': _L0_attn_in['Wk_up_c'], 'L0_attn_Wk_up_e': _L0_attn_in['Wk_up_e'], 'L0_attn_Wv_up': _L0_attn_in['Wv_up'], 'L0_attn_Wc': _L0_attn_in['Wc'], 'L0_ffn_Wqkv': _L0_ffn_in['Wqkv'], 'L0_ffn_q_scale': _L0_ffn_in['q_scale'], 'L0_ffn_k_scale': _L0_ffn_in['k_scale'], 'L0_ffn_Wo': _L0_ffn_in['Wo'], 'L0_ffn_ln_g': _L0_ffn_in['ln_g'], 'L0_ffn_ln_b': _L0_ffn_in['ln_b'], 'L0_ffn_W1': _L0_ffn_in['W1'], 'L0_ffn_b1': _L0_ffn_in['b1'], 'L0_ffn_W2': _L0_ffn_in['W2'], 'L0_ffn_b2': _L0_ffn_in['b2']}
    _x0 = _d['L0_attn_x']
    _d['L0_attn_x'] = jax.random.normal(jax.random.fold_in(jax.random.key(seed), 1), (8, 512, 128), dtype=_x0.dtype)
    del _x0
    return _d

def reference(L0_attn_x, L0_attn_Wq_down, L0_attn_Wk_down, L0_attn_Wv_down, L0_attn_Wq_up_c, L0_attn_Wq_up_e, L0_attn_Wk_up_c, L0_attn_Wk_up_e, L0_attn_Wv_up, L0_attn_Wc, L0_ffn_Wqkv, L0_ffn_q_scale, L0_ffn_k_scale, L0_ffn_Wo, L0_ffn_ln_g, L0_ffn_ln_b, L0_ffn_W1, L0_ffn_b1, L0_ffn_W2, L0_ffn_b2):

    def _L0_attn_ref(x, Wq_down, Wk_down, Wv_down, Wq_up_c, Wq_up_e, Wk_up_c, Wk_up_e, Wv_up, Wc):
        import jax, jax.numpy as jnp
        import numpy as np
        import math
        B, T, C = (2, 256, 128)
        H, L = (16, 64)
        DH = C // H
        DHE = DH // 2
        THETA = 10000.0

        def _rope_cache(t, dim):
            inv_freq = 1.0 / THETA ** (jnp.arange(0, dim, 2, dtype=jnp.float32) / dim)
            freqs = jnp.arange(t, dtype=jnp.float32)[:, None] * inv_freq[None, :]
            emb = jnp.concatenate((freqs, freqs), axis=-1)
            return (jnp.cos(emb), jnp.sin(emb))

        def _apply_rope(x, cos, sin):
            x1 = x[..., 0::2]
            x2 = x[..., 1::2]
            rot = jnp.stack((-x2, x1), axis=-1).reshape(x.shape)
            return x * cos[None, None] + rot * sin[None, None]
        b, t, c = x.shape
        q_lat = (x @ Wq_down).reshape(b, t, H, L)
        k_lat = (x @ Wk_down).reshape(b, t, H, L)
        v_lat = (x @ Wv_down).reshape(b, t, H, L)
        q_c = jnp.einsum('bthl,ld->bhtd', q_lat, Wq_up_c)
        q_e = jnp.einsum('bthl,ld->bhtd', q_lat, Wq_up_e)
        k_c = jnp.einsum('bthl,ld->bhtd', k_lat, Wk_up_c)
        k_e = jnp.einsum('bthl,ld->bhtd', k_lat, Wk_up_e)
        v = jnp.einsum('bthl,ld->bhtd', v_lat, Wv_up)
        cos, sin = _rope_cache(t, DHE)
        q = jnp.concatenate([q_c, _apply_rope(q_e, cos, sin)], axis=-1)
        k = jnp.concatenate([k_c, _apply_rope(k_e, cos, sin)], axis=-1)
        scale = 1.0 / math.sqrt(DH)
        scores = jnp.einsum('bhqd,bhkd->bhqk', q, k) * scale
        causal = jnp.tril(jnp.ones((t, t), dtype=bool))
        scores = jnp.where(causal[None, None], scores, -jnp.inf)
        att = jax.nn.softmax(scores, axis=-1)
        y = jnp.einsum('bhqk,bhkd->bhqd', att, v)
        y = y.transpose(0, 2, 1, 3).reshape(b, t, c)
        return y @ Wc

    def _L0_ffn_ref(x, Wqkv, q_scale, k_scale, Wo, ln_g, ln_b, W1, b1, W2, b2):
        import jax, jax.numpy as jnp
        import numpy as np
        DIM = 128
        DEPTH = 6
        HEADS = 16
        DIM_HEAD = 64
        WINDOW = 32
        INNER = HEADS * DIM_HEAD
        DIM_INNER = int(DIM * 4 * 2 / 3)
        QK_SCALE = 8.0

        def shift_tokens(t):
            a, s = jnp.split(t, 2, -1)
            s = jnp.pad(s, ((0, 0), (1, 0), (0, 0)))[:, :-1]
            return jnp.concatenate([a, s], -1)

        def l2norm(t):
            return t / jnp.maximum(jnp.linalg.norm(t, axis=-1, keepdims=True), 1e-12)

        def rotate_half(x):
            x1, x2 = jnp.split(x, 2, -1)
            return jnp.concatenate([-x2, x1], -1)

        def rotary_tables(n):
            half = jnp.arange(0, DIM_HEAD, 2, dtype=jnp.float32)
            inv_freq = 1.0 / 10000.0 ** (half / DIM_HEAD)
            t = jnp.arange(n, dtype=jnp.float32)
            freqs = t[:, None] * inv_freq[None, :]
            freqs = jnp.concatenate([freqs, freqs], -1)
            base_scale = (half + 0.4 * DIM_HEAD) / (1.4 * DIM_HEAD)
            power = (t - n // 2) / (WINDOW // 2)
            scale = base_scale[None, :] ** power[:, None]
            scale = jnp.concatenate([scale, scale], -1)
            return (freqs, scale)

        def local_attention(q, k, v):
            b, h, n, d = q.shape
            w = WINDOW
            nw = n // w
            bq = q.reshape(b, h, nw, w, d)
            bk = k.reshape(b, h, nw, w, d)
            bv = v.reshape(b, h, nw, w, d)

            def look(t):
                p = jnp.pad(t, ((0, 0), (0, 0), (1, 0), (0, 0), (0, 0)))
                return jnp.concatenate([p[:, :, :nw], p[:, :, 1:]], axis=3)
            bk2, bv2 = (look(bk), look(bv))
            seq = jnp.arange(n).reshape(nw, w)
            seq_p = jnp.pad(seq, ((1, 0), (0, 0)), constant_values=-1)
            jt = jnp.concatenate([seq_p[:nw], seq_p[1:]], axis=1)
            it = seq[:, :, None]
            jb = jt[:, None, :]
            mask = (it < jb) | (it > jb + w) | (jb == -1)
            sim = jnp.einsum('bhwie,bhwje->bhwij', bq, bk2) * QK_SCALE
            sim = jnp.where(mask, -jnp.finfo(sim.dtype).max, sim)
            attn = jax.nn.softmax(sim, -1)
            out = jnp.einsum('bhwij,bhwje->bhwie', attn, bv2)
            return out.reshape(b, h, n, d)

        def attn_layer(x, Wqkv, qs, ksc, Wo):
            b, n, _ = x.shape
            qkv = x @ Wqkv
            q, k, v = jnp.split(qkv, 3, -1)
            sh = lambda t: t.reshape(b, n, HEADS, DIM_HEAD).transpose(0, 2, 1, 3)
            q, k, v = (sh(q), sh(k), sh(v))
            q = l2norm(q) * qs
            k = l2norm(k) * ksc
            freqs, scale = rotary_tables(n)
            cos, sin = (jnp.cos(freqs), jnp.sin(freqs))
            q = q * cos * scale + rotate_half(q) * sin * scale
            inv = 1.0 / scale
            k = k * cos * inv + rotate_half(k) * sin * inv
            out = local_attention(q, k, v)
            out = out.transpose(0, 2, 1, 3).reshape(b, n, INNER)
            return out @ Wo

        def ffn_layer(x, g, bln, W1, b1, W2, b2):
            mu = x.mean(-1, keepdims=True)
            var = ((x - mu) ** 2).mean(-1, keepdims=True)
            xn = (x - mu) / jnp.sqrt(var + 1e-05) * g + bln
            hg = xn @ W1 + b1
            a, gate = jnp.split(hg, 2, -1)
            return a * jax.nn.gelu(gate, approximate=False) @ W2 + b2
        for i in range(DEPTH):
            x = attn_layer(shift_tokens(x), Wqkv[i], q_scale[i], k_scale[i], Wo[i]) + x
            x = ffn_layer(shift_tokens(x), ln_g[i], ln_b[i], W1[i], b1[i], W2[i], b2[i]) + x
        return x
    x = L0_attn_x
    xn = _layernorm(x, axis=-1)
    x = x + _L0_attn_ref(xn, L0_attn_Wq_down, L0_attn_Wk_down, L0_attn_Wv_down, L0_attn_Wq_up_c, L0_attn_Wq_up_e, L0_attn_Wk_up_c, L0_attn_Wk_up_e, L0_attn_Wv_up, L0_attn_Wc) + _L0_ffn_ref(xn, L0_ffn_Wqkv, L0_ffn_q_scale, L0_ffn_k_scale, L0_ffn_Wo, L0_ffn_ln_g, L0_ffn_ln_b, L0_ffn_W1, L0_ffn_b1, L0_ffn_W2, L0_ffn_b2)
    return x

_drawn_inputs = setup_inputs


def setup_inputs(seed=0):
    import zlib

    import numpy as np

    out = dict(_drawn_inputs(seed))
    spreads = {'L0_ffn_q_scale': (1.0, 0.6),
     'L0_ffn_k_scale': (1.0, 0.6),
     'L0_ffn_ln_g': (1.0, 0.6),
     'L0_ffn_ln_b': (0.0, 0.8),
     'L0_ffn_b1': (0.0, 0.8),
     'L0_ffn_b2': (0.0, 0.1)}
    factors = {'L0_attn_Wq_down': 8.0,
     'L0_attn_Wk_down': 8.0,
     'L0_attn_Wv_down': 8.0,
     'L0_attn_Wq_up_c': 8.0,
     'L0_attn_Wq_up_e': 8.0,
     'L0_attn_Wk_up_c': 8.0,
     'L0_attn_Wk_up_e': 8.0,
     'L0_attn_Wv_up': 8.0,
     'L0_attn_Wc': 8.0,
     'L0_ffn_W1': 3.638,
     'L0_ffn_W2': 3.573}
    for name, (base, spread) in spreads.items():
        noise = np.random.default_rng([zlib.crc32(name.encode()), seed]).standard_normal(out[name].shape)
        drawn = base * np.exp(spread * noise) if base else spread * noise
        out[name] = jnp.asarray(drawn.astype(out[name].dtype))
    for name, factor in factors.items():
        out[name] = (out[name] * factor).astype(out[name].dtype)
    return out
```

```python
import math
from contextlib import ExitStack

import numpy as np

import concourse.bass as bass
from concourse import mybir

F32, F32R, BF16 = mybir.dt.float32, mybir.dt.float32r, mybir.dt.bfloat16
ACT = mybir.ActivationFunctionType
ALU = mybir.AluOpType
AX = mybir.AxisListType

P = 128
B, T, C = 8, 512, 128
TT = T // P
NTOK = B * T
HEADS, DA, LAT = 16, 8, 64
DEPTH, D, WIN = 6, 64, 32
HP = HEADS // 2
INNER = HEADS * D
FF = 341
FCH = [(0, 128), (128, 128), (256, FF - 256)]
MASKED = -1.0e30
AREA = 25856
OUT_PARTS = (((6, 3), (5, 1)), ((5, 2), (4, 0)))
LAG = 6


def shape_constants():
    f32 = np.float32
    half = np.arange(0, D, 2, dtype=f32)
    inv_freq = (f32(1.0) / np.power(f32(10000.0), half / f32(D))).astype(f32)
    t = np.arange(T, dtype=f32)
    freqs = (t[:, None] * inv_freq[None, :]).astype(f32)
    freqs = np.concatenate([freqs, freqs], -1)
    base = ((half + f32(0.4 * D)) / f32(1.4 * D)).astype(f32)
    power = ((t - T // 2) / (WIN // 2)).astype(f32)
    scale = (base[None, :] ** power[:, None]).astype(f32)
    scale = np.concatenate([scale, scale], -1)
    sign = np.where(np.arange(D) < D // 2, -1.0, 1.0).astype(f32)
    cos, sin = np.cos(freqs), np.sin(freqs) * sign
    rot = np.stack([np.stack([cos * scale * 8, sin * scale * 8], 1), np.stack([cos / scale, sin / scale], 1)], 1)
    rot = rot.reshape(TT, P, 2, 2, D).transpose(1, 0, 2, 3, 4).astype(f32)
    inv4 = (f32(1.0) / np.power(f32(10000.0), np.arange(0, 4, 2, dtype=f32) / f32(4))).astype(f32)
    fr = (t[:, None] * inv4[None, :]).astype(f32)
    fr = np.concatenate([fr, fr], -1)
    s4 = np.array([-1, 1, -1, 1], f32)
    ca = np.concatenate([np.ones((T, 4), f32), np.cos(fr)], -1)
    sa = np.concatenate([np.zeros((T, 4), f32), np.sin(fr) * s4], -1)
    ca, sa = np.tile(ca, (1, HEADS)).T, np.tile(sa, (1, HEADS)).T
    qs = f32(1.0 / math.sqrt(DA))
    crot = np.stack([ca * qs, sa * qs, ca, sa], 1).astype(f32)
    row, key = np.arange(P), np.arange(2 * WIN)
    q = row % WIN
    ok = (key[None] >= q[:, None]) & (key[None] <= q[:, None] + WIN)
    first = ok & ((row[:, None] >= 2 * WIN) | (key[None] >= WIN))
    lmask = np.stack([np.tile(np.where(m, 0.0, MASKED), (1, HP)) for m in (first, ok)], 1)
    tri = np.where(np.arange(P)[None] <= np.arange(P)[:, None], 0.0, MASKED)
    bf = mybir.dt.np(BF16)
    return {
        "c_rot": rot, "c_crot": crot, "c_lmask": lmask.astype(bf), "c_tri": tri.astype(bf),
        "c_id": np.eye(P, dtype=f32), "c_idb": np.eye(P, dtype=f32).astype(bf),
        "c_hm": (np.arange(P)[:, None] // DA == np.arange(HEADS)[None]).astype(f32),
        "c_avg": np.full((P, P), 1.0 / C, f32),
    }


def build(nc, ins, out, layers=DEPTH):
    ctx = ExitStack()
    with ctx:
        def sb(name, shape, dt=F32):
            return ctx.enter_context(nc.sbuf_tensor("sb_" + name, [P] + shape, dt))

        def sem(name):
            return ctx.enter_context(nc.semaphore("s_" + name))

        scratch = nc.dram_tensor("x_plus_causal", [B, TT, P, C], F32, kind="Internal").ap()
        xd = ins["x"].rearrange("b (t p) c -> b p t c", p=P)
        scr = scratch.rearrange("b t p c -> b p t c")
        od = out.rearrange("b (t p) c -> b p t c", p=P)

        xT = sb("xT", [NTOK])
        ident = sb("ident", [P])
        identb = sb("identb", [P], BF16)
        lmask = sb("lmask", [2, HP * 2 * WIN], BF16)
        tri = sb("tri", [P], BF16)
        hm = sb("hm", [HEADS])
        avg = sb("avg", [P])
        eps = sb("eps", [1])
        wqk_hi, wqk_lo = sb("wqk_hi", [2 * INNER], F32R), sb("wqk_lo", [2 * INNER], F32R)
        wo_bd = sb("wo_bd", [HP, 2, C])
        wvo = sb("wvo", [HEADS, C])
        w1_hi, w1_lo = sb("w1_hi", [2 * FF], F32R), sb("w1_lo", [2 * FF], F32R)
        w2 = sb("w2", [3, C])
        b1 = sb("b1", [6])
        lng = sb("lng", [3])
        rot = sb("rot", [TT, 2, 2, D])
        rots = sb("rots", [TT, 2, 2, D])
        qks = sb("qks", [2, 2, D])
        xs_hi, xs_lo = sb("xs_hi", [WIN + T], F32R), sb("xs_lo", [WIN + T], F32R)
        xwin = sb("xwin", [TT, 2, 4, P], F32R)
        p2 = sb("p2", [2, HP, 2, 2 * WIN], F32R)
        ptT = sb("ptT", [2, HP, P], F32R)
        ssq, lnb, rn = sb("ssq", [2, 2, 16]), sb("lnb", [2, 2, 16]), sb("rn", [2, 2, 16])
        smax, ssum, srec = sb("smax", [2, HP]), sb("ssum", [2, HP]), sb("srec", [2, HP])
        area = sb("area", [AREA])
        at = [0]

        def take(*shape):
            n = int(np.prod(shape))
            v = area[:, at[0]:at[0] + n]
            at[0] += n
            if len(shape) == 1:
                return v
            names = " ".join("abcde"[:len(shape)])
            return v.rearrange(f"p ({names}) -> p {names}", **dict(zip("abcde", shape)))

        ysb = take(2, 8, HEADS * WIN)
        qbd = take(2, HP, 4, 2, WIN)
        kT = take(HP, WIN + T)
        sqb, t1, t2 = take(2, 512), take(2, 512), take(2, 512)
        qsum, qn = take(2, 512), take(4, 512)
        dd, pn = take(2, 512), take(2, 512)
        xdup = take(2, 4, 2, 2, WIN)
        at[0] = 0
        xn_all = take(NTOK)
        wqk_raw, wv_raw = take(2 * INNER), take(HP, C)
        lx, ld, lsq, lrs = take(2, 512), take(2, 512), take(2, 512), take(2, 512)
        gg = take(2, 3, 512)
        uu = take(2, 3, 512)
        w1 = take(2 * FF)
        at[0] = 0
        v16 = take(TT, HEADS * (P + DA))
        ptA = take(2, TT, T)
        ea, pa = take(2, 512), take(2, 512)
        crot = take(4, T)
        qm = take(2, T)
        qT, kTc = take(T), take(T)
        ra, rb_ = take(T), take(T)
        yT = take(T)
        xb = take(T)
        wcomb = take(5, P)
        upq, upk, upv = take(2, 16), take(2, 16), take(2, 8)
        wc = take(C)
        xres = take(2, TT, C)
        assert at[0] <= AREA
        wd = area[:, 8704 + 512:8704 + 512 + 3 * 1024].rearrange("p (a b c) -> p a b c", a=3, b=HP)
        xtok = area[:, 0:NTOK].rearrange("p (n c) -> p n c", c=C)
        xsq = area[:, NTOK:2 * NTOK].rearrange("p (n c) -> p n c", c=C)
        nmx, lse, lre = sb("nmx", [8]), sb("lse", [8]), sb("lre", [8])
        lnm, lnv = sb("lnm", [NTOK // P]), sb("lnv", [NTOK // P])
        mlp = p2[:, :, :, :, :].rearrange("p a b c d -> p (a b c d)").rearrange("p (s e t) -> p s e t", s=2, e=2)
        mlp_hi, mlp_lo = mlp[:, 0], mlp[:, 1]
        spare = sb("spare", [32])

        ps = [ctx.enter_context(nc.psum_tensor(f"bank{i}", [P, 512], F32)) for i in range(8)]
        pj, rbank, sbank, tbank, ybank, mbank = ps[0:2], ps[2], ps[3], ps[4], ps[5:7], ps[7]

        S = {n: sem(n) for n in (
            "const", "xload", "c_weights", "eps_set", "v16_zero", "wo_zero", "w_loaded", "w_loaded2",
            "upd", "wcomb_mm", "wcomb_ready",
            "ln0", "ln0a", "xn_tr", "xT_ready", "area_free",
            "xb_ready", "c_proj", "c_rope", "c_rope_part", "v_mm", "v_ready", "qm_ready", "c_score", "c_max",
            "c_exp", "c_rec", "c_p", "c_tr", "c_ptev", "c_pv", "yT_ready", "ca_mm", "res_in", "ca_sum", "ca_out",
            "qbd_zero", "w_split", "w_split_a", "rots_ready", "rots_part", "wvo_mm", "wvo_ready", "xs_part", "xs_ready",
            "proj", "sq", "rotd", "rot_part", "ssq", "ssq_raw", "ln_part", "rn", "add", "qn", "tr", "ev", "score",
            "smax", "sub", "exp", "ssum", "srec", "pn", "hi", "lo", "pt", "ptev", "yy", "yev0", "yev1",
            "xdup", "xwt", "xwev", "oo", "xupd",
            "lx", "lmean", "ldif", "lsq", "lvar", "lln", "lrs", "lmul", "xn", "mhi", "mlo", "gate", "gelu", "aa",
            "uu", "down", "mx",
            "f_in", "f_tr", "f_sum", "f_out",
        )}
        block = ctx.enter_context(nc.Block())

        def pipeline(eng, step):
            for t in range(LAG):
                step(t, 0, 0)
            with eng.Fori(0, B - 2) as i:
                for t in range(LAG, LAG + TT):
                    step(t, i, 1)
            for t in range(LAG, LAG + 2 * TT):
                step(t, B - 2, 2)

        def behind(t, i, part, lag):
            s = t - lag
            if (part == 0 and s < 0) or (part == 2 and s >= 2 * TT):
                return None
            return s % TT, i + s // TT

        @block.sync
        def _(sp):
            sp.dma_start(xtok, ins["x"].rearrange("b (t p) c -> p (b t) c", p=P)).then_inc(S["xload"], 16)
            for dst, name in ((ident, "c_id"), (identb, "c_idb"), (tri, "c_tri"), (hm, "c_hm"), (avg, "c_avg")):
                sp.dma_start(dst[:, :], ins[name]).then_inc(S["const"], 16)
            sp.dma_start(lmask[:, :, :], ins["c_lmask"]).then_inc(S["const"], 16)
            sp.dma_start(rot[:, :, :, :], ins["c_rot"]).then_inc(S["const"], 16)
            sp.wait_ge(S["xT_ready"], B)
            sp.dma_start(crot, ins["c_crot"]).then_inc(S["c_weights"], 16)
            for i, name in enumerate(("wqdT", "wkdT", "wvdT")):
                sp.dma_start(wd[:, i, :, :], ins[name]).then_inc(S["c_weights"], 16)
            for dst, name in ((upq, "upq"), (upk, "upk"), (upv, "upv")):
                sp.dma_start(dst, ins[name]).then_inc(S["c_weights"], 16)
            sp.dma_start(wc, ins["Wc"]).then_inc(S["c_weights"], 16)
            for b in range(B):
                sp.wait_ge(S["ca_sum"], b)
                sp.wait_ge(S["ca_out"], b * 16)
                sp.dma_start(xres[:, 0, :, :], xd[b]).then_inc(S["res_in"], 16)
                sp.wait_ge(S["ca_sum"], b + 1)
                sp.dma_start(scr[b], xres[:, 1, :, :]).then_inc(S["ca_out"], 16)
            sp.wait_ge(S["ca_out"], B * 16)

            for l in range(layers):
                sp.wait_ge(S["area_free"], 1)
                sp.wait_ge(S["wo_zero"], 1)
                sp.wait_ge(S["xupd"], l * (2 * B))
                sp.wait_ge(S["w_split"], l * 2)
                sp.wait_ge(S["wvo_mm"], l * 4)
                sp.dma_start(wqk_raw, ins["Wqkv"][l][:, 0:2 * INNER]).then_inc(S["w_loaded"], 16)
                sp.dma_start(wv_raw, ins["WvT"][l]).then_inc(S["w_loaded"], 16)
                sp.dma_start(wo_bd[0:64, :, 0, :], ins["Wo"][l][0]).then_inc(S["w_loaded"], 16)
                sp.dma_start(wo_bd[64:128, :, 1, :], ins["Wo"][l][1]).then_inc(S["w_loaded"], 16)
                sp.dma_start(qks[:, :, :, :], ins["qks"][l].unsqueeze(0).to_broadcast([P, 2, 2, D])).then_inc(S["w_loaded"], 16)
                sp.wait_ge(S["mx"], l * B)
                sp.wait_ge(S["xupd"], (l + 1) * (2 * B))
                sp.dma_start(w1, ins["W1"][l]).then_inc(S["w_loaded2"], 16)
                for j, (f0, fn) in enumerate(FCH):
                    sp.dma_start(w2[0:fn, j, :], ins["W2"][l][f0:f0 + fn, :]).then_inc(S["w_loaded2"], 16)
                    sp.dma_start(b1[0:fn, j:j + 1], ins["b1"][l][f0:f0 + fn, :]).then_inc(S["w_loaded2"], 16)
                    sp.dma_start(b1[0:fn, 3 + j:4 + j], ins["b1"][l][FF + f0:FF + f0 + fn, :]).then_inc(S["w_loaded2"], 16)
                for j, name in enumerate(("ln_g", "ln_b", "b2")):
                    sp.dma_start(lng[:, j:j + 1], ins[name][l]).then_inc(S["w_loaded2"], 16)

            sp.wait_ge(S["mx"], layers * B)
            for b in range(B):
                sp.wait_ge(S["f_sum"], b)
                sp.wait_ge(S["f_out"], b * 16)
                sp.dma_start(xres[:, 0, :, :], scr[b]).then_inc(S["f_in"], 16)
                sp.wait_ge(S["f_sum"], b + 1)
                sp.dma_start(od[b], xres[:, 1, :, :]).then_inc(S["f_out"], 16)
            sp.wait_ge(S["f_out"], B * 16)

        @block.tensor
        def _(pe):
            def mm(o, a, b, start=True, stop=True):
                return nc.tensor.matmul(o, a, b, start=start, stop=stop, skip_group_check=True)

            def split3(o, a_hi, a_lo, b_hi, b_lo):
                mm(o, a_hi, b_hi, True, False)
                mm(o, a_hi, b_lo, False, False)
                return mm(o, a_lo, b_hi, False, True)

            pe.wait_ge(S["const"], 7 * 16)
            pe.wait_ge(S["ln0"], 5)
            for b in range(B):
                if b >= 4:
                    pe.wait_ge(S["xT_ready"], b - 3)
                for t in range(TT):
                    m = nc.tensor.transpose(ps[b % 4][:, t * P:(t + 1) * P], xtok[:, b * TT + t, :], ident[:, :])
                m.then_inc(S["xn_tr"], 1)
            pe.wait_ge(S["c_weights"], 8 * 16)
            for i, (up, n) in enumerate(((upq, 16), (upk, 16), (upv, 8))):
                for hp in range(HP):
                    m = mm(ps[4 + i][:, hp * 2 * n:(hp + 1) * 2 * n], wd[:, i, hp, :],
                           up.rearrange("p a b -> p (a b)"))
                m.then_inc(S["wcomb_mm"], 1)
            pe.wait_ge(S["wcomb_ready"], 5)

            with pe.Fori(0, B) as b:
                pe.wait_ge(S["xb_ready"], b + 1)
                for i, bank in enumerate((5, 6, 5, 6)):
                    if i == 0:
                        pe.wait_ge(S["c_rope_part"], b * 4)
                    elif i == 2:
                        pe.wait_ge(S["c_rope_part"], b * 4 + 2)
                    mm(ps[bank][:, :], wcomb[:, i, :], xb).then_inc(S["c_proj"], 1)
                pe.wait_ge(S["ca_sum"], b)
                for t in range(TT):
                    m = mm(ps[7][:, t * P:(t + 1) * P], xb[:, t * P:(t + 1) * P], wcomb[:, 4, :])
                m.then_inc(S["v_mm"], 1)
                pe.wait_ge(S["c_rope"], 2 * b + 2)
                pe.wait_ge(S["yT_ready"], b)

                def score(n):
                    h, qt = n // TT, n % TT
                    if qt == 0:
                        pe.wait_ge(S["qm_ready"], b * HEADS + h + 1)
                    pe.wait_ge(S["c_exp"], b * (HEADS * TT) + n)
                    o = ps[n % 2]
                    mm(o[:, 0:(qt + 1) * P], qm[:, h % 2, qt * P:(qt + 1) * P], kTc[:, 0:(qt + 1) * P], True, False)
                    mm(o[:, qt * P:(qt + 1) * P], identb[:, :], tri[:, :], False, True).then_inc(S["c_score"], 1)

                def turn(n):
                    pe.wait_ge(S["c_p"], b * (HEADS * TT) + n + 2)
                    pe.wait_ge(S["c_ptev"], b * (HEADS * TT) + n)
                    for kt in range(n % TT + 1):
                        m = nc.tensor.transpose(ps[2 + n % 2][:, kt * P:(kt + 1) * P],
                                                pa[:, n % 2, kt * P:(kt + 1) * P], ident[:, :])
                    m.then_inc(S["c_tr"], 1)

                def weigh(h):
                    pe.wait_ge(S["c_ptev"], b * (HEADS * TT) + h * TT + TT + 1)
                    if h == 0:
                        pe.wait_ge(S["v_ready"], b + 1)
                    for kt in range(TT):
                        m = mm(ps[4][:, kt * P:T], v16[:, kt, h * P:(h + 1) * P], ptA[:, h % 2, kt, kt * P:T],
                               h == 0 and kt == 0, h == HEADS - 1 and kt == TT - 1)
                    m.then_inc(S["c_pv"], 1)

                for n in range(HEADS * TT + 3):
                    if n < HEADS * TT:
                        score(n)
                    if 2 <= n < HEADS * TT + 2:
                        turn(n - 2)
                    if n > TT and (n - 2) % TT == 0:
                        weigh((n - 2) // TT - 1)
                pe.wait_ge(S["yT_ready"], b + 1)
                for t in range(TT):
                    m = mm(ps[7][:, t * P:(t + 1) * P], yT[:, t * P:(t + 1) * P], wc)
                m.then_inc(S["ca_mm"], 1)

            with pe.Fori(0, layers) as l:
                pe.wait_ge(S["w_loaded"], (l + 1) * (5 * 16))
                pe.wait_ge(S["wo_zero"], 1)
                pe.wait_ge(S["mx"], l * B)
                for g in range(4):
                    for j in range(2):
                        hp = 2 * g + j
                        m = mm(ps[g][:, j * 256:(j + 1) * 256], wv_raw[:, hp, :],
                               wo_bd[:, hp, :, :].rearrange("p a b -> p (a b)"))
                    m.then_inc(S["wvo_mm"], 1)
                pe.wait_ge(S["w_split"], 2 * l + 2)
                pe.wait_ge(S["wvo_ready"], 4 * l + 4)

                def step(t, i, part):
                    def g_of(bt):
                        return l * B + bt

                    def project(c):
                        if not (v := behind(t, i, part, 0)):
                            return
                        tt, bt = v
                        if c == 0:
                            pe.wait_ge(S["xs_ready"], g_of(bt) * 4 + tt + 1)
                        g = g_of(bt) * 16 + (4 * tt + c)
                        pe.wait_ge(S["sq"], g)
                        pe.wait_ge(S["rotd"], g)
                        s = slice(WIN + tt * P, WIN + (tt + 1) * P)
                        w = slice(c * 512, (c + 1) * 512)
                        split3(pj[c % 2][:, :], xs_hi[:, s], xs_lo[:, s], wqk_hi[:, w], wqk_lo[:, w])\
                            .then_inc(S["proj"], 1)

                    def turn_qk(c):
                        if not (v := behind(t, i, part, 1)):
                            return
                        tt, bt = v
                        g = g_of(bt) * 16 + (4 * tt + c)
                        pe.wait_ge(S["qn"], g + 7)
                        if c % 2:
                            pe.wait_ge(S["xwev"], (g_of(bt) * 4 + tt) * 2 + c // 2 + 1)
                        else:
                            pe.wait_ge(S["ev"], g)
                        for j in range(4):
                            m = nc.tensor.transpose(rbank[:, j * P:(j + 1) * P], qn[:, c, j * P:(j + 1) * P],
                                                    ident[:, :])
                        m.then_inc(S["tr"], 1)

                    def score(wp):
                        if not (v := behind(t, i, part, 2)):
                            return
                        tt, bt = v
                        pe.wait_ge(S["ev"], g_of(bt) * 16 + 4 * tt + 4)
                        pe.wait_ge(S["sub"], g_of(bt) * 8 + 2 * tt + wp)
                        first = tt == 0 and wp == 0
                        mm(sbank[:, :], identb[:, :], lmask[:, 0 if first else 1, :], True, False)
                        for w2_ in range(2):
                            for hp in range(HP):
                                w = 2 * wp + w2_
                                k0 = tt * P + w * WIN
                                m = mm(sbank[64 * w2_:64 * w2_ + 64, hp * 64:(hp + 1) * 64],
                                       qbd[:, tt % 2, hp, w, :, :].rearrange("p a b -> p (a b)"),
                                       kT[:, hp, k0:k0 + 2 * WIN], False, w2_ == 1 and hp == HP - 1)
                        m.then_inc(S["score"], 1)

                    def turn_p(wp, half):
                        if not (v := behind(t, i, part, 3)):
                            return
                        tt, bt = v
                        m_ = g_of(bt) * 8 + 2 * tt + wp
                        pe.wait_ge(S["lo"], m_ + 2)
                        pe.wait_ge(S["ptev"], m_ * 2 + half)
                        for j in range(4):
                            m = nc.tensor.transpose(
                                tbank[:, j * P:(j + 1) * P],
                                p2[:, wp, 4 * half + j, :, :].rearrange("p a b -> p (a b)").bitcast(F32), ident[:, :])
                        m.then_inc(S["pt"], 1)

                    def weigh(lag, wp):
                        if not (v := behind(t, i, part, lag)):
                            return
                        tt, bt = v
                        m_ = g_of(bt) * 8 + 2 * tt + wp
                        pe.wait_ge(S["ptev"], m_ * 2 + 2)
                        pe.wait_ge(S["xwev"], (g_of(bt) * 4 + tt) * 2 + 2)
                        for w2_, free in ((0, "yev0"), (1, "yev1")):
                            pe.wait_ge(S[free], m_)
                            w = 2 * wp + w2_
                            rhs = ptT[:, wp, :, 64 * w2_:64 * w2_ + 64]
                            mm(ybank[w2_][:, :], xwin[:, tt, 0, w, :], rhs, True, False)
                            mm(ybank[w2_][:, :], xwin[:, tt, 1, w, :], rhs, False, True).then_inc(S["yy"], 1)

                    def windows(hl):
                        if not (v := behind(t, i, part, 1)):
                            return
                        tt, bt = v
                        g = g_of(bt) * 4 + tt
                        pe.wait_ge(S["xdup"], g * 2 + hl + 1)
                        pe.wait_ge(S["ev"], g * 4 + 2 * hl + 1)
                        for w in range(4):
                            m = nc.tensor.transpose(rbank[:, w * P:(w + 1) * P],
                                                    xdup[:, hl, w, :, :, :].rearrange("p a b c -> p (a b c)"), ident[:, :])
                        m.then_inc(S["xwt"], 1)

                    def project_out(wp):
                        for lag, k in OUT_PARTS[wp]:
                            v = behind(t, i, part, lag)
                            if not v or v[0] % 2 == 0:
                                continue
                            tt, bt = v
                            hf = tt // 2
                            if k == 0:
                                pe.wait_ge(S["yev0"], g_of(bt) * 8 + 2 * tt + 2)
                                pe.wait_ge(S["yev1"], g_of(bt) * 8 + 2 * tt + 2)
                                pe.wait_ge(S["xupd"], g_of(bt) * 2 + hf)
                            for h in range(4 * k, 4 * k + 4):
                                m = mm(mbank[:, 0:256], wvo[:, h, :], ysb[:, hf, :, h * WIN:(h + 1) * WIN],
                                       h == 0, h == HEADS - 1)
                            if k == 3:
                                m.then_inc(S["oo"], 1)

                    for wp in range(2):
                        project(2 * wp)
                        turn_qk(2 * wp)
                        turn_p(wp, 0)
                        project(2 * wp + 1)
                        score(wp)
                        windows(wp)
                        turn_p(wp, 1)
                        weigh(4 - wp, 1 - wp)
                        turn_qk(2 * wp + 1)
                        project_out(wp)

                pipeline(pe, step)

                with pe.Fori(0, B // 2) as j:
                    for e in range(2):
                        pe.wait_ge(S["lx"], l * B + 2 * j + e + 1)
                        if e == 0:
                            pe.wait_ge(S["ldif"], l * B + 2 * j)
                        mm(ps[e][:, :], avg[:, :], lx[:, e, :]).then_inc(S["lmean"], 1)
                    for e in range(2):
                        pe.wait_ge(S["lsq"], l * B + 2 * j + e + 1)
                        if e == 0:
                            pe.wait_ge(S["lln"], l * B + 2 * j)
                        mm(ps[2 + e][:, :], avg[:, :], lsq[:, e, :]).then_inc(S["lvar"], 1)
                with pe.Fori(0, B // 2) as j:
                    pe.wait_ge(S["lln"], (l + 1) * B)
                    pe.wait_ge(S["w_split_a"], 2 * l + 2)
                    for e in range(2):
                        n = l * B + 2 * j + e
                        pe.wait_ge(S["mlo"], n + 1)
                        pe.wait_ge(S["gelu"], n * 3)
                        for c, (f0, fn) in enumerate(FCH):
                            f = slice(FF + f0, FF + f0 + fn)
                            split3(ps[c][0:fn, :], w1_hi[:, f], w1_lo[:, f], mlp_hi[:, e, :], mlp_lo[:, e, :])\
                                .then_inc(S["gate"], 1)
                        pe.wait_ge(S["uu"], n * 3)
                        for c, (f0, fn) in enumerate(FCH):
                            f = slice(f0, f0 + fn)
                            split3(ps[3 + c][0:fn, :], w1_hi[:, f], w1_lo[:, f], mlp_hi[:, e, :], mlp_lo[:, e, :])\
                                .then_inc(S["aa"], 1)
                        pe.wait_ge(S["uu"], n * 3 + 3)
                        pe.wait_ge(S["mx"], n)
                        for c, (f0, fn) in enumerate(FCH):
                            m = mm(ps[6 + e][:, :], w2[0:fn, c, :], uu[0:fn, e, c, :], c == 0, c == 2)
                        m.then_inc(S["down"], 1)

            pe.wait_ge(S["mx"], layers * B)
            with pe.Fori(0, B) as b:
                pe.wait_ge(S["xb_ready"], b + (B + 1))
                pe.wait_ge(S["f_sum"], b)
                for t in range(TT):
                    m = nc.tensor.transpose(ps[0][:, t * P:(t + 1) * P], xb[:, t * P:(t + 1) * P], ident[:, :])
                m.then_inc(S["f_tr"], 1)

        @block.scalar
        def _(act):
            def copy(o, i):
                return nc.scalar.activation(o, i, ACT.Copy)

            nc.scalar.preload_act_table_set("natural_log_exp_and_others")
            act.wait_ge(S["ln0"], 3)
            nc.scalar.activation(xsq, xtok, ACT.Square).then_inc(S["ln0a"], 1)
            act.wait_ge(S["ln0"], 4)
            act.wait_ge(S["eps_set"], 1)
            nc.scalar.activation(lnm[:, :], lnv[:, :], ACT.Ln, bias=eps[:, :], scale=1.0 / C).then_inc(S["ln0a"], 1)
            act.wait_ge(S["ln0a"], 2)
            nc.scalar.activation(lnv[:, :], lnm[:, :], ACT.Exp, scale=-0.5).then_inc(S["ln0a"], 1)
            for b in range(B):
                act.wait_ge(S["xn_tr"], b + 1)
                copy(xT[:, b * T:(b + 1) * T], ps[b % 4][:, :]).then_inc(S["xT_ready"], 1)
            for i in range(2):
                act.wait_ge(S["wcomb_mm"], i + 1)
                src = ps[4 + i][:, 0:256].rearrange("p (h s d) -> p h s d", h=HEADS, s=2)
                for s in range(2):
                    copy(wcomb[:, 2 * i + s, :].rearrange("p (h d) -> p h d", h=HEADS), src[:, :, s, :])\
                        .then_inc(S["wcomb_ready"], 1)
            act.wait_ge(S["wcomb_mm"], 3)
            copy(wcomb[:, 4, :], ps[6][:, 0:128]).then_inc(S["wcomb_ready"], 1)

            with act.Fori(0, B) as b:
                act.wait_ge(S["v_mm"], b + 1)
                act.wait_ge(S["c_pv"], b * HEADS)
                act.wait_ge(S["v16_zero"], 1)
                copy(v16.rearrange("p k (h x) -> p k h x", x=P + DA)[:, :, :, 0:DA],
                     ps[7][:, :].rearrange("p (k h d) -> p k h d", k=TT, h=HEADS)).then_inc(S["v_ready"], 1)

                def exp(n):
                    qt, k = n % TT, n % 8
                    act.wait_ge(S["c_max"], b * (HEADS * TT) + n + 1)
                    act.wait_ge(S["c_p"], b * (HEADS * TT) + n)
                    nc.scalar.activation(ea[:, n % 2, 0:(qt + 1) * P], ps[n % 2][:, 0:(qt + 1) * P], ACT.Exp,
                                         bias=nmx[:, k:k + 1], accum_out=lse[:, k:k + 1]).then_inc(S["c_exp"], 1)

                def turned(n):
                    h, qt = n // TT, n % TT
                    if qt == 0 and h >= 2:
                        act.wait_ge(S["c_pv"], b * HEADS + h - 1)
                    act.wait_ge(S["c_tr"], b * (HEADS * TT) + n + 1)
                    copy(ptA[:, h % 2, 0:qt + 1, qt * P:(qt + 1) * P],
                         ps[2 + n % 2][:, 0:(qt + 1) * P].rearrange("p (k q) -> p k q", q=P))\
                        .then_inc(S["c_ptev"], 1)

                for n in range(HEADS * TT + 2):
                    if n < HEADS * TT:
                        exp(n)
                    if n >= 2:
                        turned(n - 2)
                act.wait_ge(S["c_pv"], b * HEADS + HEADS)
                act.wait_ge(S["ca_mm"], b)
                copy(yT, ps[4][:, :]).then_inc(S["yT_ready"], 1)

            with act.Fori(0, layers) as l:
                nc.scalar.preload_act_table_set("natural_log_exp_and_others")
                act.wait_ge(S["w_loaded"], (l + 1) * (5 * 16))
                act.wait_ge(S["xupd"], l * (2 * B))
                copy(wqk_hi[:, :], wqk_raw).then_inc(S["w_split"], 1)
                for g in range(4):
                    act.wait_ge(S["wvo_mm"], 4 * l + g + 1)
                    copy(wvo[:, 4 * g:4 * g + 4, :], ps[g][:, :].rearrange("p (a b) -> p a b", a=4))\
                        .then_inc(S["wvo_ready"], 1)

                def step(t, i, part):
                    def g_of(bt):
                        return l * B + bt

                    def square(c):
                        if not (v := behind(t, i, part, 0)):
                            return
                        tt, bt = v
                        g = g_of(bt) * 16 + (4 * tt + c)
                        act.wait_ge(S["proj"], g + 1)
                        act.wait_ge(S["ssq_raw"], g)
                        nc.scalar.activation(sqb[:, c % 2, :], pj[c % 2][:, :], ACT.Square).then_inc(S["sq"], 1)

                    def norms(half):
                        if not (v := behind(t, i, part, 0)):
                            return
                        tt, bt = v
                        n = (g_of(bt) * 4 + tt) * 2 + half
                        act.wait_ge(S["ssq"], n + 1)
                        nc.scalar.activation(lnb[:, tt % 2, half, :], ssq[:, tt % 2, half, :], ACT.Ln)\
                            .then_inc(S["ln_part"], 1)
                        act.wait_ge(S["ln_part"], n + 4)
                        act.wait_ge(S["qn"], (g_of(bt) * 16 + 4 * tt + 2 * half))
                        nc.scalar.activation(rn[:, tt % 2, half, :], lnb[:, tt % 2, half, :], ACT.Exp, scale=-0.5)\
                            .then_inc(S["rn"], 1)

                    def turned_qk(c):
                        if not (v := behind(t, i, part, 1)):
                            return
                        tt, bt = v
                        act.wait_ge(S["tr"], g_of(bt) * 16 + (4 * tt + c) + 4)
                        if c == 0:
                            act.wait_ge(S["score"], (g_of(bt) * 4 + tt) * 2)
                        src = rbank[:, :].rearrange("p (j w q) -> p j w q", j=4, w=4)
                        if c < 2:
                            for h2 in range(2):
                                r = slice(64 * h2, 64 * h2 + 64)
                                m = copy(qbd[r, tt % 2, 4 * c:4 * c + 4, :, h2, :], src[r])
                        else:
                            m = copy(kT[:, 4 * (c - 2):4 * (c - 2) + 4, WIN + tt * P:WIN + (tt + 1) * P],
                                     rbank[:, :].rearrange("p (j q) -> p j q", j=4))
                        m.then_inc(S["ev"], 1)

                    def exp(wp):
                        if not (v := behind(t, i, part, 2)):
                            return
                        tt, bt = v
                        act.wait_ge(S["sub"], g_of(bt) * 8 + 2 * tt + wp + 1)
                        nc.scalar.activation(dd[:, wp, :], dd[:, wp, :], ACT.Exp).then_inc(S["exp"], 1)

                    def heads_of_p(lag, wp):
                        if not (v := behind(t, i, part, lag)):
                            return
                        tt, bt = v
                        m_ = g_of(bt) * 8 + 2 * tt + wp
                        act.wait_ge(S["pn"], m_ + 1)
                        act.wait_ge(S["pt"], m_ * 2)
                        copy(p2[:, wp, :, 0, :], pn[:, wp, :].rearrange("p (h k) -> p h k", h=HP)).then_inc(S["hi"], 1)

                    def turned_p(wp, half):
                        if not (v := behind(t, i, part, 3)):
                            return
                        tt, bt = v
                        m_ = g_of(bt) * 8 + 2 * tt + wp
                        act.wait_ge(S["pt"], m_ * 2 + half + 3)
                        act.wait_ge(S["yy"], m_ * 2)
                        copy(ptT[:, wp, 4 * half:4 * half + 4, :],
                             tbank[:, :].rearrange("p (j q) -> p j q", j=4)).then_inc(S["ptev"], 1)

                    def weighed(lag, wp):
                        if not (v := behind(t, i, part, lag)):
                            return
                        tt, bt = v
                        m_ = g_of(bt) * 8 + 2 * tt + wp
                        act.wait_ge(S["yy"], m_ * 2 + 3)
                        act.wait_ge(S["oo"], g_of(bt) * 2 + tt // 2)
                        copy(ysb[:, tt // 2, 4 * (tt % 2) + 2 * wp, :], ybank[0][:, :]).then_inc(S["yev0"], 1)
                        act.wait_ge(S["yy"], m_ * 2 + 4)
                        copy(ysb[:, tt // 2, 4 * (tt % 2) + 2 * wp + 1, :], ybank[1][:, :]).then_inc(S["yev1"], 1)

                    def windows(hl):
                        if not (v := behind(t, i, part, 1)):
                            return
                        tt, bt = v
                        g = g_of(bt) * 4 + tt
                        act.wait_ge(S["xwt"], g * 2 + hl + 2)
                        if hl == 0 and not (part == 0 and t - 1 < TT):
                            act.wait_ge(S["yy"], g * 4 - 10)
                        copy(xwin[:, tt, hl, :, :], rbank[:, :].rearrange("p (w c) -> p w c", w=4))\
                            .then_inc(S["xwev"], 1)

                    for wp in range(2):
                        square(2 * wp)
                        turned_qk(2 * wp)
                        turned_p(wp, 0)
                        square(2 * wp + 1)
                        windows(wp)
                        turned_p(wp, 1)
                        heads_of_p(3 - wp, 1 - wp)
                        weighed(4 - wp, 1 - wp)
                        turned_qk(2 * wp + 1)
                        exp(wp)
                        norms(wp)

                pipeline(act, step)

                with act.Fori(0, B // 2) as j:
                    for e in range(2):
                        n = l * B + 2 * j + e
                        act.wait_ge(S["ldif"], n + 1)
                        act.wait_ge(S["lvar"], l * B + 2 * j)
                        nc.scalar.activation(lsq[:, e, :], ld[:, e, :], ACT.Square).then_inc(S["lsq"], 1)
                    for e in range(2):
                        n = l * B + 2 * j + e
                        act.wait_ge(S["lvar"], n + 1)
                        act.wait_ge(S["xn"], l * B + 2 * j)
                        nc.scalar.activation(lrs[:, e, :], ps[2 + e][:, :], ACT.Ln, bias=eps[:, :])\
                            .then_inc(S["lln"], 1)
                    for e in range(2):
                        n = l * B + 2 * j + e
                        act.wait_ge(S["lln"], n + 1)
                        nc.scalar.activation(lrs[:, e, :], lrs[:, e, :], ACT.Exp, scale=-0.5).then_inc(S["lrs"], 1)
                act.wait_ge(S["w_loaded2"], (l + 1) * (13 * 16))
                act.wait_ge(S["mx"], l * B)
                copy(w1_hi[:, :], w1).then_inc(S["w_split_a"], 1)
                with act.Fori(0, B // 2) as j:
                    for e in range(2):
                        n = l * B + 2 * j + e
                        for c, (f0, fn) in enumerate(FCH):
                            act.wait_ge(S["gate"], n * 3 + c + 1)
                            if c == 0:
                                act.wait_ge(S["uu"], (l * B + 2 * j) * 3)
                            nc.scalar.activation(gg[0:fn, e, c, :], ps[c][0:fn, :], ACT.Gelu,
                                                 bias=b1[0:fn, 3 + c:4 + c]).then_inc(S["gelu"], 1)

        @block.vector
        def _(dve):
            tt_, ts_ = nc.vector.tensor_tensor, nc.vector.tensor_scalar

            def bc(v, shape, axis):
                return v.unsqueeze(axis).to_broadcast(shape)

            nc.vector.memset(eps[:, :], 1e-5).then_inc(S["eps_set"], 1)
            column = iter(range(32))
            for name, n in (("sq", 1), ("rotd", 1), ("ssq_raw", 1), ("add", 1), ("tr", 3), ("xwt", 1), ("score", 2), ("yy", 2),
                            ("pt", 2), ("qn", 6), ("ln_part", 3), ("lo", 1), ("oo", 1), ("c_exp", 1), ("c_p", 1),
                            ("c_ptev", 1)):
                for _ in range(n):
                    c = next(column)
                    nc.vector.memset(spare[:, c:c + 1], 0.0).then_inc(S[name], 1)

            dve.wait_ge(S["xload"], 16)
            n = NTOK // P
            nc.vector.tensor_reduce(lnm[:, :], xtok, AX.X, ALU.add).then_inc(S["ln0"], 1)
            dve.wait_ge(S["ln0"], 1)
            ts_(lnv[:, :], lnm[:, :], 1.0 / C, None, ALU.mult).then_inc(S["ln0"], 1)
            dve.wait_ge(S["ln0"], 2)
            tt_(xtok, xtok, bc(lnv[:, :], [P, n, C], 2), ALU.subtract).then_inc(S["ln0"], 1)
            dve.wait_ge(S["ln0a"], 1)
            nc.vector.tensor_reduce(lnv[:, :], xsq, AX.X, ALU.add).then_inc(S["ln0"], 1)
            dve.wait_ge(S["ln0a"], 3)
            dve.wait_ge(S["ln0"], 4)
            tt_(xtok, xtok, bc(lnv[:, :], [P, n, C], 2), ALU.mult).then_inc(S["ln0"], 1)
            dve.wait_ge(S["xT_ready"], B)
            nc.vector.memset(v16.rearrange("p a b -> p (a b)"), 0.0).then_inc(S["v16_zero"], 1)

            dve.wait_ge(S["c_weights"], 8 * 16)
            dve.wait_ge(S["const"], 7 * 16)
            with dve.Fori(0, B) as b:
                dve.wait_ge(S["v_mm"], b)
                nc.vector.tensor_copy(xb, xT[:, bass.ds(b * T, T)]).then_inc(S["xb_ready"], 1)
                dve.wait_ge(S["c_score"], b * (HEADS * TT))
                for i, dst in ((0, qT), (1, kTc)):
                    dve.wait_ge(S["c_proj"], b * 4 + 2 * i + 1)
                    if i == 1:
                        dve.wait_ge(S["c_rope"], 2 * b + 1)
                    tt_(ra, ps[5][:, :], crot[:, 2 * i, :], ALU.mult).then_inc(S["c_rope_part"], 1)
                    dve.wait_ge(S["c_proj"], b * 4 + 2 * i + 2)
                    tt_(rb_, ps[6][:, :], crot[:, 2 * i + 1, :], ALU.mult).then_inc(S["c_rope_part"], 1)
                    dve.wait_ge(S["c_rope_part"], b * 4 + 2 * i + 2)
                    tt_(dst, ra, rb_, ALU.add).then_inc(S["c_rope"], 1)
                dve.wait_ge(S["c_rope"], 2 * b + 2)

                def mask_q(h):
                    if h >= 2:
                        dve.wait_ge(S["c_score"], b * (HEADS * TT) + TT * (h - 1))
                    ts_(qm[:, h % 2, :], qT, hm[:, h:h + 1], None, ALU.mult).then_inc(S["qm_ready"], 1)

                mask_q(0)
                mask_q(1)

                def one_max(n):
                    qt, k = n % TT, n % 8
                    dve.wait_ge(S["c_score"], b * (HEADS * TT) + n + 1)
                    nc.vector.tensor_reduce(nmx[:, k:k + 1], ps[n % 2][:, 0:(qt + 1) * P], AX.X, ALU.max,
                                            negate=True).then_inc(S["c_max"], 1)

                def one_norm(n):
                    qt, k = n % TT, n % 8
                    dve.wait_ge(S["c_exp"], b * (HEADS * TT) + n + 2)
                    nc.vector.reciprocal(lre[:, k:k + 1], lse[:, k:k + 1]).then_inc(S["c_rec"], 1)
                    dve.wait_ge(S["c_rec"], b * (HEADS * TT) + n + 1)
                    dve.wait_ge(S["c_tr"], b * (HEADS * TT) + max(n - 1, 0))
                    ts_(pa[:, n % 2, 0:(qt + 1) * P], ea[:, n % 2, 0:(qt + 1) * P], lre[:, k:k + 1], None,
                        ALU.mult).then_inc(S["c_p"], 1)

                for n in range(HEADS * TT + 1):
                    if n < HEADS * TT:
                        one_max(n)
                    if n >= 1:
                        one_norm(n - 1)
                    if n % TT == TT - 1 and 2 <= n // TT + 2 < HEADS:
                        mask_q(n // TT + 2)
                dve.wait_ge(S["ca_mm"], b + 1)
                dve.wait_ge(S["res_in"], 16 * b + 16)
                tt_(xres[:, 1, :, :], ps[7][:, :].rearrange("p (t c) -> p t c", t=TT), xres[:, 0, :, :], ALU.add)\
                    .then_inc(S["ca_sum"], 1)

            dve.wait_ge(S["ca_sum"], B)
            dve.wait_ge(S["ca_out"], B * 16)
            nc.vector.memset(xs_hi[:, 0:WIN + 1].bitcast(F32), 0.0)
            nc.vector.memset(xs_lo[:, 0:WIN + 1].bitcast(F32), 0.0).then_inc(S["area_free"], 1)
            nc.vector.memset(wo_bd[:, :, :, :], 0.0).then_inc(S["wo_zero"], 1)

            with dve.Fori(0, layers) as l:
                dve.wait_ge(S["mx"], l * B)
                nc.vector.memset(qbd.rearrange("p a b c d e -> p (a b c d e)"), 0.0).then_inc(S["qbd_zero"], 1)
                nc.vector.memset(kT[:, :, 0:WIN], 0.0)
                dve.wait_ge(S["w_loaded"], (l + 1) * (5 * 16))
                dve.wait_ge(S["w_split"], 2 * l + 1)
                tt_(wqk_lo[:, :], wqk_raw, wqk_hi[:, :].bitcast(F32), ALU.subtract).then_inc(S["w_split"], 1)
                for s in range(2):
                    for u in range(2):
                        m = tt_(rots[:, :, s, u, :], rot[:, :, s, u, :], bc(qks[:, s, u, :], [P, TT, D], 1), ALU.mult)
                m.then_inc(S["rots_ready"], 1)
                dve.wait_ge(S["rots_ready"], l + 1)

                def load_tile(tt, bt):
                    g = (l * B + bt) * 4 + tt
                    dve.wait_ge(S["proj"], g * 4)
                    dve.wait_ge(S["xdup"], g * 2)
                    c0, base = WIN + tt * P, bt * T + tt * P
                    late = 1 if tt == 0 else 0
                    o, o1 = slice(c0, c0 + P), slice(c0 + late, c0 + P)
                    a, c = xT[0:64, bass.ds(base, P)], xT[64:128, bass.ds(base - 1 + late, P - late)]
                    nc.vector.tensor_copy(xs_hi[0:64, o], a)
                    nc.vector.tensor_copy(xs_hi[64:128, o1], c).then_inc(S["xs_part"], 1)
                    dve.wait_ge(S["xs_part"], g + 1)
                    tt_(xs_lo[0:64, o], a, xs_hi[0:64, o].bitcast(F32), ALU.subtract)
                    tt_(xs_lo[64:128, o1], c, xs_hi[64:128, o1].bitcast(F32), ALU.subtract).then_inc(S["xs_ready"], 1)

                def step(t, i, part):
                    def g_of(bt):
                        return l * B + bt

                    def load_next():
                        if v := behind(t, i, part, -1):
                            load_tile(*v)

                    def double_windows(hl):
                        if not (v := behind(t, i, part, 0)):
                            return
                        tt, bt = v
                        g = g_of(bt) * 4 + tt
                        dve.wait_ge(S["xs_ready"], g + 1)
                        dve.wait_ge(S["xwt"], g * 2 + hl)
                        src = (xs_hi, xs_lo)[hl]
                        for own in range(2):
                            c0 = tt * P + own * WIN
                            m = nc.vector.tensor_copy(
                                xdup[:, hl, :, :, own, :],
                                bc(src[:, c0:c0 + P].bitcast(F32).rearrange("p (w k) -> p w k", w=4), [P, 4, 2, WIN], 2))
                        m.then_inc(S["xdup"], 1)

                    def rotate(c):
                        if not (v := behind(t, i, part, 0)):
                            return
                        tt, bt = v
                        g = g_of(bt) * 16 + (4 * tt + c)
                        s = c // 2
                        dve.wait_ge(S["sq"], g + 2)
                        dve.wait_ge(S["add"], g)
                        src = pj[c % 2][:, :].rearrange("p (h d) -> p h d", h=8)
                        sv = pj[c % 2][:, :].rearrange("p (h e d) -> p h e d", h=8, e=2)
                        tt_(t1[:, c % 2, :].rearrange("p (h d) -> p h d", h=8), src,
                            bc(rots[:, tt, s, 0, :], [P, 8, D], 1), ALU.mult)
                        d4 = t2[:, c % 2, :].rearrange("p (h e d) -> p h e d", h=8, e=2)
                        for e in range(2):
                            m = tt_(d4[:, :, e, :], sv[:, :, 1 - e, :],
                                    bc(rots[:, tt, s, 1, e * 32:e * 32 + 32], [P, 8, 32], 1), ALU.mult)
                        m.then_inc(S["rotd"], 1)

                    def square_sums(c):
                        if not (v := behind(t, i, part, 0)):
                            return
                        tt, bt = v
                        g = g_of(bt) * 16 + (4 * tt + c)
                        half = c // 2
                        dve.wait_ge(S["sq"], g + 2)
                        if c % 2 == 0:
                            dve.wait_ge(S["ln_part"], g_of(bt) * 8 + 2 * tt + half)
                        nc.vector.tensor_reduce(ssq[:, tt % 2, half, 8 * (c % 2):8 * (c % 2) + 8],
                                                sqb[:, c % 2, :].rearrange("p (h d) -> p h d", h=8), AX.X, ALU.add)\
                            .then_inc(S["ssq_raw"], 1)
                        if c % 2:
                            dve.wait_ge(S["ssq_raw"], g + 2)
                            ts_(ssq[:, tt % 2, half, :], ssq[:, tt % 2, half, :], 1e-24, None, ALU.max)\
                                .then_inc(S["ssq"], 1)

                    def shift(wp):
                        if not (v := behind(t, i, part, 2)):
                            return
                        tt, bt = v
                        m_ = g_of(bt) * 8 + 2 * tt + wp
                        dve.wait_ge(S["score"], m_ + 3)
                        s3 = sbank[:, :].rearrange("p (h k) -> p h k", h=HP)
                        nc.vector.tensor_reduce(smax[:, wp, :], s3, AX.X, ALU.max).then_inc(S["smax"], 1)
                        dve.wait_ge(S["smax"], m_ + 1)
                        tt_(dd[:, wp, :].rearrange("p (h k) -> p h k", h=HP), s3,
                            bc(smax[:, wp, :], [P, HP, 64], 2), ALU.subtract).then_inc(S["sub"], 1)

                    def normalise(lag, wp):
                        if not (v := behind(t, i, part, lag)):
                            return
                        tt, bt = v
                        m_ = g_of(bt) * 8 + 2 * tt + wp
                        dve.wait_ge(S["exp"], m_ + 1)
                        d3 = dd[:, wp, :].rearrange("p (h k) -> p h k", h=HP)
                        nc.vector.tensor_reduce(ssum[:, wp, :], d3, AX.X, ALU.add).then_inc(S["ssum"], 1)
                        dve.wait_ge(S["ssum"], m_ + 1)
                        nc.vector.reciprocal(srec[:, wp, :], ssum[:, wp, :]).then_inc(S["srec"], 1)
                        dve.wait_ge(S["srec"], m_ + 1)
                        dve.wait_ge(S["lo"], m_)
                        tt_(pn[:, wp, :].rearrange("p (h k) -> p h k", h=HP), d3,
                            bc(srec[:, wp, :], [P, HP, 64], 2), ALU.mult).then_inc(S["pn"], 1)

                    def update():
                        v = behind(t, i, part, LAG)
                        if not v or v[0] % 2 == 0:
                            return
                        tt, bt = v
                        hf = tt // 2
                        dve.wait_ge(S["oo"], g_of(bt) * 2 + hf + 2)
                        dst = xT[:, bass.ds(bt * T + hf * 256, 256)]
                        tt_(dst, mbank[:, 0:256], dst, ALU.add).then_inc(S["xupd"], 1)

                    for wp in range(2):
                        normalise(3 - wp, 1 - wp)
                        rotate(2 * wp)
                        rotate(2 * wp + 1)
                        shift(wp)
                        square_sums(2 * wp)
                        square_sums(2 * wp + 1)
                        double_windows(wp)
                        if wp == 0:
                            update()
                        else:
                            load_next()

                dve.wait_ge(S["mx"], l * B)
                load_tile(0, 0)
                pipeline(dve, step)

                dve.wait_ge(S["xupd"], (l + 1) * (2 * B))
                nc.vector.memset(lx[64:128, :, 0:1], 0.0)
                with dve.Fori(0, B // 2) as j:
                    for e in range(2):
                        base = (2 * j + e) * T
                        if e == 0:
                            dve.wait_ge(S["lmean"], l * B + 2 * j)
                            dve.wait_ge(S["ldif"], l * B + 2 * j)
                        nc.vector.tensor_copy(lx[0:64, e, :], xT[0:64, bass.ds(base, T)])
                        nc.vector.tensor_copy(lx[64:128, e, 1:T], xT[64:128, bass.ds(base, T - 1)])\
                            .then_inc(S["lx"], 1)
                    for e in range(2):
                        n = l * B + 2 * j + e
                        dve.wait_ge(S["lmean"], n + 1)
                        dve.wait_ge(S["lx"], n + 1)
                        tt_(ld[:, e, :], lx[:, e, :], ps[e][:, :], ALU.subtract).then_inc(S["ldif"], 1)
                    for e in range(2):
                        n = l * B + 2 * j + e
                        dve.wait_ge(S["lrs"], n + 1)
                        tt_(lrs[:, e, :], ld[:, e, :], lrs[:, e, :], ALU.mult).then_inc(S["lmul"], 1)
                    dve.wait_ge(S["w_loaded2"], (l + 1) * (13 * 16))
                    for e in range(2):
                        n = l * B + 2 * j + e
                        dve.wait_ge(S["lmul"], n + 1)
                        ts_(xn_all[:, bass.ds((2 * j + e) * T, T)], lrs[:, e, :], lng[:, 0:1], lng[:, 1:2],
                            ALU.mult, ALU.add).then_inc(S["xn"], 1)

                dve.wait_ge(S["w_split_a"], 2 * l + 1)
                tt_(w1_lo[:, :], w1, w1_hi[:, :].bitcast(F32), ALU.subtract).then_inc(S["w_split_a"], 1)
                with dve.Fori(0, B // 2) as j:
                    dve.wait_ge(S["xn"], (l + 1) * B)
                    for e in range(2):
                        n = l * B + 2 * j + e
                        dve.wait_ge(S["aa"], (l * B + 2 * j) * 3)
                        src = xn_all[:, bass.ds((2 * j + e) * T, T)]
                        nc.vector.tensor_copy(mlp_hi[:, e, :], src).then_inc(S["mhi"], 1)
                        dve.wait_ge(S["mhi"], n + 1)
                        tt_(mlp_lo[:, e, :], src, mlp_hi[:, e, :].bitcast(F32), ALU.subtract).then_inc(S["mlo"], 1)
                    for e in range(2):
                        n = l * B + 2 * j + e
                        dve.wait_ge(S["down"], l * B + 2 * j)
                        for c, (f0, fn) in enumerate(FCH):
                            dve.wait_ge(S["aa"], n * 3 + c + 1)
                            dve.wait_ge(S["gelu"], n * 3 + c + 1)
                            nc.vector.scalar_tensor_tensor(uu[0:fn, e, c, :], ps[3 + c][0:fn, :], b1[0:fn, c:c + 1],
                                                           gg[0:fn, e, c, :], ALU.add, ALU.mult).then_inc(S["uu"], 1)
                    for e in range(2):
                        n = l * B + 2 * j + e
                        dve.wait_ge(S["down"], n + 1)
                        dst = xT[:, bass.ds((2 * j + e) * T, T)]
                        nc.vector.scalar_tensor_tensor(dst, ps[6 + e][:, :], lng[:, 2:3], dst, ALU.add, ALU.add)\
                            .then_inc(S["mx"], 1)

            dve.wait_ge(S["mx"], layers * B)
            with dve.Fori(0, B) as b:
                dve.wait_ge(S["f_tr"], b)
                nc.vector.tensor_copy(xb, xT[:, bass.ds(b * T, T)]).then_inc(S["xb_ready"], 1)
                dve.wait_ge(S["f_tr"], b + 1)
                dve.wait_ge(S["f_in"], 16 * b + 16)
                tt_(xres[:, 1, :, :], ps[0][:, :].rearrange("p (t c) -> p t c", t=TT), xres[:, 0, :, :], ALU.add)\
                    .then_inc(S["f_sum"], 1)

        @block.gpsimd
        def _(pool):
            pt_ = nc.gpsimd.tensor_tensor
            with pool.Fori(0, layers) as l:
                def step(t, i, part):
                    def g_of(bt):
                        return l * B + bt

                    def add(c):
                        if not (v := behind(t, i, part, 0)):
                            return
                        tt, bt = v
                        g = g_of(bt) * 16 + (4 * tt + c)
                        pool.wait_ge(S["qn"], g + 5)
                        pool.wait_ge(S["rotd"], g + 2)
                        pt_(qsum[:, c % 2, :], t1[:, c % 2, :], t2[:, c % 2, :], ALU.add).then_inc(S["add"], 1)

                    def scale(lag, c):
                        if not (v := behind(t, i, part, lag)):
                            return
                        tt, bt = v
                        g = g_of(bt) * 16 + (4 * tt + c)
                        half = c // 2
                        pool.wait_ge(S["rn"], g_of(bt) * 8 + (2 * tt + half + 1))
                        pool.wait_ge(S["add"], g + 2)
                        pool.wait_ge(S["tr"], g)
                        r = rn[:, tt % 2, half, 8 * (c % 2):8 * (c % 2) + 8].unsqueeze(2).to_broadcast([P, 8, D])
                        pt_(qn[:, c, :].rearrange("p (h d) -> p h d", h=8),
                            qsum[:, c % 2, :].rearrange("p (h d) -> p h d", h=8), r, ALU.mult).then_inc(S["qn"], 1)

                    def rests_of_p(lag, wp):
                        if not (v := behind(t, i, part, lag)):
                            return
                        tt, bt = v
                        pool.wait_ge(S["hi"], g_of(bt) * 8 + (2 * tt + wp + 1))
                        pt_(p2[:, wp, :, 1, :], pn[:, wp, :].rearrange("p (h k) -> p h k", h=HP),
                            p2[:, wp, :, 0, :].bitcast(F32), ALU.subtract).then_inc(S["lo"], 1)

                    for wp in range(2):
                        scale(1 - wp, 2 - 2 * wp)
                        scale(1 - wp, 3 - 2 * wp)
                        add(2 * wp)
                        add(2 * wp + 1)
                        rests_of_p(3 - wp, 1 - wp)

                pipeline(pool, step)


def kernel(L0_attn_x, L0_attn_Wq_down, L0_attn_Wk_down, L0_attn_Wv_down, L0_attn_Wq_up_c, L0_attn_Wq_up_e,
           L0_attn_Wk_up_c, L0_attn_Wk_up_e, L0_attn_Wv_up, L0_attn_Wc, L0_ffn_Wqkv, L0_ffn_q_scale,
           L0_ffn_k_scale, L0_ffn_Wo, L0_ffn_ln_g, L0_ffn_ln_b, L0_ffn_W1, L0_ffn_b1, L0_ffn_W2, L0_ffn_b2):
    import concourse.bacc as bacc
    from concourse.bass_utils import run_bass_kernel_spmd

    f32 = np.float32

    def turned(w):
        return np.asarray(w).T.reshape(HP, P, C).transpose(1, 0, 2)

    def two_heads(parts):
        n = sum(p.shape[1] for p in parts)
        o = np.zeros((P, 2, n), f32)
        o[0:LAT, 0], o[LAT:P, 1] = np.concatenate(parts, 1), np.concatenate(parts, 1)
        return o

    swap4, zero4 = [1, 0, 3, 2], np.zeros((LAT, 4), f32)
    qc, qe, kc, ke, vu = (np.asarray(a) for a in (L0_attn_Wq_up_c, L0_attn_Wq_up_e, L0_attn_Wk_up_c, L0_attn_Wk_up_e,
                                                  L0_attn_Wv_up))
    W, W1, W2 = np.asarray(L0_ffn_Wqkv), np.asarray(L0_ffn_W1), np.asarray(L0_ffn_W2)
    Wo = np.asarray(L0_ffn_Wo).reshape(DEPTH, HP, 2, D, C).transpose(0, 2, 3, 1, 4)
    WvT = W[:, :, 2 * INNER:].transpose(0, 2, 1).reshape(DEPTH, HP, P, C).transpose(0, 2, 1, 3)
    qs, ks = np.asarray(L0_ffn_q_scale), np.asarray(L0_ffn_k_scale)
    half = D // 2
    qks = np.stack([np.stack([s, np.concatenate([s[:, half:], s[:, :half]], 1)], 1) for s in (qs, ks)], 1)
    arrays = {
        "x": L0_attn_x, "wqdT": turned(L0_attn_Wq_down), "wkdT": turned(L0_attn_Wk_down), "wvdT": turned(L0_attn_Wv_down),
        "upq": two_heads([qc, qe, zero4, qe[:, swap4]]), "upk": two_heads([kc, ke, zero4, ke[:, swap4]]),
        "upv": two_heads([vu]), "Wc": L0_attn_Wc, "Wqkv": W, "WvT": WvT, "Wo": Wo, "qks": qks,
        "ln_g": np.asarray(L0_ffn_ln_g)[:, :, None], "ln_b": np.asarray(L0_ffn_ln_b)[:, :, None],
        "b2": np.asarray(L0_ffn_b2)[:, :, None], "W1": W1, "b1": np.asarray(L0_ffn_b1)[:, :, None], "W2": W2,
        **shape_constants(),
    }
    arrays = {k: np.ascontiguousarray(v) for k, v in arrays.items()}
    nc = bacc.Bacc("TRN2", target_bir_lowering=False, num_devices=1)
    ins = {k: nc.dram_tensor("in_" + k, v.shape, mybir.dt.from_np(v.dtype), kind="ExternalInput").ap()
           for k, v in arrays.items()}
    out = nc.dram_tensor("out", (B, T, C), F32, kind="ExternalOutput").ap()
    build(nc, ins, out)
    r = run_bass_kernel_spmd(nc, [{"in_" + k: v for k, v in arrays.items()}], core_ids=[0])
    return r.results[0]["out"]
```

```python
import math
from contextlib import ExitStack

import numpy as np

import concourse.bass as bass
from concourse import mybir

F32, F32R, BF16 = mybir.dt.float32, mybir.dt.float32r, mybir.dt.bfloat16
ACT = mybir.ActivationFunctionType
ALU = mybir.AluOpType
AX = mybir.AxisListType

P = 128
B, T, C = 8, 512, 128
TT = T // P
NTOK = B * T
HEADS, DA, LAT = 16, 8, 64
DEPTH, D, WIN = 6, 64, 32
HP = HEADS // 2
INNER = HEADS * D
FF = 341
FCH = [(0, 128), (128, 128), (256, FF - 256)]
MASKED = -1.0e30
AREA = 25856
OUT_PARTS = (((6, 3), (5, 1)), ((5, 2), (4, 0)))
LAG = 6


def shape_constants():
    f32 = np.float32
    half = np.arange(0, D, 2, dtype=f32)
    inv_freq = (f32(1.0) / np.power(f32(10000.0), half / f32(D))).astype(f32)
    t = np.arange(T, dtype=f32)
    freqs = (t[:, None] * inv_freq[None, :]).astype(f32)
    freqs = np.concatenate([freqs, freqs], -1)
    base = ((half + f32(0.4 * D)) / f32(1.4 * D)).astype(f32)
    power = ((t - T // 2) / (WIN // 2)).astype(f32)
    scale = (base[None, :] ** power[:, None]).astype(f32)
    scale = np.concatenate([scale, scale], -1)
    sign = np.where(np.arange(D) < D // 2, -1.0, 1.0).astype(f32)
    cos, sin = np.cos(freqs), np.sin(freqs) * sign
    rot = np.stack([np.stack([cos * scale * 8, sin * scale * 8], 1), np.stack([cos / scale, sin / scale], 1)], 1)
    rot = rot.reshape(TT, P, 2, 2, D).transpose(1, 0, 2, 3, 4).astype(f32)
    inv4 = (f32(1.0) / np.power(f32(10000.0), np.arange(0, 4, 2, dtype=f32) / f32(4))).astype(f32)
    fr = (t[:, None] * inv4[None, :]).astype(f32)
    fr = np.concatenate([fr, fr], -1)
    s4 = np.array([-1, 1, -1, 1], f32)
    ca = np.concatenate([np.ones((T, 4), f32), np.cos(fr)], -1)
    sa = np.concatenate([np.zeros((T, 4), f32), np.sin(fr) * s4], -1)
    ca, sa = np.tile(ca, (1, HEADS)).T, np.tile(sa, (1, HEADS)).T
    qs = f32(1.0 / math.sqrt(DA))
    crot = np.stack([ca * qs, sa * qs, ca, sa], 1).astype(f32)
    row, key = np.arange(P), np.arange(2 * WIN)
    q = row % WIN
    ok = (key[None] >= q[:, None]) & (key[None] <= q[:, None] + WIN)
    first = ok & ((row[:, None] >= 2 * WIN) | (key[None] >= WIN))
    lmask = np.stack([np.tile(np.where(m, 0.0, MASKED), (1, HP)) for m in (first, ok)], 1)
    tri = np.where(np.arange(P)[None] <= np.arange(P)[:, None], 0.0, MASKED)
    bf = mybir.dt.np(BF16)
    return {
        "c_rot": rot, "c_crot": crot, "c_lmask": lmask.astype(bf), "c_tri": tri.astype(bf),
        "c_id": np.eye(P, dtype=f32), "c_idb": np.eye(P, dtype=f32).astype(bf),
        "c_hm": (np.arange(P)[:, None] % 32 // DA == np.arange(4)[None]).astype(f32),
        "c_avg": np.full((P, P), 1.0 / C, f32),
    }


def build(nc, ins, out, layers=DEPTH):
    ctx = ExitStack()
    with ctx:
        def sb(name, shape, dt=F32):
            return ctx.enter_context(nc.sbuf_tensor("sb_" + name, [P] + shape, dt))

        def sem(name):
            return ctx.enter_context(nc.semaphore("s_" + name))

        scratch = nc.dram_tensor("x_plus_causal", [B, TT, P, C], F32, kind="Internal").ap()
        xd = ins["x"].rearrange("b (t p) c -> b p t c", p=P)
        scr = scratch.rearrange("b t p c -> b p t c")
        od = out.rearrange("b (t p) c -> b p t c", p=P)

        xT = sb("xT", [NTOK])
        ident = sb("ident", [P])
        identb = sb("identb", [P], BF16)
        lmask = sb("lmask", [2, HP * 2 * WIN], BF16)
        tri = sb("tri", [P], BF16)
        hm = sb("hm", [4])
        avg = sb("avg", [P])
        eps = sb("eps", [1])
        wqk_hi, wqk_lo = sb("wqk_hi", [2 * INNER], F32R), sb("wqk_lo", [2 * INNER], F32R)
        wo_bd = sb("wo_bd", [HP, 2, C])
        wvo = sb("wvo", [HEADS, C])
        w1_hi, w1_lo = sb("w1_hi", [2 * FF], F32R), sb("w1_lo", [2 * FF], F32R)
        w2 = sb("w2", [3, C])
        b1 = sb("b1", [6])
        lng = sb("lng", [3])
        rot = sb("rot", [TT, 2, 2, D])
        rots = sb("rots", [TT, 2, 2, D])
        qks = sb("qks", [2, 2, D])
        xs_hi, xs_lo = sb("xs_hi", [WIN + T], F32R), sb("xs_lo", [WIN + T], F32R)
        xwin = sb("xwin", [TT, 2, 4, P], F32R)
        p2 = sb("p2", [2, HP, 2, 2 * WIN], F32R)
        ptT = sb("ptT", [2, HP, P], F32R)
        ssq, lnb, rn = sb("ssq", [2, 2, 16]), sb("lnb", [2, 2, 16]), sb("rn", [2, 2, 16])
        smax, ssum, srec = sb("smax", [2, HP]), sb("ssum", [2, HP]), sb("srec", [2, HP])
        area = sb("area", [AREA])
        at = [0]

        def take(*shape):
            n = int(np.prod(shape))
            v = area[:, at[0]:at[0] + n]
            at[0] += n
            if len(shape) == 1:
                return v
            names = " ".join("abcde"[:len(shape)])
            return v.rearrange(f"p ({names}) -> p {names}", **dict(zip("abcde", shape)))

        ysb = take(2, 8, HEADS * WIN)
        sqb, t1, t2 = take(2, 512), take(2, 512), take(2, 512)
        qsum, qn = take(2, 512), take(4, 512)
        dd, pn = take(2, 512), take(2, 512)
        xdup = take(2, 4, 2, 2, WIN)
        qbd = take(2, HP, 4, 2, WIN)
        kT = take(HP, WIN + T)
        assert at[0] <= AREA
        at[0] = 0
        xn_all = take(NTOK)
        wqk_raw, wv_raw = take(2 * INNER), take(HP, C)
        w1 = take(2 * FF)
        at_ln = at[0]
        lx, ld, lrs = take(4, 512), take(4, 512), take(4, 512)
        at[0] = at_ln
        gg = take(2, 3, 512)
        uu = take(2, 3, 512)
        assert at[0] <= AREA - 4096 - HP * (WIN + T)
        at[0] = 0
        v16 = take(TT, HEADS * (P + DA))
        ptA = take(2, TT, T)
        ea = take(2, TT, T)
        crot = take(4, T)
        ra, rb_ = take(T), take(T)
        yT = take(T)
        xb = take(T)
        wcomb = take(5, P)
        upq, upk, upv = take(2, 16), take(2, 16), take(2, 8)
        wc = take(C)
        xres = take(2, TT, C)
        assert at[0] <= AREA
        wd = area[:, 8704 + 512:8704 + 512 + 3 * 1024].rearrange("p (a b c) -> p a b c", a=3, b=HP)
        xtok = area[:, 0:NTOK].rearrange("p (n c) -> p n c", c=C)
        xsq = area[:, NTOK:2 * NTOK].rearrange("p (n c) -> p n c", c=C)
        nmx, lse, lre = sb("nmx", [8]), sb("lse", [8]), sb("lre", [8])
        lnm, lnv = sb("lnm", [NTOK // P]), sb("lnv", [NTOK // P])
        mlp = p2[:, :, :, :, :].rearrange("p a b c d -> p (a b c d)").rearrange("p (s e t) -> p s e t", s=2, e=2)
        mlp_hi, mlp_lo = mlp[:, 0], mlp[:, 1]
        split_qk = mlp
        stacks = xwin[:, :, :, :, :].rearrange("p a b c d -> p (a b c d)").rearrange("p (s g t) -> p s g t", s=2, g=4)
        qm = ptT[:, :, 0:4, :]
        spare = sb("spare", [32])

        ps = [ctx.enter_context(nc.psum_tensor(f"bank{i}", [P, 512], F32)) for i in range(8)]
        pj, rbank, sbank, tbank, ybank, mbank = ps[0:2], ps[2], ps[3], ps[4], ps[5:7], ps[7]

        S = {n: sem(n) for n in (
            "const", "xload", "c_weights", "eps_set", "v16_zero", "wo_zero", "w_loaded", "w_loaded2",
            "upd", "wcomb_mm", "wcomb_ready",
            "ln0", "ln0a", "xn_tr", "xT_ready", "area_free",
            "xb_ready", "c_proj", "c_rope", "c_rope_part", "v_mm", "v_ready", "qm_ready", "c_score", "c_max",
            "c_exp", "c_split", "stack0", "stack1", "stack2", "stack3", "c_rec", "c_p", "c_tr", "c_ptev", "c_pv", "yT_ready", "ca_mm", "res_in", "ca_sum", "ca_out",
            "kT_zero", "w_split", "w_split_h", "w_split_a", "rots_ready", "rots_part", "wvo_mm", "wvo_ready", "xs_part", "xs_ready",
            "proj", "sq", "rotd", "rot_part", "ssq", "ssq_raw", "ln_part", "rn", "add", "qn", "tr", "ev", "score",
            "smax", "sub", "exp", "ssum", "srec", "pn", "hi", "lo", "pt", "ptev", "yy", "yev0", "yev1",
            "xdup", "xwt", "xwev", "oo", "xupd",
            "lx", "lx_zero", "lmean", "ldif", "lsq", "lvar", "lln", "lrs", "lmul", "xn", "mhi", "mlo", "gate", "gelu", "aa",
            "uu", "down", "mx",
            "f_in", "f_tr", "f_sum", "f_out",
        )}
        block = ctx.enter_context(nc.Block())

        def pipeline(eng, step):
            for t in range(LAG):
                step(t, 0, 0)
            with eng.Fori(0, B - 2) as i:
                for t in range(LAG, LAG + TT):
                    step(t, i, 1)
            for t in range(LAG, LAG + 2 * TT):
                step(t, B - 2, 2)

        def behind(t, i, part, lag):
            s = t - lag
            if (part == 0 and s < 0) or (part == 2 and s >= 2 * TT):
                return None
            return s % TT, i + s // TT

        SLOTS, DRAIN = HEADS * TT, 16

        def causal(eng, slot):
            for n in range(SLOTS):
                slot(n, 0, 0)
            with eng.Fori(1, B - 1) as b:
                for n in range(SLOTS):
                    slot(n, b, 1)
            for n in range(SLOTS + DRAIN):
                slot(n, B - 1, 2)

        def earlier(n, part, lag):
            k = n - lag
            if part == 2:
                return k % SLOTS if k < SLOTS else None
            return None if part == 0 and k < 0 else k % SLOTS

        def need(eng, name, v):
            if not isinstance(v, int) or v > 0:
                eng.wait_ge(S[name], v)

        @block.sync
        def _(sp):
            sp.dma_start(xtok, ins["x"].rearrange("b (t p) c -> p (b t) c", p=P)).then_inc(S["xload"], 16)
            for dst, name in ((ident, "c_id"), (identb, "c_idb"), (tri, "c_tri"), (hm, "c_hm"), (avg, "c_avg")):
                sp.dma_start(dst[:, :], ins[name]).then_inc(S["const"], 16)
            sp.dma_start(lmask[:, :, :], ins["c_lmask"]).then_inc(S["const"], 16)
            sp.dma_start(rot[:, :, :, :], ins["c_rot"]).then_inc(S["const"], 16)
            sp.wait_ge(S["xT_ready"], B)
            sp.dma_start(crot, ins["c_crot"]).then_inc(S["c_weights"], 16)
            for i, name in enumerate(("wqdT", "wkdT", "wvdT")):
                sp.dma_start(wd[:, i, :, :], ins[name]).then_inc(S["c_weights"], 16)
            for dst, name in ((upq, "upq"), (upk, "upk"), (upv, "upv")):
                sp.dma_start(dst, ins[name]).then_inc(S["c_weights"], 16)
            sp.dma_start(wc, ins["Wc"]).then_inc(S["c_weights"], 16)
            def stack(a, hg):
                need(sp, "c_score", (a - 1) * SLOTS + 16 * (hg + 1))
                for side in range(2):
                    for term in range(4):
                        part = (term // 2, term % 2)[side]
                        sp.dma_start(stacks[32 * term:32 * term + 32, side, hg, :].bitcast(F32),
                                     split_qk[32 * hg:32 * hg + 32, side, part, :].bitcast(F32)).then_inc(S[f"stack{hg}"], 16)

            for b in range(B):
                if b == 0:
                    sp.wait_ge(S["c_split"], 4)
                    for hg in range(4):
                        stack(0, hg)
                else:
                    sp.wait_ge(S["ca_sum"], b)
                    sp.dma_start(scr[b - 1], xres[:, 1, :, :]).then_inc(S["ca_out"], 16)
                    sp.wait_ge(S["ca_out"], b * 16)
                sp.dma_start(xres[:, 0, :, :], xd[b]).then_inc(S["res_in"], 16)
                if b < B - 1:
                    sp.wait_ge(S["c_split"], 4 * (b + 2))
                    for hg in range(4):
                        stack(b + 1, hg)
            sp.wait_ge(S["ca_sum"], B)
            sp.dma_start(scr[B - 1], xres[:, 1, :, :]).then_inc(S["ca_out"], 16)
            sp.wait_ge(S["ca_out"], B * 16)

            for l in range(layers):
                sp.wait_ge(S["area_free"], 1)
                sp.wait_ge(S["wo_zero"], 1)
                sp.wait_ge(S["xupd"], l * (2 * B))
                sp.wait_ge(S["w_split"], l * 8)
                sp.wait_ge(S["wvo_mm"], l * 4)
                sp.dma_start(wqk_raw, ins["Wqkv"][l][:, 0:2 * INNER]).then_inc(S["w_loaded"], 16)
                sp.dma_start(wv_raw, ins["WvT"][l]).then_inc(S["w_loaded"], 16)
                sp.dma_start(wo_bd[0:64, :, 0, :], ins["Wo"][l][0]).then_inc(S["w_loaded"], 16)
                sp.dma_start(wo_bd[64:128, :, 1, :], ins["Wo"][l][1]).then_inc(S["w_loaded"], 16)
                sp.dma_start(qks[:, :, :, :], ins["qks"][l].unsqueeze(0).to_broadcast([P, 2, 2, D])).then_inc(S["w_loaded"], 16)
                sp.wait_ge(S["mx"], l * B)
                sp.wait_ge(S["xupd"], (l + 1) * (2 * B))
                sp.dma_start(w1, ins["W1"][l]).then_inc(S["w_loaded2"], 16)
                for j, (f0, fn) in enumerate(FCH):
                    sp.dma_start(w2[0:fn, j, :], ins["W2"][l][f0:f0 + fn, :]).then_inc(S["w_loaded2"], 16)
                    sp.dma_start(b1[0:fn, j:j + 1], ins["b1"][l][f0:f0 + fn, :]).then_inc(S["w_loaded2"], 16)
                    sp.dma_start(b1[0:fn, 3 + j:4 + j], ins["b1"][l][FF + f0:FF + f0 + fn, :]).then_inc(S["w_loaded2"], 16)
                for j, name in enumerate(("ln_g", "ln_b", "b2")):
                    sp.dma_start(lng[:, j:j + 1], ins[name][l]).then_inc(S["w_loaded2"], 16)

            sp.wait_ge(S["mx"], layers * B)
            for b in range(B):
                sp.wait_ge(S["f_sum"], b)
                sp.wait_ge(S["f_out"], b * 16)
                sp.dma_start(xres[:, 0, :, :], scr[b]).then_inc(S["f_in"], 16)
                sp.wait_ge(S["f_sum"], b + 1)
                sp.dma_start(od[b], xres[:, 1, :, :]).then_inc(S["f_out"], 16)
            sp.wait_ge(S["f_out"], B * 16)

        @block.tensor
        def _(pe):
            def mm(o, a, b, start=True, stop=True):
                return nc.tensor.matmul(o, a, b, start=start, stop=stop, skip_group_check=True)

            def split3(o, a_hi, a_lo, b_hi, b_lo):
                mm(o, a_hi, b_hi, True, False)
                mm(o, a_hi, b_lo, False, False)
                return mm(o, a_lo, b_hi, False, True)

            pe.wait_ge(S["const"], 7 * 16)
            pe.wait_ge(S["ln0"], 5)
            for b in range(B):
                if b >= 4:
                    pe.wait_ge(S["xT_ready"], b - 3)
                for t in range(TT):
                    m = nc.tensor.transpose(ps[b % 4][:, t * P:(t + 1) * P], xtok[:, b * TT + t, :], ident[:, :])
                m.then_inc(S["xn_tr"], 1)
            pe.wait_ge(S["c_weights"], 8 * 16)
            for i, (up, n) in enumerate(((upq, 16), (upk, 16), (upv, 8))):
                for hp in range(HP):
                    m = mm(ps[4 + i][:, hp * 2 * n:(hp + 1) * 2 * n], wd[:, i, hp, :],
                           up.rearrange("p a b -> p (a b)"))
                m.then_inc(S["wcomb_mm"], 1)
            pe.wait_ge(S["wcomb_ready"], 5)

            def project_causal(a, i):
                if i == 0:
                    need(pe, "xb_ready", a + 1)
                    need(pe, "v_ready", a)
                    need(pe, "ca_sum", a - 1)
                elif i % 2 == 0:
                    pe.wait_ge(S["c_rope_part"], a * 4 + i)
                if i < 4:
                    mm(ps[(5, 7)[i % 2]][:, :], wcomb[:, i, :], xb).then_inc(S["c_proj"], 1)
                else:
                    for t in range(TT):
                        m = mm(ps[5][:, t * P:(t + 1) * P], xb[:, t * P:(t + 1) * P], wcomb[:, 4, :])
                    m.then_inc(S["v_mm"], 1)

            for i in range(5):
                project_causal(0, i)

            def causal_slot(n, b, part):
                g = b * SLOTS + n
                if (k := earlier(n, part, 0)) is not None:
                    h, qt = k // TT, k % TT
                    if qt == 0:
                        pe.wait_ge(S["qm_ready"], b * HEADS + h + 1)
                    need(pe, "c_exp", g - 2 if k >= 3 else b * SLOTS)
                    o = ps[k % 3]
                    mm(o[:, 0:(qt + 1) * P], qm[:, h % 2, qt, :], stacks[:, 1, h // 4, 0:(qt + 1) * P], True, False)
                    mm(o[:, qt * P:(qt + 1) * P], identb[:, :], tri[:, :], False, True).then_inc(S["c_score"], 1)
                if (k := earlier(n, part, 7)) is not None:
                    pe.wait_ge(S["c_p"], g - 6)
                    need(pe, "c_ptev", g - 8)
                    for kt in range(k % TT + 1):
                        m = nc.tensor.transpose(ps[(3, 6)[k % 2]][:, kt * P:(kt + 1) * P],
                                                ea[:, k // TT % 2, k % TT, kt * P:(kt + 1) * P], ident[:, :])
                    m.then_inc(S["c_tr"], 1)
                if (k := earlier(n, part, 12)) is not None:
                    h, kt = k // TT, k % TT
                    if kt == 0:
                        pe.wait_ge(S["c_ptev"], g - 8)
                    if k == 0:
                        pe.wait_ge(S["v_ready"], b + 1)
                        need(pe, "yT_ready", b)
                    m = mm(ps[4][:, kt * P:T], v16[:, kt, h * P:(h + 1) * P], ptA[:, h % 2, kt, kt * P:T],
                           k == 0, k == SLOTS - 1)
                    if kt == TT - 1:
                        m.then_inc(S["c_pv"], 1)
                if (n == 14 and part) or n == SLOTS + 14:
                    after = b if n < SLOTS else b + 1
                    pe.wait_ge(S["yT_ready"], after)
                    for t in range(TT):
                        m = mm(ps[7][:, t * P:(t + 1) * P], yT[:, t * P:(t + 1) * P], wc)
                    m.then_inc(S["ca_mm"], 1)
                if part < 2 and n in (20, 22, 30, 32, 40):
                    project_causal(b + 1, (20, 22, 30, 32, 40).index(n))

            causal(pe, causal_slot)

            with pe.Fori(0, layers) as l:
                pe.wait_ge(S["mx"], l * B)

                def step(t, i, part):
                    def g_of(bt):
                        return l * B + bt

                    def join_weights():
                        if part or t >= 4:
                            return
                        if t == 0:
                            pe.wait_ge(S["wo_zero"], 1)
                        pe.wait_ge(S["w_loaded"], (l + 1) * (5 * 16))
                        pe.wait_ge(S["wvo_ready"], 4 * l + t)
                        for j in range(2):
                            hp = 2 * t + j
                            m = mm(mbank[:, j * 256:(j + 1) * 256], wv_raw[:, hp, :],
                                   wo_bd[:, hp, :, :].rearrange("p a b -> p (a b)"))
                        m.then_inc(S["wvo_mm"], 1)

                    def project(c):
                        if not (v := behind(t, i, part, 0)):
                            return
                        tt, bt = v
                        if c == 0:
                            pe.wait_ge(S["xs_ready"], g_of(bt) * 4 + tt + 1)
                        if part == 0 and t == 0:
                            pe.wait_ge(S["w_split"], 8 * l + 2 * c + 2)
                        g = g_of(bt) * 16 + (4 * tt + c)
                        pe.wait_ge(S["sq"], g)
                        pe.wait_ge(S["rotd"], g)
                        s = slice(WIN + tt * P, WIN + (tt + 1) * P)
                        w = slice(c * 512, (c + 1) * 512)
                        split3(pj[c % 2][:, :], xs_hi[:, s], xs_lo[:, s], wqk_hi[:, w], wqk_lo[:, w])\
                            .then_inc(S["proj"], 1)

                    def turn_qk(c):
                        if not (v := behind(t, i, part, 1)):
                            return
                        tt, bt = v
                        g = g_of(bt) * 16 + (4 * tt + c)
                        pe.wait_ge(S["qn"], g + 7)
                        if c % 2:
                            pe.wait_ge(S["xwev"], (g_of(bt) * 4 + tt) * 2 + c // 2 + 1)
                        else:
                            pe.wait_ge(S["ev"], g)
                        for j in range(4):
                            m = nc.tensor.transpose(rbank[:, j * P:(j + 1) * P], qn[:, c, j * P:(j + 1) * P],
                                                    ident[:, :])
                        m.then_inc(S["tr"], 1)

                    def score(wp):
                        if not (v := behind(t, i, part, 2)):
                            return
                        tt, bt = v
                        pe.wait_ge(S["ev"], g_of(bt) * 16 + 4 * tt + 4)
                        pe.wait_ge(S["sub"], g_of(bt) * 8 + 2 * tt + wp)
                        first = tt == 0 and wp == 0
                        mm(sbank[:, :], identb[:, :], lmask[:, 0 if first else 1, :], True, False)
                        for w2_ in range(2):
                            for hp in range(HP):
                                w = 2 * wp + w2_
                                k0 = tt * P + w * WIN
                                m = mm(sbank[64 * w2_:64 * w2_ + 64, hp * 64:(hp + 1) * 64],
                                       qbd[:, tt % 2, hp, w, :, :].rearrange("p a b -> p (a b)"),
                                       kT[:, hp, k0:k0 + 2 * WIN], False, w2_ == 1 and hp == HP - 1)
                        m.then_inc(S["score"], 1)

                    def turn_p(wp, half):
                        if not (v := behind(t, i, part, 3)):
                            return
                        tt, bt = v
                        m_ = g_of(bt) * 8 + 2 * tt + wp
                        pe.wait_ge(S["lo"], m_ + 2)
                        pe.wait_ge(S["ptev"], m_ * 2 + half)
                        for j in range(4):
                            m = nc.tensor.transpose(
                                tbank[:, j * P:(j + 1) * P],
                                p2[:, wp, 4 * half + j, :, :].rearrange("p a b -> p (a b)").bitcast(F32), ident[:, :])
                        m.then_inc(S["pt"], 1)

                    def weigh(lag, wp):
                        if not (v := behind(t, i, part, lag)):
                            return
                        tt, bt = v
                        m_ = g_of(bt) * 8 + 2 * tt + wp
                        pe.wait_ge(S["ptev"], m_ * 2 + 2)
                        pe.wait_ge(S["xwev"], (g_of(bt) * 4 + tt) * 2 + 2)
                        for w2_, free in ((0, "yev0"), (1, "yev1")):
                            pe.wait_ge(S[free], m_)
                            w = 2 * wp + w2_
                            rhs = ptT[:, wp, :, 64 * w2_:64 * w2_ + 64]
                            mm(ybank[w2_][:, :], xwin[:, tt, 0, w, :], rhs, True, False)
                            mm(ybank[w2_][:, :], xwin[:, tt, 1, w, :], rhs, False, True).then_inc(S["yy"], 1)

                    def windows(hl):
                        if not (v := behind(t, i, part, 1)):
                            return
                        tt, bt = v
                        g = g_of(bt) * 4 + tt
                        pe.wait_ge(S["xdup"], g * 2 + hl + 1)
                        pe.wait_ge(S["ev"], g * 4 + 2 * hl + 1)
                        for w in range(4):
                            m = nc.tensor.transpose(rbank[:, w * P:(w + 1) * P],
                                                    xdup[:, hl, w, :, :, :].rearrange("p a b c -> p (a b c)"), ident[:, :])
                        m.then_inc(S["xwt"], 1)

                    def project_out(wp):
                        for lag, k in OUT_PARTS[wp]:
                            v = behind(t, i, part, lag)
                            if not v or v[0] % 2 == 0:
                                continue
                            tt, bt = v
                            hf = tt // 2
                            if k == 0:
                                pe.wait_ge(S["yev0"], g_of(bt) * 8 + 2 * tt + 2)
                                pe.wait_ge(S["yev1"], g_of(bt) * 8 + 2 * tt + 2)
                                pe.wait_ge(S["xupd"], g_of(bt) * 2 + hf)
                            for h in range(4 * k, 4 * k + 4):
                                m = mm(mbank[:, 0:256], wvo[:, h, :], ysb[:, hf, :, h * WIN:(h + 1) * WIN],
                                       h == 0, h == HEADS - 1)
                            if k == 3:
                                m.then_inc(S["oo"], 1)

                    for wp in range(2):
                        project(2 * wp)
                        turn_qk(2 * wp)
                        turn_p(wp, 0)
                        project(2 * wp + 1)
                        score(wp)
                        windows(wp)
                        turn_p(wp, 1)
                        weigh(4 - wp, 1 - wp)
                        turn_qk(2 * wp + 1)
                        project_out(wp)
                    join_weights()

                pipeline(pe, step)

                with pe.Fori(0, 2) as j:
                    for e in range(4):
                        n = l * B + 4 * j + e
                        pe.wait_ge(S["lx"], n + 1)
                        if e == 0:
                            pe.wait_ge(S["ldif"], l * B + 4 * j)
                        mm(ps[e][:, :], avg[:, :], lx[:, e, :]).then_inc(S["lmean"], 1)
                    for e in range(4):
                        n = l * B + 4 * j + e
                        pe.wait_ge(S["lsq"], n + 1)
                        if e == 0:
                            pe.wait_ge(S["lln"], l * B + 4 * j)
                        mm(ps[4 + e][:, :], avg[:, :], lx[:, e, :]).then_inc(S["lvar"], 1)

                def down(n, e):
                    pe.wait_ge(S["uu"], n * 3 + 3)
                    pe.wait_ge(S["mx"], n - 1 if e else n)
                    for c, (f0, fn) in enumerate(FCH):
                        m = mm(ps[6 + e][:, :], w2[0:fn, c, :], uu[0:fn, e, c, :], c == 0, c == 2)
                    m.then_inc(S["down"], 1)

                def mlp_pair(n0, first):
                    for e in range(2):
                        n = n0 + e
                        pe.wait_ge(S["mlo"], n + 1)
                        pe.wait_ge(S["gelu"], n * 3)
                        for c, (f0, fn) in enumerate(FCH):
                            f = slice(FF + f0, FF + f0 + fn)
                            split3(ps[c][0:fn, :], w1_hi[:, f], w1_lo[:, f], mlp_hi[:, e, :], mlp_lo[:, e, :])\
                                .then_inc(S["gate"], 1)
                        if e or not first:
                            down(n - 1, 1 - e)
                        pe.wait_ge(S["uu"], n * 3)
                        for c, (f0, fn) in enumerate(FCH):
                            f = slice(f0, f0 + fn)
                            split3(ps[3 + c][0:fn, :], w1_hi[:, f], w1_lo[:, f], mlp_hi[:, e, :], mlp_lo[:, e, :])\
                                .then_inc(S["aa"], 1)

                pe.wait_ge(S["lln"], (l + 1) * B)
                pe.wait_ge(S["w_split_a"], 2 * l + 2)
                mlp_pair(l * B, True)
                with pe.Fori(1, B // 2) as j:
                    mlp_pair(l * B + 2 * j, False)
                down(l * B + (B - 1), 1)

            pe.wait_ge(S["mx"], layers * B)
            with pe.Fori(0, B) as b:
                pe.wait_ge(S["xb_ready"], b + (B + 1))
                pe.wait_ge(S["f_sum"], b)
                for t in range(TT):
                    m = nc.tensor.transpose(ps[0][:, t * P:(t + 1) * P], xb[:, t * P:(t + 1) * P], ident[:, :])
                m.then_inc(S["f_tr"], 1)

        @block.scalar
        def _(act):
            def copy(o, i):
                return nc.scalar.activation(o, i, ACT.Copy)

            nc.scalar.preload_act_table_set("natural_log_exp_and_others")
            act.wait_ge(S["ln0"], 3)
            nc.scalar.activation(xsq, xtok, ACT.Square).then_inc(S["ln0a"], 1)
            act.wait_ge(S["ln0"], 4)
            act.wait_ge(S["eps_set"], 1)
            nc.scalar.activation(lnm[:, :], lnv[:, :], ACT.Ln, bias=eps[:, :], scale=1.0 / C).then_inc(S["ln0a"], 1)
            act.wait_ge(S["ln0a"], 2)
            nc.scalar.activation(lnv[:, :], lnm[:, :], ACT.Exp, scale=-0.5).then_inc(S["ln0a"], 1)
            for b in range(B):
                act.wait_ge(S["xn_tr"], b + 1)
                copy(xT[:, b * T:(b + 1) * T], ps[b % 4][:, :]).then_inc(S["xT_ready"], 1)
            for i in range(2):
                act.wait_ge(S["wcomb_mm"], i + 1)
                src = ps[4 + i][:, 0:256].rearrange("p (h s d) -> p h s d", h=HEADS, s=2)
                for s in range(2):
                    copy(wcomb[:, 2 * i + s, :].rearrange("p (h d) -> p h d", h=HEADS), src[:, :, s, :])\
                        .then_inc(S["wcomb_ready"], 1)
            act.wait_ge(S["wcomb_mm"], 3)
            copy(wcomb[:, 4, :], ps[6][:, 0:128]).then_inc(S["wcomb_ready"], 1)

            def mask_q(b, h):
                act.wait_ge(S[f"stack{h // 4}"], (b + 1) * (8 * 16))
                need(act, "c_score", b * SLOTS + TT * (h - 1))
                nc.scalar.activation(qm[:, h % 2, :, :], stacks[:, 0, h // 4, :].bitcast(F32).rearrange("p (a b) -> p a b", a=4), ACT.Copy,
                                     scale=hm[:, h % 4:h % 4 + 1]).then_inc(S["qm_ready"], 1)

            act.wait_ge(S["const"], 7 * 16)
            mask_q(0, 0)

            def causal_slot(n, b, part):
                g = b * SLOTS + n
                if (k := earlier(n, part, 8)) is not None:
                    h, qt = k // TT, k % TT
                    if qt == 0:
                        need(act, "c_pv", b * HEADS + (n - 8) // TT - 1)
                    act.wait_ge(S["c_tr"], g - 7)
                    copy(ptA[:, h % 2, 0:qt + 1, qt * P:(qt + 1) * P],
                         ps[(3, 6)[k % 2]][:, 0:(qt + 1) * P].rearrange("p (k q) -> p k q", q=P))\
                        .then_inc(S["c_ptev"], 1)
                if (k := earlier(n, part, 0)) is not None:
                    qt = k % TT
                    act.wait_ge(S["c_max"], g + 1)
                    need(act, "c_tr", g - 7)
                    nc.scalar.activation(ea[:, k // TT % 2, qt, 0:(qt + 1) * P], ps[k % 3][:, 0:(qt + 1) * P], ACT.Exp,
                                         bias=nmx[:, k % 8:k % 8 + 1], accum_out=lse[:, k % 8:k % 8 + 1])\
                        .then_inc(S["c_exp"], 1)
                    if qt == 0:
                        if k < SLOTS - TT:
                            mask_q(b, k // TT + 1)
                        elif part < 2:
                            mask_q(b + 1, 0)
                if (n == 11 and part) or n == SLOTS + 11:
                    after = b if n < SLOTS else b + 1
                    act.wait_ge(S["c_pv"], after * HEADS)
                    need(act, "ca_mm", after - 1)
                    copy(yT, ps[4][:, :]).then_inc(S["yT_ready"], 1)
                if n == 11:
                    act.wait_ge(S["v_mm"], b + 1)
                    act.wait_ge(S["v16_zero"], 1)
                    copy(v16.rearrange("p k (h x) -> p k h x", x=P + DA)[:, :, :, 0:DA],
                         ps[5][:, :].rearrange("p (k h d) -> p k h d", k=TT, h=HEADS)).then_inc(S["v_ready"], 1)

            causal(act, causal_slot)

            with act.Fori(0, layers) as l:
                nc.scalar.preload_act_table_set("natural_log_exp_and_others")
                act.wait_ge(S["w_loaded"], (l + 1) * (5 * 16))
                act.wait_ge(S["xupd"], l * (2 * B))
                for c in range(4):
                    w = slice(c * 512, (c + 1) * 512)
                    copy(wqk_hi[:, w], wqk_raw[:, w]).then_inc(S["w_split_h"], 1)

                def step(t, i, part):
                    def g_of(bt):
                        return l * B + bt

                    def joined_weights():
                        if part or t >= 4:
                            return
                        act.wait_ge(S["wvo_mm"], 4 * l + t + 1)
                        copy(wvo[:, 4 * t:4 * t + 4, :], mbank[:, :].rearrange("p (a b) -> p a b", a=4))\
                            .then_inc(S["wvo_ready"], 1)

                    def square(c):
                        if not (v := behind(t, i, part, 0)):
                            return
                        tt, bt = v
                        g = g_of(bt) * 16 + (4 * tt + c)
                        act.wait_ge(S["proj"], g + 1)
                        act.wait_ge(S["ssq_raw"], g)
                        nc.scalar.activation(sqb[:, c % 2, :], pj[c % 2][:, :], ACT.Square).then_inc(S["sq"], 1)

                    def norms(half):
                        if not (v := behind(t, i, part, 0)):
                            return
                        tt, bt = v
                        n = (g_of(bt) * 4 + tt) * 2 + half
                        act.wait_ge(S["ssq"], n + 1)
                        nc.scalar.activation(lnb[:, tt % 2, half, :], ssq[:, tt % 2, half, :], ACT.Ln)\
                            .then_inc(S["ln_part"], 1)
                        act.wait_ge(S["ln_part"], n + 4)
                        act.wait_ge(S["qn"], (g_of(bt) * 16 + 4 * tt + 2 * half))
                        nc.scalar.activation(rn[:, tt % 2, half, :], lnb[:, tt % 2, half, :], ACT.Exp, scale=-0.5)\
                            .then_inc(S["rn"], 1)

                    def turned_qk(c):
                        if not (v := behind(t, i, part, 1)):
                            return
                        tt, bt = v
                        act.wait_ge(S["tr"], g_of(bt) * 16 + (4 * tt + c) + 4)
                        if c == 0:
                            act.wait_ge(S["score"], (g_of(bt) * 4 + tt) * 2)
                        src = rbank[:, :].rearrange("p (j w q) -> p j w q", j=4, w=4)
                        if c < 2:
                            for h2 in range(2):
                                r = slice(64 * h2, 64 * h2 + 64)
                                m = copy(qbd[r, tt % 2, 4 * c:4 * c + 4, :, h2, :], src[r])
                        else:
                            m = copy(kT[:, 4 * (c - 2):4 * (c - 2) + 4, WIN + tt * P:WIN + (tt + 1) * P],
                                     rbank[:, :].rearrange("p (j q) -> p j q", j=4))
                        m.then_inc(S["ev"], 1)

                    def exp(wp):
                        if not (v := behind(t, i, part, 2)):
                            return
                        tt, bt = v
                        act.wait_ge(S["sub"], g_of(bt) * 8 + 2 * tt + wp + 1)
                        nc.scalar.activation(dd[:, wp, :], dd[:, wp, :], ACT.Exp).then_inc(S["exp"], 1)

                    def heads_of_p(lag, wp):
                        if not (v := behind(t, i, part, lag)):
                            return
                        tt, bt = v
                        m_ = g_of(bt) * 8 + 2 * tt + wp
                        act.wait_ge(S["pn"], m_ + 2)
                        act.wait_ge(S["pt"], m_ * 2)
                        copy(p2[:, wp, :, 0, :], pn[:, wp, :].rearrange("p (h k) -> p h k", h=HP)).then_inc(S["hi"], 1)

                    def turned_p(wp, half):
                        if not (v := behind(t, i, part, 3)):
                            return
                        tt, bt = v
                        m_ = g_of(bt) * 8 + 2 * tt + wp
                        act.wait_ge(S["pt"], m_ * 2 + half + 3)
                        act.wait_ge(S["yy"], m_ * 2)
                        copy(ptT[:, wp, 4 * half:4 * half + 4, :],
                             tbank[:, :].rearrange("p (j q) -> p j q", j=4)).then_inc(S["ptev"], 1)

                    def weighed(lag, wp):
                        if not (v := behind(t, i, part, lag)):
                            return
                        tt, bt = v
                        m_ = g_of(bt) * 8 + 2 * tt + wp
                        act.wait_ge(S["yy"], m_ * 2 + 3)
                        act.wait_ge(S["oo"], g_of(bt) * 2 + tt // 2)
                        copy(ysb[:, tt // 2, 4 * (tt % 2) + 2 * wp, :], ybank[0][:, :]).then_inc(S["yev0"], 1)
                        act.wait_ge(S["yy"], m_ * 2 + 4)
                        copy(ysb[:, tt // 2, 4 * (tt % 2) + 2 * wp + 1, :], ybank[1][:, :]).then_inc(S["yev1"], 1)

                    def windows(hl):
                        if not (v := behind(t, i, part, 1)):
                            return
                        tt, bt = v
                        g = g_of(bt) * 4 + tt
                        act.wait_ge(S["xwt"], g * 2 + hl + 2)
                        if hl == 0 and not (part == 0 and t - 1 < TT):
                            act.wait_ge(S["yy"], g * 4 - 10)
                        copy(xwin[:, tt, hl, :, :], rbank[:, :].rearrange("p (w c) -> p w c", w=4))\
                            .then_inc(S["xwev"], 1)

                    for wp in range(2):
                        square(2 * wp)
                        turned_qk(2 * wp)
                        turned_p(wp, 0)
                        square(2 * wp + 1)
                        windows(wp)
                        turned_p(wp, 1)
                        heads_of_p(3 - wp, 1 - wp)
                        weighed(4 - wp, 1 - wp)
                        turned_qk(2 * wp + 1)
                        exp(wp)
                        norms(wp)
                    joined_weights()

                pipeline(act, step)

                with act.Fori(0, 2) as j:
                    for e in range(4):
                        n = l * B + 4 * j + e
                        act.wait_ge(S["ldif"], n + 1)
                        nc.scalar.activation(lx[:, e, :], ld[:, e, :], ACT.Square).then_inc(S["lsq"], 1)
                    for e in range(4):
                        n = l * B + 4 * j + e
                        act.wait_ge(S["lvar"], n + 1)
                        act.wait_ge(S["xn"], l * B + 4 * j)
                        nc.scalar.activation(lrs[:, e, :], ps[4 + e][:, :], ACT.Ln, bias=eps[:, :])\
                            .then_inc(S["lln"], 1)
                        act.wait_ge(S["lln"], n + 1)
                        nc.scalar.activation(lrs[:, e, :], lrs[:, e, :], ACT.Exp, scale=-0.5).then_inc(S["lrs"], 1)
                act.wait_ge(S["w_loaded2"], (l + 1) * (13 * 16))
                act.wait_ge(S["mx"], l * B)
                copy(w1_hi[:, :], w1).then_inc(S["w_split_a"], 1)
                act.wait_ge(S["xn"], (l + 1) * B)
                with act.Fori(0, B // 2) as j:
                    for e in range(2):
                        n = l * B + 2 * j + e
                        for c, (f0, fn) in enumerate(FCH):
                            act.wait_ge(S["gate"], n * 3 + c + 1)
                            if c == 0:
                                act.wait_ge(S["uu"], (l * B + 2 * j) * 3)
                            nc.scalar.activation(gg[0:fn, e, c, :], ps[c][0:fn, :], ACT.Gelu,
                                                 bias=b1[0:fn, 3 + c:4 + c]).then_inc(S["gelu"], 1)

        @block.vector
        def _(dve):
            tt_, ts_ = nc.vector.tensor_tensor, nc.vector.tensor_scalar

            def bc(v, shape, axis):
                return v.unsqueeze(axis).to_broadcast(shape)

            nc.vector.memset(eps[:, :], 1e-5).then_inc(S["eps_set"], 1)
            column = iter(range(32))
            for name, n in (("sq", 1), ("rotd", 1), ("ssq_raw", 1), ("add", 1), ("tr", 3), ("xwt", 1), ("score", 2), ("yy", 2),
                            ("pt", 2), ("qn", 6), ("ln_part", 3), ("lo", 1), ("pn", 1), ("oo", 1)):
                for _ in range(n):
                    c = next(column)
                    nc.vector.memset(spare[:, c:c + 1], 0.0).then_inc(S[name], 1)

            nc.vector.memset(wo_bd[:, :, :, :], 0.0).then_inc(S["wo_zero"], 1)
            dve.wait_ge(S["xload"], 16)
            n = NTOK // P
            nc.vector.tensor_reduce(lnm[:, :], xtok, AX.X, ALU.add).then_inc(S["ln0"], 1)
            dve.wait_ge(S["ln0"], 1)
            ts_(lnv[:, :], lnm[:, :], 1.0 / C, None, ALU.mult).then_inc(S["ln0"], 1)
            dve.wait_ge(S["ln0"], 2)
            tt_(xtok, xtok, bc(lnv[:, :], [P, n, C], 2), ALU.subtract).then_inc(S["ln0"], 1)
            dve.wait_ge(S["ln0a"], 1)
            nc.vector.tensor_reduce(lnv[:, :], xsq, AX.X, ALU.add).then_inc(S["ln0"], 1)
            dve.wait_ge(S["ln0a"], 3)
            dve.wait_ge(S["ln0"], 4)
            tt_(xtok, xtok, bc(lnv[:, :], [P, n, C], 2), ALU.mult).then_inc(S["ln0"], 1)
            dve.wait_ge(S["xT_ready"], B)
            nc.vector.memset(v16.rearrange("p a b -> p (a b)"), 0.0).then_inc(S["v16_zero"], 1)

            dve.wait_ge(S["c_weights"], 8 * 16)
            dve.wait_ge(S["const"], 7 * 16)
            def tokens(a):
                need(dve, "v_mm", a)
                nc.vector.tensor_copy(xb, xT[:, bass.ds(a * T, T)]).then_inc(S["xb_ready"], 1)

            def rope(a, side, stage):
                if stage == 0:
                    need(dve, "stack3", a * (8 * 16))
                    dve.wait_ge(S["c_proj"], a * 4 + 2 * side + 1)
                    need(dve, "c_split", a * 4 + 2 * side)
                    tt_(ra, ps[5][:, :], crot[:, 2 * side, :], ALU.mult).then_inc(S["c_rope_part"], 1)
                elif stage == 1:
                    dve.wait_ge(S["c_proj"], a * 4 + 2 * side + 2)
                    tt_(rb_, ps[7][:, :], crot[:, 2 * side + 1, :], ALU.mult).then_inc(S["c_rope_part"], 1)
                elif stage == 2:
                    dve.wait_ge(S["c_rope_part"], a * 4 + 2 * side + 2)
                    tt_(ra, ra, rb_, ALU.add).then_inc(S["c_rope"], 1)
                elif stage == 3:
                    dve.wait_ge(S["c_rope"], 2 * a + side + 1)
                    nc.vector.tensor_copy(split_qk[:, side, 0, :], ra).then_inc(S["c_split"], 1)
                else:
                    dve.wait_ge(S["c_split"], a * 4 + 2 * side + 1)
                    tt_(split_qk[:, side, 1, :], ra, split_qk[:, side, 0, :].bitcast(F32), ALU.subtract)\
                        .then_inc(S["c_split"], 1)

            tokens(0)
            for stage in range(10):
                rope(0, stage // 5, stage % 5)

            def causal_slot(n, b, part):
                g = b * SLOTS + n
                if (k := earlier(n, part, 5)) is not None:
                    h, qt = k // TT, k % TT
                    heads = b * HEADS + (n - 5) // TT + 1
                    if qt == 0:
                        dve.wait_ge(S["c_exp"], g - 1)
                        need(dve, "c_p", g - 9)
                        r = slice(4 * (h % 2), 4 * (h % 2) + 4)
                        nc.vector.reciprocal(lre[:, r], lse[:, r]).then_inc(S["c_rec"], 1)
                    dve.wait_ge(S["c_rec"], heads)
                    tile = ea[:, h % 2, qt, 0:(qt + 1) * P]
                    ts_(tile, tile, lre[:, k % 8:k % 8 + 1], None, ALU.mult).then_inc(S["c_p"], 1)
                if (k := earlier(n, part, 0)) is not None:
                    dve.wait_ge(S["c_score"], g + 1)
                    need(dve, "c_exp", g - 7)
                    nc.vector.tensor_reduce(nmx[:, k % 8:k % 8 + 1], ps[k % 3][:, 0:(k % TT + 1) * P], AX.X, ALU.max,
                                            negate=True).then_inc(S["c_max"], 1)
                if (n == 15 and part) or n == SLOTS + 15:
                    after = b if n < SLOTS else b + 1
                    dve.wait_ge(S["ca_mm"], after)
                    dve.wait_ge(S["res_in"], after * 16)
                    tt_(xres[:, 1, :, :], ps[7][:, :].rearrange("p (t c) -> p t c", t=TT), xres[:, 0, :, :], ALU.add)\
                        .then_inc(S["ca_sum"], 1)
                if part < 2:
                    if n == 18:
                        tokens(b + 1)
                    if 22 <= n < 27 or 32 <= n < 37:
                        rope(b + 1, n // 10 - 2, n % 10 - 2)

            causal(dve, causal_slot)

            dve.wait_ge(S["ca_sum"], B)
            dve.wait_ge(S["ca_out"], B * 16)
            nc.vector.memset(xs_hi[:, 0:WIN + 1].bitcast(F32), 0.0)
            nc.vector.memset(xs_lo[:, 0:WIN + 1].bitcast(F32), 0.0).then_inc(S["area_free"], 1)
            nc.vector.memset(qbd.rearrange("p a b c d e -> p (a b c d e)"), 0.0)
            nc.vector.memset(kT[:, :, 0:WIN], 0.0)

            with dve.Fori(0, layers) as l:
                dve.wait_ge(S["w_loaded"], (l + 1) * (5 * 16))
                for c in range(4):
                    w = slice(c * 512, (c + 1) * 512)
                    dve.wait_ge(S["w_split_h"], 4 * l + c + 1)
                    tt_(wqk_lo[:, w], wqk_raw[:, w], wqk_hi[:, w].bitcast(F32), ALU.subtract).then_inc(S["w_split"], 2)
                for s in range(2):
                    for u in range(2):
                        m = tt_(rots[:, :, s, u, :], rot[:, :, s, u, :], bc(qks[:, s, u, :], [P, TT, D], 1), ALU.mult)
                m.then_inc(S["rots_ready"], 1)
                dve.wait_ge(S["rots_ready"], l + 1)

                def load_tile(tt, bt, again=True):
                    g = (l * B + bt) * 4 + tt
                    if again:
                        dve.wait_ge(S["proj"], g * 4 - 12)
                        dve.wait_ge(S["xdup"], g * 2 - 6)
                    c0, base = WIN + tt * P, bt * T + tt * P
                    late = 1 if tt == 0 else 0
                    o, o1 = slice(c0, c0 + P), slice(c0 + late, c0 + P)
                    a, c = xT[0:64, bass.ds(base, P)], xT[64:128, bass.ds(base - 1 + late, P - late)]
                    nc.vector.tensor_copy(xs_hi[0:64, o], a)
                    nc.vector.tensor_copy(xs_hi[64:128, o1], c).then_inc(S["xs_part"], 1)
                    dve.wait_ge(S["xs_part"], g + 1)
                    tt_(xs_lo[0:64, o], a, xs_hi[0:64, o].bitcast(F32), ALU.subtract)
                    tt_(xs_lo[64:128, o1], c, xs_hi[64:128, o1].bitcast(F32), ALU.subtract).then_inc(S["xs_ready"], 1)

                def step(t, i, part):
                    def g_of(bt):
                        return l * B + bt

                    def load_next():
                        if v := behind(t, i, part, -1):
                            load_tile(*v, again=not (part == 0 and t + 1 < TT))

                    def double_windows(hl):
                        if not (v := behind(t, i, part, 0)):
                            return
                        tt, bt = v
                        g = g_of(bt) * 4 + tt
                        dve.wait_ge(S["xs_ready"], g + 1)
                        dve.wait_ge(S["xwt"], g * 2 + hl)
                        src = (xs_hi, xs_lo)[hl]
                        for own in range(2):
                            c0 = tt * P + own * WIN
                            m = nc.vector.tensor_copy(
                                xdup[:, hl, :, :, own, :],
                                bc(src[:, c0:c0 + P].bitcast(F32).rearrange("p (w k) -> p w k", w=4), [P, 4, 2, WIN], 2))
                        m.then_inc(S["xdup"], 1)

                    def rotate(c):
                        if not (v := behind(t, i, part, 0)):
                            return
                        tt, bt = v
                        g = g_of(bt) * 16 + (4 * tt + c)
                        s = c // 2
                        dve.wait_ge(S["sq"], g + 2)
                        dve.wait_ge(S["add"], g)
                        src = pj[c % 2][:, :].rearrange("p (h d) -> p h d", h=8)
                        sv = pj[c % 2][:, :].rearrange("p (h e d) -> p h e d", h=8, e=2)
                        tt_(t1[:, c % 2, :].rearrange("p (h d) -> p h d", h=8), src,
                            bc(rots[:, tt, s, 0, :], [P, 8, D], 1), ALU.mult)
                        d4 = t2[:, c % 2, :].rearrange("p (h e d) -> p h e d", h=8, e=2)
                        for e in range(2):
                            m = tt_(d4[:, :, e, :], sv[:, :, 1 - e, :],
                                    bc(rots[:, tt, s, 1, e * 32:e * 32 + 32], [P, 8, 32], 1), ALU.mult)
                        m.then_inc(S["rotd"], 1)

                    def square_sums(c):
                        if not (v := behind(t, i, part, 0)):
                            return
                        tt, bt = v
                        g = g_of(bt) * 16 + (4 * tt + c)
                        half = c // 2
                        dve.wait_ge(S["sq"], g + 2)
                        if c % 2 == 0:
                            dve.wait_ge(S["ln_part"], g_of(bt) * 8 + 2 * tt + half)
                        nc.vector.tensor_reduce(ssq[:, tt % 2, half, 8 * (c % 2):8 * (c % 2) + 8],
                                                sqb[:, c % 2, :].rearrange("p (h d) -> p h d", h=8), AX.X, ALU.add)\
                            .then_inc(S["ssq_raw"], 1)
                        if c % 2:
                            dve.wait_ge(S["ssq_raw"], g + 2)
                            ts_(ssq[:, tt % 2, half, :], ssq[:, tt % 2, half, :], 1e-24, None, ALU.max)\
                                .then_inc(S["ssq"], 1)

                    def shift(wp):
                        if not (v := behind(t, i, part, 2)):
                            return
                        tt, bt = v
                        m_ = g_of(bt) * 8 + 2 * tt + wp
                        dve.wait_ge(S["score"], m_ + 3)
                        s3 = sbank[:, :].rearrange("p (h k) -> p h k", h=HP)
                        nc.vector.tensor_reduce(smax[:, wp, :], s3, AX.X, ALU.max).then_inc(S["smax"], 1)
                        dve.wait_ge(S["smax"], m_ + 1)
                        dve.wait_ge(S["pn"], m_)
                        tt_(dd[:, wp, :].rearrange("p (h k) -> p h k", h=HP), s3,
                            bc(smax[:, wp, :], [P, HP, 64], 2), ALU.subtract).then_inc(S["sub"], 1)

                    def sums(lag, wp):
                        if not (v := behind(t, i, part, lag)):
                            return
                        tt, bt = v
                        m_ = g_of(bt) * 8 + 2 * tt + wp
                        dve.wait_ge(S["exp"], m_ + 1)
                        d3 = dd[:, wp, :].rearrange("p (h k) -> p h k", h=HP)
                        nc.vector.tensor_reduce(ssum[:, wp, :], d3, AX.X, ALU.add).then_inc(S["ssum"], 1)
                        dve.wait_ge(S["ssum"], m_ + 1)
                        nc.vector.reciprocal(srec[:, wp, :], ssum[:, wp, :]).then_inc(S["srec"], 1)

                    def update():
                        v = behind(t, i, part, LAG)
                        if not v or v[0] % 2 == 0:
                            return
                        tt, bt = v
                        hf = tt // 2
                        dve.wait_ge(S["oo"], g_of(bt) * 2 + hf + 2)
                        dst = xT[:, bass.ds(bt * T + hf * 256, 256)]
                        tt_(dst, mbank[:, 0:256], dst, ALU.add).then_inc(S["xupd"], 1)

                    for wp in range(2):
                        sums(3 - wp, 1 - wp)
                        rotate(2 * wp)
                        rotate(2 * wp + 1)
                        shift(wp)
                        square_sums(2 * wp)
                        square_sums(2 * wp + 1)
                        double_windows(wp)
                        if wp == 0:
                            update()
                            load_next()

                dve.wait_ge(S["mx"], l * B)
                load_tile(0, 0, again=False)
                pipeline(dve, step)

                dve.wait_ge(S["xupd"], (l + 1) * (2 * B))
                nc.vector.memset(lx[64:128, :, 0:1], 0.0).then_inc(S["lx_zero"], 1)
                with dve.Fori(0, 2) as j:
                    for e in range(4):
                        n = l * B + 4 * j + e
                        base = (4 * j + e) * T
                        dve.wait_ge(S["lvar"], l * B + 4 * j)
                        if e == 0:
                            dve.wait_ge(S["lx_zero"], 2 * l + j + 1)
                        nc.vector.tensor_copy(lx[0:64, e, :], xT[0:64, bass.ds(base, T)])
                        nc.vector.tensor_copy(lx[64:128, e, 1:T], xT[64:128, bass.ds(base, T - 1)])\
                            .then_inc(S["lx"], 1)
                    for e in range(4):
                        n = l * B + 4 * j + e
                        dve.wait_ge(S["lmean"], n + 1)
                        dve.wait_ge(S["lx"], n + 1)
                        tt_(ld[:, e, :], lx[:, e, :], ps[e][:, :], ALU.subtract).then_inc(S["ldif"], 1)
                    for e in range(4):
                        n = l * B + 4 * j + e
                        dve.wait_ge(S["lrs"], n + 1)
                        tt_(lrs[:, e, :], ld[:, e, :], lrs[:, e, :], ALU.mult).then_inc(S["lmul"], 1)
                        if e == 0:
                            dve.wait_ge(S["w_loaded2"], (l + 1) * (13 * 16))
                        dve.wait_ge(S["lmul"], n + 1)
                        ts_(xn_all[:, bass.ds((4 * j + e) * T, T)], lrs[:, e, :], lng[:, 0:1], lng[:, 1:2],
                            ALU.mult, ALU.add).then_inc(S["xn"], 1)
                    dve.wait_ge(S["lvar"], l * B + 4 * j + 4)
                    nc.vector.memset(lx[64:128, :, 0:1], 0.0).then_inc(S["lx_zero"], 1)

                dve.wait_ge(S["w_split_a"], 2 * l + 1)
                tt_(w1_lo[:, :], w1, w1_hi[:, :].bitcast(F32), ALU.subtract).then_inc(S["w_split_a"], 1)

                def split_tokens(n, first, e):
                    dve.wait_ge(S["aa"], (n - 1) * 3)
                    src = xn_all[:, bass.ds(first * T, T)]
                    nc.vector.tensor_copy(mlp_hi[:, e, :], src).then_inc(S["mhi"], 1)
                    dve.wait_ge(S["mhi"], n + 1)
                    tt_(mlp_lo[:, e, :], src, mlp_hi[:, e, :].bitcast(F32), ALU.subtract).then_inc(S["mlo"], 1)

                def gated(n, e, c):
                    f0, fn = FCH[c]
                    dve.wait_ge(S["down"], l * B)
                    dve.wait_ge(S["aa"], n * 3 + c + 1)
                    dve.wait_ge(S["gelu"], n * 3 + c + 1)
                    nc.vector.scalar_tensor_tensor(uu[0:fn, e, c, :], ps[3 + c][0:fn, :], b1[0:fn, c:c + 1],
                                                   gg[0:fn, e, c, :], ALU.add, ALU.mult).then_inc(S["uu"], 1)

                def add_result(n, batch, e):
                    dve.wait_ge(S["down"], n + 1)
                    dst = xT[:, bass.ds(batch * T, T)]
                    nc.vector.scalar_tensor_tensor(dst, ps[6 + e][:, :], lng[:, 2:3], dst, ALU.add, ALU.add)\
                        .then_inc(S["mx"], 1)

                dve.wait_ge(S["xn"], (l + 1) * B)
                for e in range(2):
                    src = xn_all[:, e * T:(e + 1) * T]
                    nc.vector.tensor_copy(mlp_hi[:, e, :], src).then_inc(S["mhi"], 1)
                    dve.wait_ge(S["mhi"], l * B + e + 1)
                    tt_(mlp_lo[:, e, :], src, mlp_hi[:, e, :].bitcast(F32), ALU.subtract).then_inc(S["mlo"], 1)
                for c in range(3):
                    gated(l * B, 0, c)
                with dve.Fori(1, B // 2) as j:
                    for e in range(2):
                        n = l * B + 2 * j + e
                        split_tokens(n, 2 * j + e, e)
                        dve.wait_ge(S["down"], n - 2)
                        for c in range(3):
                            gated(n - 1, 1 - e, c)
                        add_result(n - 2, 2 * j + e - 2, e)
                for c in range(3):
                    gated(l * B + (B - 1), 1, c)
                for e in range(2):
                    add_result(l * B + (B - 2 + e), B - 2 + e, e)

            dve.wait_ge(S["mx"], layers * B)
            with dve.Fori(0, B) as b:
                dve.wait_ge(S["f_tr"], b)
                nc.vector.tensor_copy(xb, xT[:, bass.ds(b * T, T)]).then_inc(S["xb_ready"], 1)
                dve.wait_ge(S["f_tr"], b + 1)
                dve.wait_ge(S["f_in"], 16 * b + 16)
                tt_(xres[:, 1, :, :], ps[0][:, :].rearrange("p (t c) -> p t c", t=TT), xres[:, 0, :, :], ALU.add)\
                    .then_inc(S["f_sum"], 1)

        @block.gpsimd
        def _(pool):
            pt_ = nc.gpsimd.tensor_tensor
            with pool.Fori(0, layers) as l:
                def step(t, i, part):
                    def g_of(bt):
                        return l * B + bt

                    def add(c):
                        if not (v := behind(t, i, part, 0)):
                            return
                        tt, bt = v
                        g = g_of(bt) * 16 + (4 * tt + c)
                        pool.wait_ge(S["qn"], g + 5)
                        pool.wait_ge(S["rotd"], g + 2)
                        pt_(qsum[:, c % 2, :], t1[:, c % 2, :], t2[:, c % 2, :], ALU.add).then_inc(S["add"], 1)

                    def scale(lag, c):
                        if not (v := behind(t, i, part, lag)):
                            return
                        tt, bt = v
                        g = g_of(bt) * 16 + (4 * tt + c)
                        half = c // 2
                        pool.wait_ge(S["rn"], g_of(bt) * 8 + (2 * tt + half + 1))
                        pool.wait_ge(S["add"], g + 2)
                        pool.wait_ge(S["tr"], g)
                        r = rn[:, tt % 2, half, 8 * (c % 2):8 * (c % 2) + 8].unsqueeze(2).to_broadcast([P, 8, D])
                        pt_(qn[:, c, :].rearrange("p (h d) -> p h d", h=8),
                            qsum[:, c % 2, :].rearrange("p (h d) -> p h d", h=8), r, ALU.mult).then_inc(S["qn"], 1)

                    def normalise(lag, wp):
                        if not (v := behind(t, i, part, lag)):
                            return
                        tt, bt = v
                        m_ = g_of(bt) * 8 + 2 * tt + wp
                        pool.wait_ge(S["srec"], m_ + 1)
                        pool.wait_ge(S["lo"], m_)
                        pt_(pn[:, wp, :].rearrange("p (h k) -> p h k", h=HP),
                            dd[:, wp, :].rearrange("p (h k) -> p h k", h=HP),
                            srec[:, wp, :].unsqueeze(2).to_broadcast([P, HP, 64]), ALU.mult).then_inc(S["pn"], 1)

                    def rests_of_p(lag, wp):
                        if not (v := behind(t, i, part, lag)):
                            return
                        tt, bt = v
                        pool.wait_ge(S["hi"], g_of(bt) * 8 + (2 * tt + wp + 1))
                        pt_(p2[:, wp, :, 1, :], pn[:, wp, :].rearrange("p (h k) -> p h k", h=HP),
                            p2[:, wp, :, 0, :].bitcast(F32), ALU.subtract).then_inc(S["lo"], 1)

                    for wp in range(2):
                        scale(1 - wp, 2 - 2 * wp)
                        scale(1 - wp, 3 - 2 * wp)
                        normalise(3 - wp, 1 - wp)
                        add(2 * wp)
                        add(2 * wp + 1)
                        rests_of_p(3 - wp, 1 - wp)

                pipeline(pool, step)


def kernel(L0_attn_x, L0_attn_Wq_down, L0_attn_Wk_down, L0_attn_Wv_down, L0_attn_Wq_up_c, L0_attn_Wq_up_e,
           L0_attn_Wk_up_c, L0_attn_Wk_up_e, L0_attn_Wv_up, L0_attn_Wc, L0_ffn_Wqkv, L0_ffn_q_scale,
           L0_ffn_k_scale, L0_ffn_Wo, L0_ffn_ln_g, L0_ffn_ln_b, L0_ffn_W1, L0_ffn_b1, L0_ffn_W2, L0_ffn_b2):
    import concourse.bacc as bacc
    from concourse.bass_utils import run_bass_kernel_spmd

    f32 = np.float32

    def turned(w):
        return np.asarray(w).T.reshape(HP, P, C).transpose(1, 0, 2)

    def two_heads(parts):
        n = sum(p.shape[1] for p in parts)
        o = np.zeros((P, 2, n), f32)
        o[0:LAT, 0], o[LAT:P, 1] = np.concatenate(parts, 1), np.concatenate(parts, 1)
        return o

    swap4, zero4 = [1, 0, 3, 2], np.zeros((LAT, 4), f32)
    qc, qe, kc, ke, vu = (np.asarray(a) for a in (L0_attn_Wq_up_c, L0_attn_Wq_up_e, L0_attn_Wk_up_c, L0_attn_Wk_up_e,
                                                  L0_attn_Wv_up))
    W, W1, W2 = np.asarray(L0_ffn_Wqkv), np.asarray(L0_ffn_W1), np.asarray(L0_ffn_W2)
    Wo = np.asarray(L0_ffn_Wo).reshape(DEPTH, HP, 2, D, C).transpose(0, 2, 3, 1, 4)
    WvT = W[:, :, 2 * INNER:].transpose(0, 2, 1).reshape(DEPTH, HP, P, C).transpose(0, 2, 1, 3)
    qs, ks = np.asarray(L0_ffn_q_scale), np.asarray(L0_ffn_k_scale)
    half = D // 2
    qks = np.stack([np.stack([s, np.concatenate([s[:, half:], s[:, :half]], 1)], 1) for s in (qs, ks)], 1)
    arrays = {
        "x": L0_attn_x, "wqdT": turned(L0_attn_Wq_down), "wkdT": turned(L0_attn_Wk_down), "wvdT": turned(L0_attn_Wv_down),
        "upq": two_heads([qc, qe, zero4, qe[:, swap4]]), "upk": two_heads([kc, ke, zero4, ke[:, swap4]]),
        "upv": two_heads([vu]), "Wc": L0_attn_Wc, "Wqkv": W, "WvT": WvT, "Wo": Wo, "qks": qks,
        "ln_g": np.asarray(L0_ffn_ln_g)[:, :, None], "ln_b": np.asarray(L0_ffn_ln_b)[:, :, None],
        "b2": np.asarray(L0_ffn_b2)[:, :, None], "W1": W1, "b1": np.asarray(L0_ffn_b1)[:, :, None], "W2": W2,
        **shape_constants(),
    }
    arrays = {k: np.ascontiguousarray(v) for k, v in arrays.items()}
    nc = bacc.Bacc("TRN2", target_bir_lowering=False, num_devices=1)
    ins = {k: nc.dram_tensor("in_" + k, v.shape, mybir.dt.from_np(v.dtype), kind="ExternalInput").ap()
           for k, v in arrays.items()}
    out = nc.dram_tensor("out", (B, T, C), F32, kind="ExternalOutput").ap()
    build(nc, ins, out)
    r = run_bass_kernel_spmd(nc, [{"in_" + k: v for k, v in arrays.items()}], core_ids=[0])
    return r.results[0]["out"]
```

```python
import math
from contextlib import ExitStack

import numpy as np

import concourse.bass as bass
from concourse import mybir

F32, F32R, BF16 = mybir.dt.float32, mybir.dt.float32r, mybir.dt.bfloat16
ACT = mybir.ActivationFunctionType
ALU = mybir.AluOpType
AX = mybir.AxisListType

P = 128
B, T, C = 8, 512, 128
TT = T // P
NTOK = B * T
HEADS, DA, LAT = 16, 8, 64
DEPTH, D, WIN = 6, 64, 32
HP = HEADS // 2
INNER = HEADS * D
FF = 341
FCH = [(0, 128), (128, 128), (256, FF - 256)]
MASKED = -1.0e30
AREA = 25856
OUT_PARTS = (((6, 3), (5, 1)), ((5, 2), (4, 0)))
LAG = 6


def shape_constants():
    f32 = np.float32
    half = np.arange(0, D, 2, dtype=f32)
    inv_freq = (f32(1.0) / np.power(f32(10000.0), half / f32(D))).astype(f32)
    t = np.arange(T, dtype=f32)
    freqs = (t[:, None] * inv_freq[None, :]).astype(f32)
    freqs = np.concatenate([freqs, freqs], -1)
    base = ((half + f32(0.4 * D)) / f32(1.4 * D)).astype(f32)
    power = ((t - T // 2) / (WIN // 2)).astype(f32)
    scale = (base[None, :] ** power[:, None]).astype(f32)
    scale = np.concatenate([scale, scale], -1)
    sign = np.where(np.arange(D) < D // 2, -1.0, 1.0).astype(f32)
    cos, sin = np.cos(freqs), np.sin(freqs) * sign
    rot = np.stack([np.stack([cos * scale * 8, sin * scale * 8], 1), np.stack([cos / scale, sin / scale], 1)], 1)
    rot = rot.reshape(TT, P, 2, 2, D).transpose(1, 0, 2, 3, 4).astype(f32)
    inv4 = (f32(1.0) / np.power(f32(10000.0), np.arange(0, 4, 2, dtype=f32) / f32(4))).astype(f32)
    fr = (t[:, None] * inv4[None, :]).astype(f32)
    fr = np.concatenate([fr, fr], -1)
    s4 = np.array([-1, 1, -1, 1], f32)
    ca = np.concatenate([np.ones((T, 4), f32), np.cos(fr)], -1)
    sa = np.concatenate([np.zeros((T, 4), f32), np.sin(fr) * s4], -1)
    ca, sa = np.tile(ca, (1, HEADS)).T, np.tile(sa, (1, HEADS)).T
    qs = f32(1.0 / math.sqrt(DA))
    crot = np.stack([ca * qs, sa * qs, ca, sa], 1).astype(f32)
    row, key = np.arange(P), np.arange(2 * WIN)
    q = row % WIN
    ok = (key[None] >= q[:, None]) & (key[None] <= q[:, None] + WIN)
    first = ok & ((row[:, None] >= 2 * WIN) | (key[None] >= WIN))
    lmask = np.stack([np.tile(np.where(m, 0.0, MASKED), (1, HP)) for m in (first, ok)], 1)
    tri = np.where(np.arange(P)[None] <= np.arange(P)[:, None], 0.0, MASKED)
    bf = mybir.dt.np(BF16)
    return {
        "c_rot": rot, "c_crot": crot, "c_lmask": lmask.astype(bf), "c_tri": tri.astype(bf),
        "c_id": np.eye(P, dtype=f32), "c_idb": np.eye(P, dtype=f32).astype(bf),
        "c_hm": (np.arange(P)[:, None] % 32 // DA == np.arange(4)[None]).astype(f32),
        "c_avg": np.full((P, P), 1.0 / C, f32),
    }


def build(nc, ins, out, layers=DEPTH):
    ctx = ExitStack()
    with ctx:
        def sb(name, shape, dt=F32):
            return ctx.enter_context(nc.sbuf_tensor("sb_" + name, [P] + shape, dt))

        def sem(name):
            return ctx.enter_context(nc.semaphore("s_" + name))

        scratch = nc.dram_tensor("x_plus_causal", [B, TT, P, C], F32, kind="Internal").ap()
        xd = ins["x"].rearrange("b (t p) c -> b p t c", p=P)
        scr = scratch.rearrange("b t p c -> b p t c")
        od = out.rearrange("b (t p) c -> b p t c", p=P)

        xT = sb("xT", [NTOK])
        ident = sb("ident", [P])
        identb = sb("identb", [P], BF16)
        lmask = sb("lmask", [2, HP * 2 * WIN], BF16)
        tri = sb("tri", [P], BF16)
        hm = sb("hm", [4])
        avg = sb("avg", [P])
        eps = sb("eps", [1])
        wqk_hi, wqk_lo = sb("wqk_hi", [2 * INNER], F32R), sb("wqk_lo", [2 * INNER], F32R)
        wo_bd = sb("wo_bd", [HP, 2, C])
        wvo = sb("wvo", [HEADS, C])
        w1_hi, w1_lo = sb("w1_hi", [2 * FF], F32R), sb("w1_lo", [2 * FF], F32R)
        w2_hi, w2_lo = sb("w2_hi", [3, C], F32R), sb("w2_lo", [3, C], F32R)
        b1 = sb("b1", [6])
        lng = sb("lng", [3])
        rot = sb("rot", [TT, 2, 2, D])
        rots = sb("rots", [TT, 2, 2, D])
        qks = sb("qks", [2, 2, D])
        xs = sb("xs", [WIN + T])
        xs_hi, xs_lo = sb("xs_hi", [2, P], F32R), sb("xs_lo", [2, P], F32R)
        xwin = sb("xwin", [TT, 2, 4, P], F32R)
        p2 = sb("p2", [2, HP, 2, 2 * WIN], F32R)
        ptT = sb("ptT", [2, HP, P], F32R)
        ssq, lnb, rn = sb("ssq", [2, 2, 16]), sb("lnb", [2, 2, 16]), sb("rn", [2, 2, 16])
        smax, ssum, srec = sb("smax", [2, HP]), sb("ssum", [2, HP]), sb("srec", [2, HP])
        area = sb("area", [AREA])
        at = [0]

        def take(*shape):
            n = int(np.prod(shape))
            v = area[:, at[0]:at[0] + n]
            at[0] += n
            if len(shape) == 1:
                return v
            names = " ".join("abcde"[:len(shape)])
            return v.rearrange(f"p ({names}) -> p {names}", **dict(zip("abcde", shape)))

        ysb = take(2, 8, HEADS * WIN)
        sqb, t1, t2 = take(2, 512), take(2, 512), take(2, 512)
        qsum, qn = take(2, 512), take(4, 512)
        dd, pn = take(2, 512), take(2, 512)
        xdup, xw = take(4, 2, 2, WIN), take(512)
        qbd = take(2, HP, 4, 2, WIN)
        kT = take(HP, WIN + T)
        assert at[0] <= AREA
        at[0] = 0
        xn_all = take(NTOK)
        wqk_raw, wv_raw = take(2 * INNER), take(HP, C)
        w1, w2 = take(2 * FF), take(3, C)
        at_ln = at[0]
        ld, lrs = take(B, T), take(B, T)
        at[0] = at_ln
        gg = take(2, 3, 512)
        uu = take(2, 3, 512)
        assert at[0] <= AREA - 4096 - HP * (WIN + T)
        at[0] = 0
        v16 = take(TT, HEADS * (P + DA))
        ptA = take(4, TT, T)
        ea_ = take(2, (TT + 1) * TT // 2 * P)
        crot = take(4, T)
        ra, rb_ = take(T), take(T)
        yT = take(T)
        xb = take(T)
        wcomb = take(5, P)
        upq, upk, upv = take(2, 16), take(2, 16), take(2, 8)
        wc = take(C)
        xres = take(2, TT, C)
        assert at[0] <= AREA
        wd = area[:, 8704 + 512:8704 + 512 + 3 * 1024].rearrange("p (a b c) -> p a b c", a=3, b=HP)
        xtok = area[:, 0:NTOK].rearrange("p (n c) -> p n c", c=C)
        lx = xn_all.rearrange("p (b t) -> p b t", t=T)
        final = area[:, AREA - 2 * NTOK:AREA].rearrange("p (s b t c) -> p s b t c", s=2, b=B, t=TT)
        nmx, lse, lre = sb("nmx", [8]), sb("lse", [8]), sb("lre", [8])
        lnm, lnv, lnr = sb("lnm", [NTOK // P]), sb("lnv", [NTOK // P]), sb("lnr", [NTOK // P])
        mlp = p2[:, :, :, :, :].rearrange("p a b c d -> p (a b c d)").rearrange("p (s e t) -> p s e t", s=2, e=2)
        mlp_hi, mlp_lo = mlp[:, 0], mlp[:, 1]
        split_qk = mlp
        stacks = xwin[:, :, :, :, :].rearrange("p a b c d -> p (a b c d)").rearrange("p (s g t) -> p s g t", s=2, g=4)
        qm = ptT[:, :, 0:4, :]
        chunks = [stacks[:, i // 4, i % 4, :] for i in range(8)]
        chunks += [ptT[:, i // 2, 4 * (i % 2):4 * (i % 2) + 4, :].rearrange("p a b -> p (a b)") for i in range(4)]
        uu_hi = [chunks[0:3], chunks[3:6]]
        uu_lo = [chunks[6:9], chunks[9:12]]

        def ea(h, qt, k0, k1):
            c0 = qt * (qt + 1) // 2 * P
            return ea_[:, h % 2, c0 + k0:c0 + k1]

        spare = sb("spare", [32])

        ps = [ctx.enter_context(nc.psum_tensor(f"bank{i}", [P, 512], F32)) for i in range(8)]
        pj, rbank, sbank, tbank, ybank, mbank = ps[0:2], ps[2], ps[3], ps[4], ps[5:7], ps[7]

        S = {n: sem(n) for n in (
            "const", "xload0", "xload1", "xload2", "xload3", "c_weights", "eps_set", "v16_zero", "wo_zero", "w_loaded", "w_loaded2", "w1_loaded", "w2_loaded",
            "wcomb_mm", "wcomb_ready",
            "ln0_mean", "ln0_sq", "ln0_rstd", "ln0_x", "xn_tr", "xT_ready", "xs_zero",
            "xb_ready", "c_proj", "c_rope", "c_rope_part", "v_mm", "v_ready", "qm_ready", "c_score", "c_max",
            "c_exp", "c_split", "stack0", "stack1", "stack2", "stack3", "c_rec", "c_p", "c_tr", "c_ptev", "c_pv", "yT_ready", "ca_mm", "res_in", "ca_sum", "ca_out",
            "kT_zero", "w_split", "w_split_h", "w_split_a", "rots_ready", "wvo_mm", "wvo_ready", "xs_part", "xs_ready",
            "proj", "sq", "rotd", "ssq", "ssq_raw", "ln_part", "rn", "add", "qn", "tr", "ev", "score",
            "smax", "sub", "exp", "ssum", "srec", "pn", "hi", "lo", "pt", "ptev", "yy", "yev0", "yev1",
            "xdup", "xwt", "xwev", "xwh", "xwl", "oo", "xupd",
            "lx", "lx_zero", "lmean", "ldif", "lsq", "lvar", "lln", "lrs", "lmul", "xn", "mhi", "mlo", "gate", "gelu", "aa",
            "uu", "uh", "ul", "w2_split", "down", "mx",
            "f_in", "f_tr", "f_sum", "f_out",
        )}
        block = ctx.enter_context(nc.Block())

        def pipeline(eng, step):
            for t in range(LAG):
                step(t, 0, 0)
            with eng.Fori(0, B - 2) as i:
                for t in range(LAG, LAG + TT):
                    step(t, i, 1)
            for t in range(LAG, LAG + 2 * TT):
                step(t, B - 2, 2)

        def behind(t, i, part, lag):
            s = t - lag
            if (part == 0 and s < 0) or (part == 2 and s >= 2 * TT):
                return None
            return s % TT, i + s // TT

        SLOTS, DRAIN = HEADS * TT, 19

        def causal(eng, slot):
            for n in range(SLOTS):
                slot(n, 0, 0)
            with eng.Fori(1, B - 1) as b:
                for n in range(SLOTS):
                    slot(n, b, 1)
            for n in range(SLOTS + DRAIN):
                slot(n, B - 1, 2)

        def earlier(n, part, lag):
            k = n - lag
            if part == 2:
                return k % SLOTS if k < SLOTS else None
            return None if part == 0 and k < 0 else k % SLOTS

        def need(eng, name, v):
            if not isinstance(v, int) or v > 0:
                eng.wait_ge(S[name], v)

        @block.sync
        def _(sp):
            tokens = ins["x"].rearrange("b (t p) c -> p (b t) c", p=P)
            for q in range(4):
                sp.dma_start(xtok[:, 8 * q:8 * q + 8, :], tokens[:, 8 * q:8 * q + 8, :]).then_inc(S[f"xload{q}"], 16)
            for dst, name in ((ident, "c_id"), (identb, "c_idb"), (tri, "c_tri"), (hm, "c_hm"), (avg, "c_avg")):
                sp.dma_start(dst[:, :], ins[name]).then_inc(S["const"], 16)
            sp.dma_start(lmask[:, :, :], ins["c_lmask"]).then_inc(S["const"], 16)
            sp.dma_start(rot[:, :, :, :], ins["c_rot"]).then_inc(S["const"], 16)
            for i, name in enumerate(("wqdT", "wkdT", "wvdT")):
                sp.dma_start(wd[:, i, :, :], ins[name]).then_inc(S["c_weights"], 16)
            for dst, name in ((upq, "upq"), (upk, "upk"), (upv, "upv")):
                sp.dma_start(dst, ins[name]).then_inc(S["c_weights"], 16)
            sp.dma_start(wc, ins["Wc"]).then_inc(S["c_weights"], 16)
            sp.dma_start(crot, ins["c_crot"]).then_inc(S["c_weights"], 16)
            def stack(a, hg):
                need(sp, "c_score", (a - 1) * SLOTS + 16 * (hg + 1))
                for side in range(2):
                    for term in range(4):
                        part = (term // 2, term % 2)[side]
                        sp.dma_start(stacks[32 * term:32 * term + 32, side, hg, :].bitcast(F32),
                                     split_qk[32 * hg:32 * hg + 32, side, part, :].bitcast(F32)).then_inc(S[f"stack{hg}"], 16)

            for b in range(B):
                if b == 0:
                    sp.wait_ge(S["c_split"], 4)
                    for hg in range(4):
                        stack(0, hg)
                else:
                    sp.wait_ge(S["ca_sum"], b)
                    sp.dma_start(scr[b - 1], xres[:, 1, :, :]).then_inc(S["ca_out"], 16)
                    sp.wait_ge(S["ca_out"], b * 16)
                sp.dma_start(xres[:, 0, :, :], xd[b]).then_inc(S["res_in"], 16)
                if b < B - 1:
                    sp.wait_ge(S["c_split"], 4 * (b + 2))
                    for hg in range(4):
                        stack(b + 1, hg)
            for l in range(layers + 1):
                source = min(l, layers - 1)
                sp.wait_ge(S["c_pv"], B * HEADS)
                sp.wait_ge(S["wo_zero"], 1)
                sp.wait_ge(S["xupd"], l * (2 * B))
                sp.wait_ge(S["w_split"], l * 8)
                sp.wait_ge(S["wvo_mm"], l * 4)
                sp.dma_start(wqk_raw, ins["Wqkv"][source][:, 0:2 * INNER]).then_inc(S["w_loaded"], 16)
                sp.dma_start(wv_raw, ins["WvT"][source]).then_inc(S["w_loaded"], 16)
                sp.dma_start(wo_bd[0:64, :, 0, :], ins["Wo"][source][0]).then_inc(S["w_loaded"], 16)
                sp.dma_start(wo_bd[64:128, :, 1, :], ins["Wo"][source][1]).then_inc(S["w_loaded"], 16)
                sp.dma_start(qks[:, :, :, :], ins["qks"][source].unsqueeze(0).to_broadcast([P, 2, 2, D])).then_inc(S["w_loaded"], 16)
                if l == layers:
                    break
                if l == 0:
                    sp.wait_ge(S["ca_sum"], B)
                    sp.dma_start(scr[B - 1], xres[:, 1, :, :]).then_inc(S["ca_out"], 16)
                sp.wait_ge(S["mx"], l * B)
                for j, name in enumerate(("ln_g", "ln_b", "b2")):
                    sp.dma_start(lng[:, j:j + 1], ins[name][l]).then_inc(S["w_loaded2"], 16)
                for j, (f0, fn) in enumerate(FCH):
                    sp.dma_start(b1[0:fn, j:j + 1], ins["b1"][l][f0:f0 + fn, :]).then_inc(S["w_loaded2"], 16)
                    sp.dma_start(b1[0:fn, 3 + j:4 + j], ins["b1"][l][FF + f0:FF + f0 + fn, :]).then_inc(S["w_loaded2"], 16)
                sp.wait_ge(S["xupd"], (l + 1) * (2 * B))
                sp.dma_start(w1, ins["W1"][l]).then_inc(S["w1_loaded"], 16)
                for j, (f0, fn) in enumerate(FCH):
                    sp.dma_start(w2[0:fn, j, :], ins["W2"][l][f0:f0 + fn, :]).then_inc(S["w2_loaded"], 16)

            sp.dma_start(final[:, 0, :, :, :], scratch.rearrange("b t p c -> p b t c")).then_inc(S["f_in"], 16)
            for b in range(B):
                sp.wait_ge(S["f_sum"], b + 1)
                sp.dma_start(od[b], final[:, 1, b, :, :]).then_inc(S["f_out"], 16)
            sp.wait_ge(S["f_out"], B * 16)

        @block.tensor
        def _(pe):
            def mm(o, a, b, start=True, stop=True):
                return nc.tensor.matmul(o, a, b, start=start, stop=stop, skip_group_check=True)

            def split3(o, a_hi, a_lo, b_hi, b_lo):
                mm(o, a_hi, b_hi, True, False)
                mm(o, a_hi, b_lo, False, False)
                return mm(o, a_lo, b_hi, False, True)

            pe.wait_ge(S["const"], 7 * 16)
            for b in range(B):
                if b == 4:
                    pe.wait_ge(S["c_weights"], 8 * 16)
                    for i, (up, n) in enumerate(((upq, 16), (upk, 16), (upv, 8))):
                        for hp in range(HP):
                            m = mm(ps[4 + i][:, hp * 2 * n:(hp + 1) * 2 * n], wd[:, i, hp, :],
                                   up.rearrange("p a b -> p (a b)"))
                        m.then_inc(S["wcomb_mm"], 1)
                pe.wait_ge(S["ln0_x"], b // 2 + 1)
                if b >= 4:
                    pe.wait_ge(S["xT_ready"], b - 3)
                for t in range(TT):
                    m = nc.tensor.transpose(ps[b % 4][:, t * P:(t + 1) * P], xtok[:, b * TT + t, :], ident[:, :])
                m.then_inc(S["xn_tr"], 1)
            pe.wait_ge(S["wcomb_ready"], 5)

            def project_causal(a, i):
                if i == 0:
                    need(pe, "xb_ready", a + 1)
                    need(pe, "v_ready", a)
                    need(pe, "ca_sum", a - 1)
                elif i % 2 == 0:
                    pe.wait_ge(S["c_rope_part"], a * 4 + i)
                if i < 4:
                    mm(ps[(5, 7)[i % 2]][:, :], wcomb[:, i, :], xb).then_inc(S["c_proj"], 1)
                else:
                    for t in range(TT):
                        m = mm(ps[5][:, t * P:(t + 1) * P], xb[:, t * P:(t + 1) * P], wcomb[:, 4, :])
                    m.then_inc(S["v_mm"], 1)

            for i in range(5):
                project_causal(0, i)

            def causal_slot(n, b, part):
                g = b * SLOTS + n
                if (k := earlier(n, part, 0)) is not None:
                    h, qt = k // TT, k % TT
                    if qt == 0:
                        pe.wait_ge(S["qm_ready"], b * HEADS + h + 1)
                    need(pe, "c_exp", g - 2 if k >= 3 else b * SLOTS)
                    o = ps[k % 3]
                    mm(o[:, 0:(qt + 1) * P], qm[:, h % 2, qt, :], stacks[:, 1, h // 4, 0:(qt + 1) * P], True, False)
                    mm(o[:, qt * P:(qt + 1) * P], identb[:, :], tri[:, :], False, True).then_inc(S["c_score"], 1)
                if (k := earlier(n, part, 7)) is not None:
                    pe.wait_ge(S["c_p"], g - 6)
                    need(pe, "c_ptev", g - 8)
                    for kt in range(k % TT + 1):
                        m = nc.tensor.transpose(ps[(3, 6)[k % 2]][:, kt * P:(kt + 1) * P],
                                                ea(k // TT, k % TT, kt * P, (kt + 1) * P), ident[:, :])
                    m.then_inc(S["c_tr"], 1)
                if (k := earlier(n, part, 15)) is not None:
                    h, kt = k // TT, k % TT
                    if kt == 0:
                        pe.wait_ge(S["c_ptev"], g - 11)
                    if k == 0:
                        pe.wait_ge(S["v_ready"], b + 1)
                        need(pe, "yT_ready", b)
                    m = mm(ps[4][:, kt * P:T], v16[:, kt, h * P:(h + 1) * P], ptA[:, h % 4, kt, kt * P:T],
                           k == 0, k == SLOTS - 1)
                    if kt == TT - 1:
                        m.then_inc(S["c_pv"], 1)
                if (n == 17 and part) or n == SLOTS + 17:
                    after = b if n < SLOTS else b + 1
                    pe.wait_ge(S["yT_ready"], after)
                    for t in range(TT):
                        m = mm(ps[7][:, t * P:(t + 1) * P], yT[:, t * P:(t + 1) * P], wc)
                    m.then_inc(S["ca_mm"], 1)
                if part < 2 and n in (20, 22, 30, 32, 40):
                    project_causal(b + 1, (20, 22, 30, 32, 40).index(n))

            causal(pe, causal_slot)

            with pe.Fori(0, layers) as l:
                def mean(b):
                    pe.wait_ge(S["lx"], l * B + b + 1)
                    if b >= 4:
                        pe.wait_ge(S["ldif"], l * B + b - 3)
                    mm(ps[b % 4][:, :], avg[:, :], lx[:, b, :]).then_inc(S["lmean"], 1)

                def variance(b):
                    pe.wait_ge(S["lsq"], l * B + b + 1)
                    if b >= 4:
                        pe.wait_ge(S["lln"], l * B + b - 3)
                    mm(ps[4 + b % 4][:, :], avg[:, :], lx[:, b, :]).then_inc(S["lvar"], 1)

                pe.wait_ge(S["gelu"], l * (3 * B))

                def step(t, i, part):
                    def g_of(bt):
                        return l * B + bt

                    def join_weights():
                        if part or t >= 4:
                            return
                        if t == 0:
                            pe.wait_ge(S["wo_zero"], 1)
                            pe.wait_ge(S["mx"], l * B)
                        pe.wait_ge(S["w_loaded"], (l + 1) * (5 * 16))
                        pe.wait_ge(S["wvo_ready"], 4 * l + t)
                        for j in range(2):
                            hp = 2 * t + j
                            m = mm(mbank[:, j * 256:(j + 1) * 256], wv_raw[:, hp, :],
                                   wo_bd[:, hp, :, :].rearrange("p a b -> p (a b)"))
                        m.then_inc(S["wvo_mm"], 1)

                    def project(c):
                        if not (v := behind(t, i, part, 0)):
                            return
                        tt, bt = v
                        if c == 0:
                            pe.wait_ge(S["xs_ready"], g_of(bt) * 4 + tt + 1)
                        if part == 0 and t == 0:
                            pe.wait_ge(S["w_split"], 8 * l + 2 * c + 2)
                        g = g_of(bt) * 16 + (4 * tt + c)
                        pe.wait_ge(S["sq"], g)
                        pe.wait_ge(S["rotd"], g)
                        w = slice(c * 512, (c + 1) * 512)
                        split3(pj[c % 2][:, :], xs_hi[:, tt % 2, :], xs_lo[:, tt % 2, :], wqk_hi[:, w], wqk_lo[:, w])\
                            .then_inc(S["proj"], 1)

                    def turn_qk(c):
                        if not (v := behind(t, i, part, 1)):
                            return
                        tt, bt = v
                        g = g_of(bt) * 16 + (4 * tt + c)
                        pe.wait_ge(S["qn"], g + 7)
                        if c == 1:
                            pe.wait_ge(S["xwev"], g_of(bt) * 4 + tt + 1)
                        else:
                            pe.wait_ge(S["ev"], g)
                        for j in range(4):
                            m = nc.tensor.transpose(rbank[:, j * P:(j + 1) * P], qn[:, c, j * P:(j + 1) * P],
                                                    ident[:, :])
                        m.then_inc(S["tr"], 1)

                    def score(wp):
                        if not (v := behind(t, i, part, 2)):
                            return
                        tt, bt = v
                        pe.wait_ge(S["ev"], g_of(bt) * 16 + 4 * tt + 4)
                        pe.wait_ge(S["sub"], g_of(bt) * 8 + 2 * tt + wp)
                        first = tt == 0 and wp == 0
                        mm(sbank[:, :], identb[:, :], lmask[:, 0 if first else 1, :], True, False)
                        for w2_ in range(2):
                            for hp in range(HP):
                                w = 2 * wp + w2_
                                k0 = tt * P + w * WIN
                                m = mm(sbank[64 * w2_:64 * w2_ + 64, hp * 64:(hp + 1) * 64],
                                       qbd[:, tt % 2, hp, w, :, :].rearrange("p a b -> p (a b)"),
                                       kT[:, hp, k0:k0 + 2 * WIN], False, w2_ == 1 and hp == HP - 1)
                        m.then_inc(S["score"], 1)

                    def turn_p(wp, half):
                        if not (v := behind(t, i, part, 3)):
                            return
                        tt, bt = v
                        m_ = g_of(bt) * 8 + 2 * tt + wp
                        pe.wait_ge(S["lo"], m_ + 2)
                        pe.wait_ge(S["ptev"], m_ * 2 + half)
                        for j in range(4):
                            m = nc.tensor.transpose(
                                tbank[:, j * P:(j + 1) * P],
                                p2[:, wp, 4 * half + j, :, :].rearrange("p a b -> p (a b)").bitcast(F32), ident[:, :])
                        m.then_inc(S["pt"], 1)

                    def weigh(lag, wp):
                        if not (v := behind(t, i, part, lag)):
                            return
                        tt, bt = v
                        m_ = g_of(bt) * 8 + 2 * tt + wp
                        pe.wait_ge(S["ptev"], m_ * 2 + 2)
                        pe.wait_ge(S["xwl"], g_of(bt) * 4 + tt + 1)
                        for w2_, free in ((0, "yev0"), (1, "yev1")):
                            pe.wait_ge(S[free], m_)
                            w = 2 * wp + w2_
                            rhs = ptT[:, wp, :, 64 * w2_:64 * w2_ + 64]
                            mm(ybank[w2_][:, :], xwin[:, tt, 0, w, :], rhs, True, False)
                            mm(ybank[w2_][:, :], xwin[:, tt, 1, w, :], rhs, False, True).then_inc(S["yy"], 1)

                    def windows():
                        if not (v := behind(t, i, part, 1)):
                            return
                        tt, bt = v
                        g = g_of(bt) * 4 + tt
                        pe.wait_ge(S["xdup"], g + 1)
                        pe.wait_ge(S["ev"], g * 4 + 1)
                        for w in range(4):
                            m = nc.tensor.transpose(rbank[:, w * P:(w + 1) * P],
                                                    xdup[:, w, :, :, :].rearrange("p a b c -> p (a b c)"), ident[:, :])
                        m.then_inc(S["xwt"], 1)

                    def project_out(wp):
                        for lag, k in OUT_PARTS[wp]:
                            v = behind(t, i, part, lag)
                            if not v or v[0] % 2 == 0:
                                continue
                            tt, bt = v
                            hf = tt // 2
                            if k == 0:
                                pe.wait_ge(S["yev0"], g_of(bt) * 8 + 2 * tt + 2)
                                pe.wait_ge(S["yev1"], g_of(bt) * 8 + 2 * tt + 2)
                                pe.wait_ge(S["xupd"], g_of(bt) * 2 + hf)
                            for h in range(4 * k, 4 * k + 4):
                                m = mm(mbank[:, 0:256], wvo[:, h, :], ysb[:, hf, :, h * WIN:(h + 1) * WIN],
                                       h == 0, h == HEADS - 1)
                            if k == 3:
                                m.then_inc(S["oo"], 1)

                    if part == 2 and t == LAG + 2 * TT - 1:
                        pe.wait_ge(S["rotd"], (l + 1) * (16 * B) + 1)
                        pe.wait_ge(S["sq"], (l + 1) * (16 * B) + 1)
                        pe.wait_ge(S["ev"], (l + 1) * (16 * B))
                        pe.wait_ge(S["sub"], (l + 1) * (8 * B))
                        for b in range(4):
                            mean(b)
                    for wp in range(2):
                        project(2 * wp)
                        turn_qk(2 * wp)
                        turn_p(wp, 0)
                        project(2 * wp + 1)
                        score(wp)
                        if wp == 0:
                            windows()
                        turn_p(wp, 1)
                        weigh(4 - wp, 1 - wp)
                        turn_qk(2 * wp + 1)
                        project_out(wp)
                    join_weights()

                pipeline(pe, step)

                for b in range(4):
                    if b == 3:
                        pe.wait_ge(S["xupd"], (l + 1) * (2 * B))
                    variance(b)
                    mean(b + 4)
                for b in range(4, B):
                    variance(b)

                def down(n, e):
                    pe.wait_ge(S["ul"], n * 3 + 3)
                    pe.wait_ge(S["mx"], n - 1 if e else n)
                    for c, (f0, fn) in enumerate(FCH):
                        mm(ps[6 + e][:, :], w2_hi[0:fn, c, :], uu_hi[e][c][0:fn], c == 0, False)
                        mm(ps[6 + e][:, :], w2_hi[0:fn, c, :], uu_lo[e][c][0:fn], False, False)
                        m = mm(ps[6 + e][:, :], w2_lo[0:fn, c, :], uu_hi[e][c][0:fn], False, c == 2)
                    m.then_inc(S["down"], 1)

                def mlp_pair(n0, first):
                    for e in range(2):
                        n = n0 + e
                        pe.wait_ge(S["mlo"], n + 1)
                        pe.wait_ge(S["gelu"], n * 3)
                        for c, (f0, fn) in enumerate(FCH):
                            f = slice(FF + f0, FF + f0 + fn)
                            split3(ps[c][0:fn, :], w1_hi[:, f], w1_lo[:, f], mlp_hi[:, e, :], mlp_lo[:, e, :])\
                                .then_inc(S["gate"], 1)
                        if first and e == 0:
                            pe.wait_ge(S["lln"], (l + 1) * B)
                        pe.wait_ge(S["uu"], n * 3)
                        for c, (f0, fn) in enumerate(FCH):
                            f = slice(f0, f0 + fn)
                            split3(ps[3 + c][0:fn, :], w1_hi[:, f], w1_lo[:, f], mlp_hi[:, e, :], mlp_lo[:, e, :])\
                                .then_inc(S["aa"], 1)
                        if e and first:
                            pe.wait_ge(S["w2_split"], 2 * l + 2)
                        if e or not first:
                            down(n - 1, 1 - e)

                pe.wait_ge(S["ldif"], (l + 1) * B)
                pe.wait_ge(S["w_split_a"], 2 * l + 2)
                mlp_pair(l * B, True)
                with pe.Fori(1, B // 2) as j:
                    mlp_pair(l * B + 2 * j, False)
                down(l * B + (B - 1), 1)

            pe.wait_ge(S["gelu"], layers * B * 3)
            pe.wait_ge(S["uu"], layers * B * 3)
            for b in range(B):
                pe.wait_ge(S["mx"], (layers - 1) * B + (b + 1 if b < 6 else B))
                for t in range(TT):
                    c0 = b * T + t * P
                    m = nc.tensor.transpose(ps[b][:, t * P:(t + 1) * P], xT[:, c0:c0 + P], ident[:, :])
                m.then_inc(S["f_tr"], 1)

        @block.scalar
        def _(act):
            def copy(o, i):
                return nc.scalar.activation(o, i, ACT.Copy)

            nc.scalar.preload_act_table_set("natural_log_exp_and_others")
            act.wait_ge(S["eps_set"], 1)

            def turned_tokens(b):
                act.wait_ge(S["xn_tr"], b + 1)
                copy(xT[:, b * T:(b + 1) * T], ps[b % 4][:, :]).then_inc(S["xT_ready"], 1)

            for q in range(4):
                act.wait_ge(S["ln0_mean"], 2 * q + 2)
                for i in range(8 * q, 8 * q + 8):
                    if i >= 2:
                        act.wait_ge(S["ln0_sq"], i - 1)
                    nc.scalar.activation(xb[:, (i % 2) * P:(i % 2) * P + P], xtok[:, i, :], ACT.Square,
                                         bias=lnm[:, i:i + 1], accum_out=lnv[:, i:i + 1]).then_inc(S["ln0_sq"], 1)
                tiles = slice(8 * q, 8 * q + 8)
                act.wait_ge(S["ln0_sq"], 8 * q + 8)
                nc.scalar.activation(lnr[:, tiles], lnv[:, tiles], ACT.Ln, bias=eps[:, :], scale=1.0 / C)\
                    .then_inc(S["ln0_rstd"], 1)
                act.wait_ge(S["ln0_rstd"], 2 * q + 1)
                nc.scalar.activation(lnr[:, tiles], lnr[:, tiles], ACT.Exp, scale=-0.5).then_inc(S["ln0_rstd"], 1)
                if q:
                    turned_tokens(2 * q - 2)
                    turned_tokens(2 * q - 1)
            turned_tokens(B - 2)
            turned_tokens(B - 1)
            for i in range(2):
                act.wait_ge(S["wcomb_mm"], i + 1)
                src = ps[4 + i][:, 0:256].rearrange("p (h s d) -> p h s d", h=HEADS, s=2)
                for s in range(2):
                    copy(wcomb[:, 2 * i + s, :].rearrange("p (h d) -> p h d", h=HEADS), src[:, :, s, :])\
                        .then_inc(S["wcomb_ready"], 1)
            act.wait_ge(S["wcomb_mm"], 3)
            copy(wcomb[:, 4, :], ps[6][:, 0:128]).then_inc(S["wcomb_ready"], 1)

            def causal_slot(n, b, part):
                g = b * SLOTS + n
                if (k := earlier(n, part, 8)) is not None:
                    h, qt = k // TT, k % TT
                    if qt == 0:
                        need(act, "c_pv", b * HEADS + (n - 8) // TT - 3)
                    act.wait_ge(S["c_tr"], g - 7)
                    copy(ptA[:, h % 4, 0:qt + 1, qt * P:(qt + 1) * P],
                         ps[(3, 6)[k % 2]][:, 0:(qt + 1) * P].rearrange("p (k q) -> p k q", q=P))\
                        .then_inc(S["c_ptev"], 1)
                if (k := earlier(n, part, 0)) is not None:
                    qt = k % TT
                    act.wait_ge(S["c_max"], g + 1)
                    need(act, "c_tr", g - 7)
                    nc.scalar.activation(ea(k // TT, qt, 0, (qt + 1) * P), ps[k % 3][:, 0:(qt + 1) * P], ACT.Exp,
                                         bias=nmx[:, k % 8:k % 8 + 1], accum_out=lse[:, k % 8:k % 8 + 1])\
                        .then_inc(S["c_exp"], 1)
                if (n == 15 and part) or n == SLOTS + 15:
                    after = b if n < SLOTS else b + 1
                    act.wait_ge(S["c_pv"], after * HEADS)
                    need(act, "ca_mm", after - 1)
                    copy(yT, ps[4][:, :]).then_inc(S["yT_ready"], 1)
                if n == 15:
                    act.wait_ge(S["v_mm"], b + 1)
                    act.wait_ge(S["v16_zero"], 1)
                    copy(v16.rearrange("p k (h x) -> p k h x", x=P + DA)[:, :, :, 0:DA],
                         ps[5][:, :].rearrange("p (k h d) -> p k h d", k=TT, h=HEADS)).then_inc(S["v_ready"], 1)

            causal(act, causal_slot)

            def heads_of_weights(l):
                act.wait_ge(S["w_loaded"], (l + 1) * (5 * 16))
                for c in range(4):
                    w = slice(c * 512, (c + 1) * 512)
                    copy(wqk_hi[:, w], wqk_raw[:, w]).then_inc(S["w_split_h"], 1)

            heads_of_weights(0)
            with act.Fori(0, layers) as l:
                def square_tokens(b):
                    act.wait_ge(S["ldif"], l * B + b + 1)
                    nc.scalar.activation(lx[:, b, :], ld[:, b, :], ACT.Square).then_inc(S["lsq"], 1)

                nc.scalar.preload_act_table_set("natural_log_exp_and_others")
                def step(t, i, part):
                    def g_of(bt):
                        return l * B + bt

                    def joined_weights():
                        if part or t >= 4:
                            return
                        act.wait_ge(S["wvo_mm"], 4 * l + t + 1)
                        copy(wvo[:, 4 * t:4 * t + 4, :], mbank[:, :].rearrange("p (a b) -> p a b", a=4))\
                            .then_inc(S["wvo_ready"], 1)

                    def square(c):
                        if not (v := behind(t, i, part, 0)):
                            return
                        tt, bt = v
                        g = g_of(bt) * 16 + (4 * tt + c)
                        act.wait_ge(S["proj"], g + 1)
                        act.wait_ge(S["ssq_raw"], g)
                        nc.scalar.activation(sqb[:, c % 2, :], pj[c % 2][:, :], ACT.Square).then_inc(S["sq"], 1)

                    def norms(half):
                        if not (v := behind(t, i, part, 0)):
                            return
                        tt, bt = v
                        n = (g_of(bt) * 4 + tt) * 2 + half
                        act.wait_ge(S["ssq"], n + 1)
                        nc.scalar.activation(lnb[:, tt % 2, half, :], ssq[:, tt % 2, half, :], ACT.Ln)\
                            .then_inc(S["ln_part"], 1)
                        act.wait_ge(S["ln_part"], n + 4)
                        act.wait_ge(S["qn"], (g_of(bt) * 16 + 4 * tt + 2 * half))
                        nc.scalar.activation(rn[:, tt % 2, half, :], lnb[:, tt % 2, half, :], ACT.Exp, scale=-0.5)\
                            .then_inc(S["rn"], 1)

                    def turned_qk(c):
                        if not (v := behind(t, i, part, 1)):
                            return
                        tt, bt = v
                        act.wait_ge(S["tr"], g_of(bt) * 16 + (4 * tt + c) + 4)
                        if part == 0 and t == 1:
                            act.wait_ge(S["kT_zero"], 1)
                        if c == 0:
                            act.wait_ge(S["score"], (g_of(bt) * 4 + tt) * 2)
                        src = rbank[:, :].rearrange("p (j w q) -> p j w q", j=4, w=4)
                        if c < 2:
                            for h2 in range(2):
                                r = slice(64 * h2, 64 * h2 + 64)
                                m = copy(qbd[r, tt % 2, 4 * c:4 * c + 4, :, h2, :], src[r])
                        else:
                            m = copy(kT[:, 4 * (c - 2):4 * (c - 2) + 4, WIN + tt * P:WIN + (tt + 1) * P],
                                     rbank[:, :].rearrange("p (j q) -> p j q", j=4))
                        m.then_inc(S["ev"], 1)

                    def exp(wp):
                        if not (v := behind(t, i, part, 2)):
                            return
                        tt, bt = v
                        act.wait_ge(S["sub"], g_of(bt) * 8 + 2 * tt + wp + 1)
                        nc.scalar.activation(dd[:, wp, :], dd[:, wp, :], ACT.Exp).then_inc(S["exp"], 1)

                    def heads_of_p(lag, wp):
                        if not (v := behind(t, i, part, lag)):
                            return
                        tt, bt = v
                        m_ = g_of(bt) * 8 + 2 * tt + wp
                        act.wait_ge(S["pn"], m_ + 2)
                        act.wait_ge(S["pt"], m_ * 2)
                        copy(p2[:, wp, :, 0, :], pn[:, wp, :].rearrange("p (h k) -> p h k", h=HP)).then_inc(S["hi"], 1)

                    def turned_p(wp, half):
                        if not (v := behind(t, i, part, 3)):
                            return
                        tt, bt = v
                        m_ = g_of(bt) * 8 + 2 * tt + wp
                        act.wait_ge(S["pt"], m_ * 2 + half + 3)
                        act.wait_ge(S["yy"], m_ * 2)
                        copy(ptT[:, wp, 4 * half:4 * half + 4, :],
                             tbank[:, :].rearrange("p (j q) -> p j q", j=4)).then_inc(S["ptev"], 1)

                    def weighed(lag, wp):
                        if not (v := behind(t, i, part, lag)):
                            return
                        tt, bt = v
                        m_ = g_of(bt) * 8 + 2 * tt + wp
                        act.wait_ge(S["yy"], m_ * 2 + 3)
                        act.wait_ge(S["oo"], g_of(bt) * 2 + tt // 2)
                        copy(ysb[:, tt // 2, 4 * (tt % 2) + 2 * wp, :], ybank[0][:, :]).then_inc(S["yev0"], 1)
                        act.wait_ge(S["yy"], m_ * 2 + 4)
                        copy(ysb[:, tt // 2, 4 * (tt % 2) + 2 * wp + 1, :], ybank[1][:, :]).then_inc(S["yev1"], 1)

                    def windows():
                        if not (v := behind(t, i, part, 1)):
                            return
                        tt, bt = v
                        g = g_of(bt) * 4 + tt
                        act.wait_ge(S["xwt"], g + 1)
                        act.wait_ge(S["xwl"], g)
                        copy(xw, rbank[:, :]).then_inc(S["xwev"], 1)

                    def heads_of_windows():
                        if not (v := behind(t, i, part, 1)):
                            return
                        tt, bt = v
                        g = g_of(bt) * 4 + tt
                        if not (part == 0 and t - 1 < TT):
                            act.wait_ge(S["yy"], g * 4 - 10)
                        act.wait_ge(S["xwev"], g + 1)
                        copy(xwin[:, tt, 0, :, :], xw.rearrange("p (w c) -> p w c", w=4)).then_inc(S["xwh"], 1)

                    for wp in range(2):
                        square(2 * wp)
                        turned_qk(2 * wp)
                        turned_p(wp, 0)
                        square(2 * wp + 1)
                        if wp == 0:
                            windows()
                        else:
                            heads_of_windows()
                        turned_p(wp, 1)
                        heads_of_p(3 - wp, 1 - wp)
                        weighed(4 - wp, 1 - wp)
                        turned_qk(2 * wp + 1)
                        exp(wp)
                        norms(wp)
                    joined_weights()
                    if part == 2 and t == LAG + 2 * TT - 1:
                        for b in range(4):
                            square_tokens(b)

                pipeline(act, step)

                def inverse_deviation(b):
                    act.wait_ge(S["lvar"], l * B + b + 1)
                    nc.scalar.activation(lrs[:, b, :], ps[4 + b % 4][:, :], ACT.Ln, bias=eps[:, :]).then_inc(S["lln"], 1)
                    act.wait_ge(S["lln"], l * B + b + 1)
                    nc.scalar.activation(lrs[:, b, :], lrs[:, b, :], ACT.Exp, scale=-0.5).then_inc(S["lrs"], 1)

                for b in range(4):
                    inverse_deviation(b)
                    square_tokens(b + 4)
                    if b == 1:
                        act.wait_ge(S["w1_loaded"], (l + 1) * 16)
                        act.wait_ge(S["mx"], l * B)
                        copy(w1_hi[:, :], w1).then_inc(S["w_split_a"], 1)
                for b in range(4, B):
                    inverse_deviation(b)
                act.wait_ge(S["w_loaded2"], (l + 1) * (9 * 16))
                act.wait_ge(S["w2_loaded"], (l + 1) * (3 * 16))
                for c, (f0, fn) in enumerate(FCH):
                    m = copy(w2_hi[0:fn, c, :], w2[0:fn, c, :])
                m.then_inc(S["w2_split"], 1)
                nc.scalar.preload_act_table_set("gelu_and_others")
                act.wait_ge(S["xn"], (l + 1) * B)

                def heads_of_values(n, e, first=False):
                    for c, (f0, fn) in enumerate(FCH):
                        act.wait_ge(S["uu"], n * 3 + c + 1)
                        if c == 0 and not first:
                            act.wait_ge(S["down"], n - 1)
                        copy(uu_hi[e][c][0:fn], uu[0:fn, e, c, :]).then_inc(S["uh"], 1)

                def gates(n, e):
                    for c, (f0, fn) in enumerate(FCH):
                        act.wait_ge(S["gate"], n * 3 + c + 1)
                        if c == 0:
                            act.wait_ge(S["uu"], (n - 1) * 3)
                        nc.scalar.activation(gg[0:fn, e, c, :], ps[c][0:fn, :], ACT.Gelu,
                                             bias=b1[0:fn, 3 + c:4 + c]).then_inc(S["gelu"], 1)

                for e in range(2):
                    if e:
                        heads_of_values(l * B, 0, first=True)
                    for c, (f0, fn) in enumerate(FCH):
                        act.wait_ge(S["gate"], (l * B + e) * 3 + c + 1)
                        nc.scalar.activation(gg[0:fn, e, c, :], ps[c][0:fn, :], ACT.Gelu,
                                             bias=b1[0:fn, 3 + c:4 + c]).then_inc(S["gelu"], 1)
                with act.Fori(1, B // 2) as j:
                    for e in range(2):
                        n = l * B + 2 * j + e
                        heads_of_values(n - 1, 1 - e)
                        gates(n, e)
                heads_of_values(l * B + (B - 1), 1)
                heads_of_weights(l + 1)

        @block.vector
        def _(dve):
            tt_, ts_ = nc.vector.tensor_tensor, nc.vector.tensor_scalar

            def bc(v, shape, axis):
                return v.unsqueeze(axis).to_broadcast(shape)

            nc.vector.memset(eps[:, :], 1e-5).then_inc(S["eps_set"], 1)
            column = iter(range(32))
            for name, n in (("sq", 1), ("rotd", 1), ("ssq_raw", 1), ("add", 1), ("tr", 3), ("score", 2), ("yy", 2),
                            ("pt", 2), ("qn", 6), ("ln_part", 3), ("lo", 1), ("pn", 1), ("oo", 1)):
                for _ in range(n):
                    c = next(column)
                    nc.vector.memset(spare[:, c:c + 1], 0.0).then_inc(S[name], 1)

            nc.vector.memset(wo_bd[:, :, :, :], 0.0).then_inc(S["wo_zero"], 1)
            def normalise_tokens(q):
                dve.wait_ge(S["ln0_rstd"], 2 * q + 2)
                for i in range(8 * q, 8 * q + 8):
                    m = ts_(xtok[:, i, :], xtok[:, i, :], lnm[:, i:i + 1], lnr[:, i:i + 1], ALU.add, ALU.mult)
                m.then_inc(S["ln0_x"], 1)

            for q in range(4):
                tiles = slice(8 * q, 8 * q + 8)
                dve.wait_ge(S[f"xload{q}"], 16)
                nc.vector.tensor_reduce(lnm[:, tiles], xtok[:, tiles, :], AX.X, ALU.add).then_inc(S["ln0_mean"], 1)
                dve.wait_ge(S["ln0_mean"], 2 * q + 1)
                ts_(lnm[:, tiles], lnm[:, tiles], -1.0 / C, None, ALU.mult).then_inc(S["ln0_mean"], 1)
                if q:
                    normalise_tokens(q - 1)
            normalise_tokens(3)
            dve.wait_ge(S["xT_ready"], B)

            dve.wait_ge(S["c_weights"], 8 * 16)
            dve.wait_ge(S["const"], 7 * 16)
            def tokens(a):
                need(dve, "v_mm", a)
                nc.vector.tensor_copy(xb, xT[:, bass.ds(a * T, T)]).then_inc(S["xb_ready"], 1)

            def rope(a, side, stage):
                if stage == 0:
                    need(dve, "stack3", a * (8 * 16))
                    dve.wait_ge(S["c_proj"], a * 4 + 2 * side + 1)
                    need(dve, "c_split", a * 4 + 2 * side)
                    tt_(ra, ps[5][:, :], crot[:, 2 * side, :], ALU.mult).then_inc(S["c_rope_part"], 1)
                elif stage == 1:
                    dve.wait_ge(S["c_proj"], a * 4 + 2 * side + 2)
                    tt_(rb_, ps[7][:, :], crot[:, 2 * side + 1, :], ALU.mult).then_inc(S["c_rope_part"], 1)
                elif stage == 2:
                    dve.wait_ge(S["c_rope_part"], a * 4 + 2 * side + 2)
                    tt_(ra, ra, rb_, ALU.add).then_inc(S["c_rope"], 1)
                elif stage == 3:
                    dve.wait_ge(S["c_rope"], 2 * a + side + 1)
                    nc.vector.tensor_copy(split_qk[:, side, 0, :], ra).then_inc(S["c_split"], 1)
                else:
                    dve.wait_ge(S["c_split"], a * 4 + 2 * side + 1)
                    tt_(split_qk[:, side, 1, :], ra, split_qk[:, side, 0, :].bitcast(F32), ALU.subtract)\
                        .then_inc(S["c_split"], 1)

            tokens(0)
            for stage in range(10):
                rope(0, stage // 5, stage % 5)

            def causal_slot(n, b, part):
                g = b * SLOTS + n
                if (k := earlier(n, part, 5)) is not None:
                    h, qt = k // TT, k % TT
                    heads = b * HEADS + (n - 5) // TT + 1
                    if qt == 0:
                        dve.wait_ge(S["c_exp"], g - 1)
                        need(dve, "c_p", g - 9)
                        r = slice(4 * (h % 2), 4 * (h % 2) + 4)
                        nc.vector.reciprocal(lre[:, r], lse[:, r]).then_inc(S["c_rec"], 1)
                    dve.wait_ge(S["c_rec"], heads)
                    tile = ea(h, qt, 0, (qt + 1) * P)
                    ts_(tile, tile, lre[:, k % 8:k % 8 + 1], None, ALU.mult).then_inc(S["c_p"], 1)
                if (k := earlier(n, part, 0)) is not None:
                    dve.wait_ge(S["c_score"], g + 1)
                    need(dve, "c_exp", g - 7)
                    nc.vector.tensor_reduce(nmx[:, k % 8:k % 8 + 1], ps[k % 3][:, 0:(k % TT + 1) * P], AX.X, ALU.max,
                                            negate=True).then_inc(S["c_max"], 1)
                if (n == 18 and part) or n == SLOTS + 18:
                    after = b if n < SLOTS else b + 1
                    dve.wait_ge(S["ca_mm"], after)
                    dve.wait_ge(S["res_in"], after * 16)
                    tt_(xres[:, 1, :, :], ps[7][:, :].rearrange("p (t c) -> p t c", t=TT), xres[:, 0, :, :], ALU.add)\
                        .then_inc(S["ca_sum"], 1)
                if part < 2:
                    if n == 18:
                        tokens(b + 1)
                    if 22 <= n < 27 or 32 <= n < 37:
                        rope(b + 1, n // 10 - 2, n % 10 - 2)

            causal(dve, causal_slot)

            dve.wait_ge(S["ca_sum"], B)
            nc.vector.memset(xs[:, 0:WIN + 1], 0.0).then_inc(S["xs_zero"], 1)

            def prepare_weights(l):
                dve.wait_ge(S["w_loaded"], (l + 1) * (5 * 16))
                for c in range(4):
                    w = slice(c * 512, (c + 1) * 512)
                    dve.wait_ge(S["w_split_h"], 4 * l + c + 1)
                    tt_(wqk_lo[:, w], wqk_raw[:, w], wqk_hi[:, w].bitcast(F32), ALU.subtract).then_inc(S["w_split"], 2)
                for s in range(2):
                    for u in range(2):
                        m = tt_(rots[:, :, s, u, :], rot[:, :, s, u, :], bc(qks[:, s, u, :], [P, TT, D], 1), ALU.mult)
                m.then_inc(S["rots_ready"], 1)
                dve.wait_ge(S["rots_ready"], l + 1)

            prepare_weights(0)
            with dve.Fori(0, layers) as l:
                def deviation(b):
                    dve.wait_ge(S["lmean"], l * B + b + 1)
                    dve.wait_ge(S["lx"], l * B + b + 1)
                    tt_(ld[:, b, :], lx[:, b, :], ps[b % 4][:, :], ALU.subtract).then_inc(S["ldif"], 1)

                def shift_tokens(b):
                    nc.vector.tensor_copy(lx[0:64, b, :], xT[0:64, b * T:(b + 1) * T])
                    nc.vector.tensor_copy(lx[64:128, b, 1:T], xT[64:128, b * T:(b + 1) * T - 1]).then_inc(S["lx"], 1)

                def load_tile(tt, bt, first, again):
                    g = (l * B + bt) * 4 + tt
                    if not first:
                        dve.wait_ge(S["proj"], g * 4 - 4)
                        if again:
                            dve.wait_ge(S["xdup"], g - 3)
                    c0, base = WIN + tt * P, bt * T + tt * P
                    late = 1 if tt == 0 else 0
                    hi, lo = xs_hi[:, tt % 2, :], xs_lo[:, tt % 2, :]
                    nc.vector.tensor_copy(xs[0:64, c0:c0 + P], xT[0:64, bass.ds(base, P)])
                    nc.vector.tensor_copy(xs[64:128, c0 + late:c0 + P], xT[64:128, bass.ds(base - 1 + late, P - late)])\
                        .then_inc(S["xs_part"], 1)
                    dve.wait_ge(S["xs_part"], 2 * g + 1)
                    nc.vector.tensor_copy(hi, xs[:, c0:c0 + P]).then_inc(S["xs_part"], 1)
                    dve.wait_ge(S["xs_part"], 2 * g + 2)
                    tt_(lo, xs[:, c0:c0 + P], hi.bitcast(F32), ALU.subtract).then_inc(S["xs_ready"], 1)

                def step(t, i, part):
                    def g_of(bt):
                        return l * B + bt

                    def load_next():
                        if v := behind(t, i, part, -1):
                            load_tile(*v, part == 0 and t + 1 < 2, not (part == 0 and t + 1 < TT))

                    def double_windows():
                        if not (v := behind(t, i, part, 0)):
                            return
                        tt, bt = v
                        g = g_of(bt) * 4 + tt
                        dve.wait_ge(S["xs_ready"], g + 1)
                        dve.wait_ge(S["xwt"], g)
                        for own in range(2):
                            c0 = tt * P + own * WIN
                            m = nc.vector.tensor_copy(
                                xdup[:, :, :, own, :],
                                bc(xs[:, c0:c0 + P].rearrange("p (w k) -> p w k", w=4), [P, 4, 2, WIN], 2))
                        m.then_inc(S["xdup"], 1)

                    def rests_of_windows():
                        if not (v := behind(t, i, part, 1)):
                            return
                        tt, bt = v
                        g = g_of(bt) * 4 + tt
                        dve.wait_ge(S["xwh"], g + 1)
                        tt_(xwin[:, tt, 1, :, :], xw.rearrange("p (w c) -> p w c", w=4),
                            xwin[:, tt, 0, :, :].bitcast(F32), ALU.subtract).then_inc(S["xwl"], 1)

                    def rotate(c):
                        if not (v := behind(t, i, part, 0)):
                            return
                        tt, bt = v
                        g = g_of(bt) * 16 + (4 * tt + c)
                        s = c // 2
                        dve.wait_ge(S["sq"], g + 2)
                        dve.wait_ge(S["add"], g)
                        src = pj[c % 2][:, :].rearrange("p (h d) -> p h d", h=8)
                        sv = pj[c % 2][:, :].rearrange("p (h e d) -> p h e d", h=8, e=2)
                        tt_(t1[:, c % 2, :].rearrange("p (h d) -> p h d", h=8), src,
                            bc(rots[:, tt, s, 0, :], [P, 8, D], 1), ALU.mult)
                        d4 = t2[:, c % 2, :].rearrange("p (h e d) -> p h e d", h=8, e=2)
                        for e in range(2):
                            m = tt_(d4[:, :, e, :], sv[:, :, 1 - e, :],
                                    bc(rots[:, tt, s, 1, e * 32:e * 32 + 32], [P, 8, 32], 1), ALU.mult)
                        m.then_inc(S["rotd"], 1)

                    def square_sums(c):
                        if not (v := behind(t, i, part, 0)):
                            return
                        tt, bt = v
                        g = g_of(bt) * 16 + (4 * tt + c)
                        half = c // 2
                        dve.wait_ge(S["sq"], g + 2)
                        if c % 2 == 0:
                            dve.wait_ge(S["ln_part"], g_of(bt) * 8 + 2 * tt + half)
                        nc.vector.tensor_reduce(ssq[:, tt % 2, half, 8 * (c % 2):8 * (c % 2) + 8],
                                                sqb[:, c % 2, :].rearrange("p (h d) -> p h d", h=8), AX.X, ALU.add)\
                            .then_inc(S["ssq_raw"], 1)
                        if c % 2:
                            dve.wait_ge(S["ssq_raw"], g + 2)
                            ts_(ssq[:, tt % 2, half, :], ssq[:, tt % 2, half, :], 1e-24, None, ALU.max)\
                                .then_inc(S["ssq"], 1)

                    def shift(wp):
                        if not (v := behind(t, i, part, 2)):
                            return
                        tt, bt = v
                        m_ = g_of(bt) * 8 + 2 * tt + wp
                        dve.wait_ge(S["score"], m_ + 3)
                        s3 = sbank[:, :].rearrange("p (h k) -> p h k", h=HP)
                        nc.vector.tensor_reduce(smax[:, wp, :], s3, AX.X, ALU.max).then_inc(S["smax"], 1)
                        dve.wait_ge(S["smax"], m_ + 1)
                        dve.wait_ge(S["pn"], m_)
                        tt_(dd[:, wp, :].rearrange("p (h k) -> p h k", h=HP), s3,
                            bc(smax[:, wp, :], [P, HP, 64], 2), ALU.subtract).then_inc(S["sub"], 1)

                    def sums(lag, wp):
                        if not (v := behind(t, i, part, lag)):
                            return
                        tt, bt = v
                        m_ = g_of(bt) * 8 + 2 * tt + wp
                        dve.wait_ge(S["exp"], m_ + 1)
                        d3 = dd[:, wp, :].rearrange("p (h k) -> p h k", h=HP)
                        nc.vector.tensor_reduce(ssum[:, wp, :], d3, AX.X, ALU.add).then_inc(S["ssum"], 1)
                        dve.wait_ge(S["ssum"], m_ + 1)
                        nc.vector.reciprocal(srec[:, wp, :], ssum[:, wp, :]).then_inc(S["srec"], 1)

                    def shift_early():
                        if part == 2 and t == LAG + 2 * TT - 2:
                            dve.wait_ge(S["oo"], (l + 1) * (2 * B))
                            dve.wait_ge(S["xupd"], (l + 1) * (2 * B) - 2)
                            nc.vector.memset(lx[64:128, :, 0:1], 0.0).then_inc(S["lx_zero"], 1)
                            dve.wait_ge(S["lx_zero"], l + 1)
                            for b in range(B - 1):
                                shift_tokens(b)

                    def update():
                        v = behind(t, i, part, LAG)
                        if not v or v[0] % 2 == 0:
                            return
                        tt, bt = v
                        hf = tt // 2
                        dve.wait_ge(S["oo"], g_of(bt) * 2 + hf + 2)
                        dst = xT[:, bass.ds(bt * T + hf * 256, 256)]
                        tt_(dst, mbank[:, 0:256], dst, ALU.add).then_inc(S["xupd"], 1)

                    if part == 2 and t == LAG + 2 * TT - 1:
                        dve.wait_ge(S["pt"], (l + 1) * (16 * B) + 2)
                        dve.wait_ge(S["tr"], (l + 1) * (16 * B) + 3)
                        dve.wait_ge(S["xwh"], (l + 1) * (4 * B))
                        for b in range(4):
                            deviation(b)
                    for wp in range(2):
                        sums(3 - wp, 1 - wp)
                        rotate(2 * wp)
                        rotate(2 * wp + 1)
                        shift(wp)
                        square_sums(2 * wp)
                        square_sums(2 * wp + 1)
                        if wp == 1:
                            double_windows()
                            rests_of_windows()
                        else:
                            update()
                            load_next()
                    shift_early()

                dve.wait_ge(S["mx"], l * B)
                dve.wait_ge(S["xs_zero"], 1)
                load_tile(0, 0, True, False)
                pipeline(dve, step)

                def gain(b):
                    dve.wait_ge(S["lmul"], l * B + b + 1)
                    ts_(xn_all[:, b * T:(b + 1) * T], lrs[:, b, :], lng[:, 0:1], lng[:, 1:2], ALU.mult, ALU.add)\
                        .then_inc(S["xn"], 1)

                dve.wait_ge(S["xupd"], (l + 1) * (2 * B))
                shift_tokens(B - 1)
                dve.wait_ge(S["w_loaded2"], (l + 1) * (9 * 16))
                deviation(4)
                for b in range(B):
                    if b + 5 < B:
                        deviation(b + 5)
                    gain(b)
                    if b == B - 5:
                        for e in range(2):
                            src = xn_all[:, e * T:(e + 1) * T]
                            dve.wait_ge(S["xn"], l * B + e + 1)
                            nc.vector.tensor_copy(mlp_hi[:, e, :], src).then_inc(S["mhi"], 1)
                            dve.wait_ge(S["mhi"], l * B + e + 1)
                            tt_(mlp_lo[:, e, :], src, mlp_hi[:, e, :].bitcast(F32), ALU.subtract).then_inc(S["mlo"], 1)
                    if b == 2:
                        dve.wait_ge(S["w_split_a"], 2 * l + 1)
                        tt_(w1_lo[:, :], w1, w1_hi[:, :].bitcast(F32), ALU.subtract).then_inc(S["w_split_a"], 1)
                dve.wait_ge(S["w2_split"], 2 * l + 1)
                for c, (f0, fn) in enumerate(FCH):
                    m = tt_(w2_lo[0:fn, c, :], w2[0:fn, c, :], w2_hi[0:fn, c, :].bitcast(F32), ALU.subtract)
                m.then_inc(S["w2_split"], 1)

                def split_tokens(n, first, e):
                    dve.wait_ge(S["aa"], (n - 1) * 3)
                    src = xn_all[:, bass.ds(first * T, T)]
                    nc.vector.tensor_copy(mlp_hi[:, e, :], src).then_inc(S["mhi"], 1)
                    dve.wait_ge(S["mhi"], n + 1)
                    tt_(mlp_lo[:, e, :], src, mlp_hi[:, e, :].bitcast(F32), ALU.subtract).then_inc(S["mlo"], 1)

                def gated(n, e, c):
                    f0, fn = FCH[c]
                    dve.wait_ge(S["aa"], n * 3 + c + 1)
                    dve.wait_ge(S["gelu"], n * 3 + c + 1)
                    nc.vector.scalar_tensor_tensor(uu[0:fn, e, c, :], ps[3 + c][0:fn, :], b1[0:fn, c:c + 1],
                                                   gg[0:fn, e, c, :], ALU.add, ALU.mult).then_inc(S["uu"], 1)

                def add_result(n, batch, e):
                    dve.wait_ge(S["down"], n + 1)
                    dst = xT[:, bass.ds(batch * T, T)]
                    nc.vector.scalar_tensor_tensor(dst, ps[6 + e][:, :], lng[:, 2:3], dst, ALU.add, ALU.add)\
                        .then_inc(S["mx"], 1)

                dve.wait_ge(S["xn"], (l + 1) * B)
                for c in range(3):
                    gated(l * B, 0, c)
                with dve.Fori(1, B // 2) as j:
                    for e in range(2):
                        n = l * B + 2 * j + e
                        split_tokens(n, 2 * j + e, e)
                        dve.wait_ge(S["ul"], (n - 2) * 3)
                        for c in range(3):
                            gated(n - 1, 1 - e, c)
                        add_result(n - 2, 2 * j + e - 2, e)
                for c in range(3):
                    gated(l * B + (B - 1), 1, c)
                add_result(l * B + (B - 2), B - 2, 0)
                prepare_weights(l + 1)
                add_result(l * B + (B - 1), B - 1, 1)

            dve.wait_ge(S["f_in"], 16)
            for b in range(B):
                dve.wait_ge(S["f_tr"], b + 1)
                tt_(final[:, 1, b, :, :], ps[b][:, :].rearrange("p (t c) -> p t c", t=TT), final[:, 0, b, :, :], ALU.add)\
                    .then_inc(S["f_sum"], 1)

        @block.gpsimd
        def _(pool):
            pt_ = nc.gpsimd.tensor_tensor
            pool.wait_ge(S["xT_ready"], B)
            nc.gpsimd.memset(v16.rearrange("p a b -> p (a b)"), 0.0).then_inc(S["v16_zero"], 1)

            def mask_q(b, h):
                pool.wait_ge(S[f"stack{h // 4}"], (b + 1) * (8 * 16))
                need(pool, "c_score", b * SLOTS + TT * (h - 1))
                pt_(qm[:, h % 2, :, :], stacks[:, 0, h // 4, :].bitcast(F32).rearrange("p (a b) -> p a b", a=4),
                    hm[:, h % 4:h % 4 + 1].unsqueeze(2).to_broadcast([P, TT, P]), ALU.mult).then_inc(S["qm_ready"], 1)

            pool.wait_ge(S["const"], 7 * 16)
            for h in range(HEADS):
                mask_q(0, h)
            with pool.Fori(1, B) as b:
                for h in range(HEADS):
                    mask_q(b, h)
            pool.wait_ge(S["ca_out"], B * 16)
            pool.wait_ge(S["wcomb_ready"], 5)
            nc.gpsimd.memset(qbd.rearrange("p a b c d e -> p (a b c d e)"), 0.0)
            nc.gpsimd.memset(kT[:, :, 0:WIN], 0.0).then_inc(S["kT_zero"], 1)
            with pool.Fori(0, layers) as l:
                def step(t, i, part):
                    def g_of(bt):
                        return l * B + bt

                    def add(c):
                        if not (v := behind(t, i, part, 0)):
                            return
                        tt, bt = v
                        g = g_of(bt) * 16 + (4 * tt + c)
                        pool.wait_ge(S["qn"], g + 5)
                        pool.wait_ge(S["rotd"], g + 2)
                        pt_(qsum[:, c % 2, :], t1[:, c % 2, :], t2[:, c % 2, :], ALU.add).then_inc(S["add"], 1)

                    def scale(lag, c):
                        if not (v := behind(t, i, part, lag)):
                            return
                        tt, bt = v
                        g = g_of(bt) * 16 + (4 * tt + c)
                        half = c // 2
                        pool.wait_ge(S["rn"], g_of(bt) * 8 + (2 * tt + half + 1))
                        pool.wait_ge(S["add"], g + 2)
                        pool.wait_ge(S["tr"], g)
                        r = rn[:, tt % 2, half, 8 * (c % 2):8 * (c % 2) + 8].unsqueeze(2).to_broadcast([P, 8, D])
                        pt_(qn[:, c, :].rearrange("p (h d) -> p h d", h=8),
                            qsum[:, c % 2, :].rearrange("p (h d) -> p h d", h=8), r, ALU.mult).then_inc(S["qn"], 1)

                    def normalise(lag, wp):
                        if not (v := behind(t, i, part, lag)):
                            return
                        tt, bt = v
                        m_ = g_of(bt) * 8 + 2 * tt + wp
                        pool.wait_ge(S["srec"], m_ + 1)
                        pool.wait_ge(S["lo"], m_)
                        pt_(pn[:, wp, :].rearrange("p (h k) -> p h k", h=HP),
                            dd[:, wp, :].rearrange("p (h k) -> p h k", h=HP),
                            srec[:, wp, :].unsqueeze(2).to_broadcast([P, HP, 64]), ALU.mult).then_inc(S["pn"], 1)

                    def rests_of_p(lag, wp):
                        if not (v := behind(t, i, part, lag)):
                            return
                        tt, bt = v
                        pool.wait_ge(S["hi"], g_of(bt) * 8 + (2 * tt + wp + 1))
                        pt_(p2[:, wp, :, 1, :], pn[:, wp, :].rearrange("p (h k) -> p h k", h=HP),
                            p2[:, wp, :, 0, :].bitcast(F32), ALU.subtract).then_inc(S["lo"], 1)

                    for wp in range(2):
                        scale(1 - wp, 2 - 2 * wp)
                        scale(1 - wp, 3 - 2 * wp)
                        normalise(3 - wp, 1 - wp)
                        add(2 * wp)
                        add(2 * wp + 1)
                        rests_of_p(3 - wp, 1 - wp)

                pipeline(pool, step)

                for b in range(B):
                    pool.wait_ge(S["lrs"], l * B + b + 1)
                    pt_(lrs[:, b, :], ld[:, b, :], lrs[:, b, :], ALU.mult).then_inc(S["lmul"], 1)

                with pool.Fori(0, B // 2) as j:
                    for e in range(2):
                        n = l * B + 2 * j + e
                        for c, (f0, fn) in enumerate(FCH):
                            pool.wait_ge(S["uh"], n * 3 + c + 1)
                            pt_(uu_lo[e][c][0:fn], uu[0:fn, e, c, :], uu_hi[e][c][0:fn].bitcast(F32), ALU.subtract)\
                                .then_inc(S["ul"], 1)


def kernel(L0_attn_x, L0_attn_Wq_down, L0_attn_Wk_down, L0_attn_Wv_down, L0_attn_Wq_up_c, L0_attn_Wq_up_e,
           L0_attn_Wk_up_c, L0_attn_Wk_up_e, L0_attn_Wv_up, L0_attn_Wc, L0_ffn_Wqkv, L0_ffn_q_scale,
           L0_ffn_k_scale, L0_ffn_Wo, L0_ffn_ln_g, L0_ffn_ln_b, L0_ffn_W1, L0_ffn_b1, L0_ffn_W2, L0_ffn_b2):
    import concourse.bacc as bacc
    from concourse.bass_utils import run_bass_kernel_spmd

    f32 = np.float32

    def turned(w):
        return np.asarray(w).T.reshape(HP, P, C).transpose(1, 0, 2)

    def two_heads(parts):
        n = sum(p.shape[1] for p in parts)
        o = np.zeros((P, 2, n), f32)
        o[0:LAT, 0], o[LAT:P, 1] = np.concatenate(parts, 1), np.concatenate(parts, 1)
        return o

    swap4, zero4 = [1, 0, 3, 2], np.zeros((LAT, 4), f32)
    qc, qe, kc, ke, vu = (np.asarray(a) for a in (L0_attn_Wq_up_c, L0_attn_Wq_up_e, L0_attn_Wk_up_c, L0_attn_Wk_up_e,
                                                  L0_attn_Wv_up))
    W, W1, W2 = np.asarray(L0_ffn_Wqkv), np.asarray(L0_ffn_W1), np.asarray(L0_ffn_W2)
    Wo = np.asarray(L0_ffn_Wo).reshape(DEPTH, HP, 2, D, C).transpose(0, 2, 3, 1, 4)
    WvT = W[:, :, 2 * INNER:].transpose(0, 2, 1).reshape(DEPTH, HP, P, C).transpose(0, 2, 1, 3)
    qs, ks = np.asarray(L0_ffn_q_scale), np.asarray(L0_ffn_k_scale)
    half = D // 2
    qks = np.stack([np.stack([s, np.concatenate([s[:, half:], s[:, :half]], 1)], 1) for s in (qs, ks)], 1)
    arrays = {
        "x": L0_attn_x, "wqdT": turned(L0_attn_Wq_down), "wkdT": turned(L0_attn_Wk_down), "wvdT": turned(L0_attn_Wv_down),
        "upq": two_heads([qc, qe, zero4, qe[:, swap4]]), "upk": two_heads([kc, ke, zero4, ke[:, swap4]]),
        "upv": two_heads([vu]), "Wc": L0_attn_Wc, "Wqkv": W, "WvT": WvT, "Wo": Wo, "qks": qks,
        "ln_g": np.asarray(L0_ffn_ln_g)[:, :, None], "ln_b": np.asarray(L0_ffn_ln_b)[:, :, None],
        "b2": np.asarray(L0_ffn_b2)[:, :, None], "W1": W1, "b1": np.asarray(L0_ffn_b1)[:, :, None], "W2": W2,
        **shape_constants(),
    }
    arrays = {k: np.ascontiguousarray(v) for k, v in arrays.items()}
    nc = bacc.Bacc("TRN2", target_bir_lowering=False, num_devices=1)
    ins = {k: nc.dram_tensor("in_" + k, v.shape, mybir.dt.from_np(v.dtype), kind="ExternalInput").ap()
           for k, v in arrays.items()}
    out = nc.dram_tensor("out", (B, T, C), F32, kind="ExternalOutput").ap()
    build(nc, ins, out)
    r = run_bass_kernel_spmd(nc, [{"in_" + k: v for k, v in arrays.items()}], core_ids=[0])
    return r.results[0]["out"]
```
